# Optimizing a Trainium2 kernel written in Bass

```python
import numpy as np
import jax
import jax.numpy as jnp

def _softmax(x, axis=-1):
    return jax.nn.softmax(x, axis=axis)

def _gelu(x):
    return jax.nn.gelu(x, approximate=True)

def _silu(x):
    return jax.nn.silu(x)

def _sigmoid(x):
    return jax.nn.sigmoid(x)

def _layernorm(x, axis=-1, eps=1e-05):
    m = jnp.mean(x, axis=axis, keepdims=True)
    v = jnp.var(x, axis=axis, keepdims=True)
    return (x - m) / jnp.sqrt(v + eps)

def _scatter_add(tgt, idx, src, axis=0):
    return tgt.at[idx].add(src)

def _segment_sum(src, seg, n):
    return jax.ops.segment_sum(src, seg, n)
kernel_name = 'mk_decoder_preln_d2_seqx_r8_81ce50'

def setup_inputs(seed: int=0):
    np.random.seed(seed)
    _w = jnp.asarray

    def _rec_inputs():
        import jax
        import jax.numpy as jnp
        _rk = jax.random.key(seed)
        x = 7.22e-05 + 1 * jax.random.normal(jax.random.fold_in(_rk, 1), (8, 256, 128), jnp.float32)
        _lenS = 256 - jax.random.randint(jax.random.fold_in(_rk, 7), (8,), 0, max(1, 256 // 4) + 1, jnp.int32)
        _lenS2 = 1601 - jax.random.randint(jax.random.fold_in(_rk, 8), (8,), 0, max(1, 1601 // 4) + 1, jnp.int32)
        _ctx_1024P = jax.random.normal(jax.random.fold_in(_rk, 11), (8, 16, 128), jnp.float32)
        _ctx_1024c = jax.random.dirichlet(jax.random.fold_in(_rk, 511), 0.3 * jnp.ones((16,), jnp.float32), (8, 1601))
        _ctx_1024t = jnp.einsum('bsk,bkd->bsd', _ctx_1024c, _ctx_1024P)
        _ctx_1024t = _ctx_1024t * jax.lax.rsqrt(jnp.mean(jnp.square(_ctx_1024t)) + 1e-12) * 0.953939
        ctx_1024 = 4.13588e-05 + 0.999923 * (_ctx_1024t + 0.3 * jax.random.normal(jax.random.fold_in(_rk, 611), (8, 1601, 128), jnp.float32))
        return (x, ctx_1024)
    x, ctx_1024 = _rec_inputs()

    def _L0_attn_setup():
        import jax, jax.numpy as jnp
        import numpy as np
        B, L, D = (2, 512, 128)
        DS, RK, K = (16, 64, 3)
        EPS = 1e-05
        key = jax.random.key(seed)
        ks = jax.random.split(key, 16)
        s = 0.02
        inp = {'x': jax.random.normal(ks[0], (B, L, D), jnp.float32), 'gamma': jnp.ones((D,), jnp.float32), 'beta': jnp.zeros((D,), jnp.float32), 'W_in': jax.random.normal(ks[1], (D, 2 * D), jnp.float32) * s, 'conv_w': jax.random.normal(ks[2], (K, 1, D), jnp.float32) * s, 'conv_b': jnp.zeros((D,), jnp.float32), 'W_xp': jax.random.normal(ks[3], (D, RK), jnp.float32) * s, 'W_Bg': jax.random.normal(ks[4], (D, DS), jnp.float32) * s, 'W_Cg': jax.random.normal(ks[5], (D, DS), jnp.float32) * s, 'W_dt': jax.random.normal(ks[6], (RK, D), jnp.float32) * s, 'b_dt': jnp.zeros((D,), jnp.float32), 'W_Bp': jax.random.normal(ks[7], (DS, D), jnp.float32) * s, 'W_Cp': jax.random.normal(ks[8], (DS, D), jnp.float32) * s, 'A': -jnp.exp(jax.random.normal(ks[9], (D,), jnp.float32) * 0.5), 'D_skip': jnp.ones((D,), jnp.float32), 'W_out': jax.random.normal(ks[10], (D, D), jnp.float32) * s}
        return inp
    _L0_attn_all = _L0_attn_setup()
    _L0_attn_in = {k: v for k, v in _L0_attn_all.items() if k in ('gamma', 'beta', 'W_in', 'conv_w', 'conv_b', 'W_xp', 'W_Bg', 'W_Cg', 'W_dt', 'b_dt', 'W_Bp', 'W_Cp', 'A', 'D_skip', 'W_out')}
    del _L0_attn_all

    def _L0_xattn_setup():
        import jax, jax.numpy as jnp
        import numpy as np
        D_MODEL = 128
        NUM_HEADS = 16
        D_K = D_MODEL // NUM_HEADS
        key = jax.random.key(seed)
        ks = jax.random.split(key, 12)
        B, S, D = (4, 256, D_MODEL)
        s = 1.0 / np.sqrt(D)
        return {'q': jax.random.normal(ks[0], (B, S, D), jnp.float32), 'k': jax.random.normal(ks[1], (B, S, D), jnp.float32), 'v': jax.random.normal(ks[2], (B, S, D), jnp.float32), 'w_q': jax.random.normal(ks[3], (D, D), jnp.float32) * s, 'b_q': jax.random.normal(ks[4], (D,), jnp.float32) * s, 'w_k': jax.random.normal(ks[5], (D, D), jnp.float32) * s, 'b_k': jax.random.normal(ks[6], (D,), jnp.float32) * s, 'w_v': jax.random.normal(ks[7], (D, D), jnp.float32) * s, 'b_v': jax.random.normal(ks[8], (D,), jnp.float32) * s, 'w_0': jax.random.normal(ks[9], (D, D), jnp.float32) * s, 'b_0': jax.random.normal(ks[10], (D,), jnp.float32) * s}
    _L0_xattn_all = _L0_xattn_setup()
    _L0_xattn_in = {k: v for k, v in _L0_xattn_all.items() if k in ('w_q', 'b_q', 'w_k', 'b_k', 'w_v', 'b_v', 'w_0', 'b_0')}
    del _L0_xattn_all

    def _L0_ffn_setup():
        import jax, jax.numpy as jnp
        import numpy as np
        DIM = 128
        DEPTH = 2
        HEADS = 8
        DIM_HEAD = 64
        WINDOW = 64
        INNER = HEADS * DIM_HEAD
        HID = int(DIM * 4 * 2 / 3)
        B, N = (2, 1024)
        QK_SCALE = 8.0

        def shift_token(t):
            t1, t2 = jnp.split(t, 2, axis=-1)
            t2 = jnp.pad(t2, ((0, 0), (1, 0), (0, 0)))[:, :-1]
            return jnp.concatenate([t1, t2], axis=-1)

        def l2norm(t):
            return t / jnp.clip(jnp.linalg.norm(t, axis=-1, keepdims=True), 1e-12)

        def rotate_half(x):
            x1, x2 = jnp.split(x, 2, axis=-1)
            return jnp.concatenate([-x2, x1], axis=-1)

        def rotary_xpos(q, k):
            n = q.shape[-2]
            half_idx = jnp.arange(0, DIM_HEAD, 2, dtype=jnp.float32)
            inv_freq = 1.0 / 10000.0 ** (half_idx / DIM_HEAD)
            t = jnp.arange(n, dtype=jnp.float32)
            freqs = t[:, None] * inv_freq[None, :]
            freqs = jnp.concatenate([freqs, freqs], axis=-1)
            base = (half_idx + 0.4 * DIM_HEAD) / (1.4 * DIM_HEAD)
            power = (t - n // 2) / float(WINDOW // 2)
            scale = base[None, :] ** power[:, None]
            scale = jnp.concatenate([scale, scale], axis=-1)
            cos, sin = (jnp.cos(freqs), jnp.sin(freqs))
            q = q * cos * scale + rotate_half(q) * sin * scale
            k = k * cos / scale + rotate_half(k) * sin / scale
            return (q, k)

        def local_attention(q, k, v):
            b, h, n, d = q.shape
            w = n // WINDOW
            bq = q.reshape(b, h, w, WINDOW, d) * QK_SCALE
            bk = k.reshape(b, h, w, WINDOW, d)
            bv = v.reshape(b, h, w, WINDOW, d)

            def look_around(t):
                p = jnp.pad(t, ((0, 0), (0, 0), (1, 0), (0, 0), (0, 0)))
                return jnp.concatenate([p[:, :, :w], p[:, :, 1:]], axis=3)
            bk, bv = (look_around(bk), look_around(bv))
            bt = jnp.arange(n).reshape(w, WINDOW)
            btp = jnp.pad(bt, ((1, 0), (0, 0)), constant_values=-1)
            btk = jnp.concatenate([btp[:w], btp[1:]], axis=1)
            sim = jnp.einsum('bhwid,bhwjd->bhwij', bq, bk)
            i = bt[:, :, None]
            j = btk[:, None, :]
            mask = (i < j) | (i > j + WINDOW) | (j == -1)
            sim = jnp.where(mask, -jnp.finfo(sim.dtype).max, sim)
            attn = jax.nn.softmax(sim, axis=-1)
            out = jnp.einsum('bhwij,bhwjd->bhwid', attn, bv)
            return out.reshape(b, h, n, d)

        def _layer(x, wqkv, qs, ksc, wo, lg, lb, w1, b1, w2, b2):
            b, n, _ = x.shape
            h = shift_token(x)
            qkv = h @ wqkv
            q, k, v = jnp.split(qkv, 3, axis=-1)
            to_heads = lambda t: t.reshape(b, n, HEADS, DIM_HEAD).transpose(0, 2, 1, 3)
            q, k, v = (to_heads(q), to_heads(k), to_heads(v))
            q = l2norm(q) * qs
            k = l2norm(k) * ksc
            q, k = rotary_xpos(q, k)
            o = local_attention(q, k, v)
            o = o.transpose(0, 2, 1, 3).reshape(b, n, INNER)
            x = x + o @ wo
            h = shift_token(x)
            mu = h.mean(-1, keepdims=True)
            var = h.var(-1, keepdims=True)
            h = (h - mu) / jnp.sqrt(var + 1e-05) * lg + lb
            h = h @ w1 + b1
            a, g = jnp.split(h, 2, axis=-1)
            h = a * jax.nn.gelu(g, approximate=False)
            x = x + h @ w2 + b2
            return x
        key = jax.random.key(seed)
        ks = jax.random.split(key, 6)
        return {'x': jax.random.normal(ks[0], (B, N, DIM), jnp.float32), 'wqkv': jax.random.normal(ks[1], (DEPTH, DIM, 3 * INNER), jnp.float32) * 0.02, 'q_scale': jnp.ones((DEPTH, DIM_HEAD), jnp.float32), 'k_scale': jnp.ones((DEPTH, DIM_HEAD), jnp.float32), 'wo': jax.random.normal(ks[2], (DEPTH, INNER, DIM), jnp.float32) * 0.02, 'ln_g': jnp.ones((DEPTH, DIM), jnp.float32), 'ln_b': jnp.zeros((DEPTH, DIM), jnp.float32), 'w1': jax.random.normal(ks[3], (DEPTH, DIM, 2 * HID), jnp.float32) * 0.02, 'b1': jnp.zeros((DEPTH, 2 * HID), jnp.float32), 'w2': jax.random.normal(ks[4], (DEPTH, HID, DIM), jnp.float32) * 0.02, 'b2': jnp.zeros((DEPTH, DIM), jnp.float32)}
    _L0_ffn_all = _L0_ffn_setup()
    _L0_ffn_in = {k: v for k, v in _L0_ffn_all.items() if k in ('wqkv', 'q_scale', 'k_scale', 'wo', 'ln_g', 'ln_b', 'w1', 'b1', 'w2', 'b2')}
    del _L0_ffn_all

    def _L1_attn_setup():
        import jax, jax.numpy as jnp
        import numpy as np
        import math
        B, S, D_IN, D_KQ, D_OUT = (4, 256, 128, 128, 128)
        key = jax.random.key(seed)
        ks = jax.random.split(key, 7)
        sc = 0.02
        return {'x': jax.random.normal(ks[0], (B, S, D_IN), jnp.float32), 'Wq': jax.random.normal(ks[1], (D_KQ, D_IN), jnp.float32) * sc, 'bq': jax.random.normal(ks[2], (D_KQ,), jnp.float32) * sc, 'Wk': jax.random.normal(ks[3], (D_KQ, D_IN), jnp.float32) * sc, 'bk': jax.random.normal(ks[4], (D_KQ,), jnp.float32) * sc, 'Wv': jax.random.normal(ks[5], (D_OUT, D_IN), jnp.float32) * sc, 'bv': jax.random.normal(ks[6], (D_OUT,), jnp.float32) * sc}
    _L1_attn_all = _L1_attn_setup()
    _L1_attn_in = {k: v for k, v in _L1_attn_all.items() if k in ('Wq', 'bq', 'Wk', 'bk', 'Wv', 'bv')}
    del _L1_attn_all

    def _L1_xattn_setup():
        import jax, jax.numpy as jnp
        import numpy as np
        B, S, D = (2, 256, 128)
        H, HD = (16, 64)
        key = jax.random.key(seed)
        ks = jax.random.split(key, 10)
        scale = 1.0 / np.sqrt(D)
        inputs_q = jax.random.normal(ks[0], (B, S, D), dtype=jnp.float32)
        inputs_kv = inputs_q
        Wq = jax.random.normal(ks[1], (D, H, HD), dtype=jnp.float32) * scale
        Wk = jax.random.normal(ks[2], (D, H, HD), dtype=jnp.float32) * scale
        Wv = jax.random.normal(ks[3], (D, H, HD), dtype=jnp.float32) * scale
        Wo = jax.random.normal(ks[4], (H, HD, D), dtype=jnp.float32) * scale
        bq = jnp.zeros((H, HD), dtype=jnp.float32)
        bk = jnp.zeros((H, HD), dtype=jnp.float32)
        bv = jnp.zeros((H, HD), dtype=jnp.float32)
        bo = jnp.zeros((D,), dtype=jnp.float32)
        return {'inputs_q': inputs_q, 'inputs_kv': inputs_kv, 'Wq': Wq, 'bq': bq, 'Wk': Wk, 'bk': bk, 'Wv': Wv, 'bv': bv, 'Wo': Wo, 'bo': bo}
    _L1_xattn_all = _L1_xattn_setup()
    _L1_xattn_in = {k: v for k, v in _L1_xattn_all.items() if k in ('Wq', 'bq', 'Wk', 'bk', 'Wv', 'bv', 'Wo', 'bo')}
    del _L1_xattn_all

    def _L1_ffn_setup():
        import jax, jax.numpy as jnp
        import numpy as np
        MAX_VAL = 100.0
        key = jax.random.key(seed)
        k1, k2, k3 = jax.random.split(key, 3)
        B, S, D_IN, D_OUT = (4, 1024, 128, 128)
        x = jax.random.normal(k1, (B, S, D_IN), dtype=jnp.float32)
        weights = jax.random.normal(k2, (D_OUT, D_IN), dtype=jnp.float32)
        scale = jnp.ones((D_OUT,), dtype=jnp.float32)
        bias = jax.random.normal(k3, (D_OUT,), dtype=jnp.float32)
        return {'x': x, 'weights': weights, 'scale': scale, 'bias': bias}
    _L1_ffn_all = _L1_ffn_setup()
    _L1_ffn_in = {k: v for k, v in _L1_ffn_all.items() if k in ('weights', 'scale', 'bias')}
    del _L1_ffn_all
    return {'x': x, 'ctx_1024': ctx_1024, 'L0_attn_gamma': _L0_attn_in['gamma'], 'L0_attn_beta': _L0_attn_in['beta'], 'L0_attn_W_in': _L0_attn_in['W_in'], 'L0_attn_conv_w': _L0_attn_in['conv_w'], 'L0_attn_conv_b': _L0_attn_in['conv_b'], 'L0_attn_W_xp': _L0_attn_in['W_xp'], 'L0_attn_W_Bg': _L0_attn_in['W_Bg'], 'L0_attn_W_Cg': _L0_attn_in['W_Cg'], 'L0_attn_W_dt': _L0_attn_in['W_dt'], 'L0_attn_b_dt': _L0_attn_in['b_dt'], 'L0_attn_W_Bp': _L0_attn_in['W_Bp'], 'L0_attn_W_Cp': _L0_attn_in['W_Cp'], 'L0_attn_A': _L0_attn_in['A'], 'L0_attn_D_skip': _L0_attn_in['D_skip'], 'L0_attn_W_out': _L0_attn_in['W_out'], 'L0_xattn_w_q': _L0_xattn_in['w_q'], 'L0_xattn_b_q': _L0_xattn_in['b_q'], 'L0_xattn_w_k': _L0_xattn_in['w_k'], 'L0_xattn_b_k': _L0_xattn_in['b_k'], 'L0_xattn_w_v': _L0_xattn_in['w_v'], 'L0_xattn_b_v': _L0_xattn_in['b_v'], 'L0_xattn_w_0': _L0_xattn_in['w_0'], 'L0_xattn_b_0': _L0_xattn_in['b_0'], 'L0_ffn_wqkv': _L0_ffn_in['wqkv'], 'L0_ffn_q_scale': _L0_ffn_in['q_scale'], 'L0_ffn_k_scale': _L0_ffn_in['k_scale'], 'L0_ffn_wo': _L0_ffn_in['wo'], 'L0_ffn_ln_g': _L0_ffn_in['ln_g'], 'L0_ffn_ln_b': _L0_ffn_in['ln_b'], 'L0_ffn_w1': _L0_ffn_in['w1'], 'L0_ffn_b1': _L0_ffn_in['b1'], 'L0_ffn_w2': _L0_ffn_in['w2'], 'L0_ffn_b2': _L0_ffn_in['b2'], 'L1_attn_Wq': _L1_attn_in['Wq'], 'L1_attn_bq': _L1_attn_in['bq'], 'L1_attn_Wk': _L1_attn_in['Wk'], 'L1_attn_bk': _L1_attn_in['bk'], 'L1_attn_Wv': _L1_attn_in['Wv'], 'L1_attn_bv': _L1_attn_in['bv'], 'L1_xattn_Wq': _L1_xattn_in['Wq'], 'L1_xattn_bq': _L1_xattn_in['bq'], 'L1_xattn_Wk': _L1_xattn_in['Wk'], 'L1_xattn_bk': _L1_xattn_in['bk'], 'L1_xattn_Wv': _L1_xattn_in['Wv'], 'L1_xattn_bv': _L1_xattn_in['bv'], 'L1_xattn_Wo': _L1_xattn_in['Wo'], 'L1_xattn_bo': _L1_xattn_in['bo'], 'L1_ffn_weights': _L1_ffn_in['weights'], 'L1_ffn_scale': _L1_ffn_in['scale'], 'L1_ffn_bias': _L1_ffn_in['bias']}

def reference(x, ctx_1024, L0_attn_gamma, L0_attn_beta, L0_attn_W_in, L0_attn_conv_w, L0_attn_conv_b, L0_attn_W_xp, L0_attn_W_Bg, L0_attn_W_Cg, L0_attn_W_dt, L0_attn_b_dt, L0_attn_W_Bp, L0_attn_W_Cp, L0_attn_A, L0_attn_D_skip, L0_attn_W_out, L0_xattn_w_q, L0_xattn_b_q, L0_xattn_w_k, L0_xattn_b_k, L0_xattn_w_v, L0_xattn_b_v, L0_xattn_w_0, L0_xattn_b_0, L0_ffn_wqkv, L0_ffn_q_scale, L0_ffn_k_scale, L0_ffn_wo, L0_ffn_ln_g, L0_ffn_ln_b, L0_ffn_w1, L0_ffn_b1, L0_ffn_w2, L0_ffn_b2, L1_attn_Wq, L1_attn_bq, L1_attn_Wk, L1_attn_bk, L1_attn_Wv, L1_attn_bv, L1_xattn_Wq, L1_xattn_bq, L1_xattn_Wk, L1_xattn_bk, L1_xattn_Wv, L1_xattn_bv, L1_xattn_Wo, L1_xattn_bo, L1_ffn_weights, L1_ffn_scale, L1_ffn_bias):
    import jax
    import jax.numpy as jnp

    def _L0_attn_ref(x, gamma, beta, W_in, conv_w, conv_b, W_xp, W_Bg, W_Cg, W_dt, b_dt, W_Bp, W_Cp, A, D_skip, W_out):
        import jax, jax.numpy as jnp
        import numpy as np
        B, L, D = (2, 512, 128)
        DS, RK, K = (16, 64, 3)
        EPS = 1e-05
        d = x.shape[-1]
        mu = jnp.mean(x, -1, keepdims=True)
        var = jnp.mean(jnp.square(x - mu), -1, keepdims=True)
        xn = (x - mu) * jax.lax.rsqrt(var + EPS) * gamma + beta
        xz = xn @ W_in
        xb, z = jnp.split(xz, 2, axis=-1)
        xc = jax.lax.conv_general_dilated(xb, conv_w, window_strides=(1,), padding='SAME', dimension_numbers=('NWC', 'WIO', 'NWC'), feature_group_count=d) + conv_b
        x_act = jax.nn.silu(xc)
        delta = jax.nn.softplus(x_act @ W_xp @ W_dt + b_dt)
        Bm = x_act @ W_Bg @ W_Bp
        Cm = x_act @ W_Cg @ W_Cp
        dA = jnp.exp(delta * A)
        dBx = delta * Bm * x_act

        def step(h, ab):
            a, bx = ab
            h = a * h + bx
            return (h, h)
        h0 = jnp.zeros_like(dA[:, 0])
        _, hs = jax.lax.scan(step, h0, (dA.transpose(1, 0, 2), dBx.transpose(1, 0, 2)))
        y = Cm * hs.transpose(1, 0, 2)
        out_ssm = y + x_act * D_skip
        gated = out_ssm * jax.nn.silu(z)
        return gated @ W_out + x

    def _L0_xattn_ref(q, k, v, w_q, b_q, w_k, b_k, w_v, b_v, w_0, b_0):
        import jax, jax.numpy as jnp
        import numpy as np
        D_MODEL = 128
        NUM_HEADS = 16
        D_K = D_MODEL // NUM_HEADS
        B = q.shape[0]
        H, dk = (NUM_HEADS, D_K)

        def split_heads(x):
            return x.reshape(B, -1, H, dk).transpose(0, 2, 1, 3)
        qh = split_heads(q @ w_q + b_q)
        kh = split_heads(k @ w_k + b_k)
        vh = split_heads(v @ w_v + b_v)
        scores = jnp.einsum('bhsd,bhtd->bhst', qh, kh) / np.sqrt(dk).astype(jnp.float32)
        dists = jax.nn.softmax(scores, axis=-1)
        attn = jnp.einsum('bhst,bhtd->bhsd', dists, vh)
        attn = attn.reshape(B, -1, D_MODEL)
        return attn @ w_0 + b_0

    def _L0_ffn_ref(x, wqkv, q_scale, k_scale, wo, ln_g, ln_b, w1, b1, w2, b2):
        import jax, jax.numpy as jnp
        import numpy as np
        DIM = 128
        DEPTH = 2
        HEADS = 8
        DIM_HEAD = 64
        WINDOW = 64
        INNER = HEADS * DIM_HEAD
        HID = int(DIM * 4 * 2 / 3)
        B, N = (2, 1024)
        QK_SCALE = 8.0

        def shift_token(t):
            t1, t2 = jnp.split(t, 2, axis=-1)
            t2 = jnp.pad(t2, ((0, 0), (1, 0), (0, 0)))[:, :-1]
            return jnp.concatenate([t1, t2], axis=-1)

        def l2norm(t):
            return t / jnp.clip(jnp.linalg.norm(t, axis=-1, keepdims=True), 1e-12)

        def rotate_half(x):
            x1, x2 = jnp.split(x, 2, axis=-1)
            return jnp.concatenate([-x2, x1], axis=-1)

        def rotary_xpos(q, k):
            n = q.shape[-2]
            half_idx = jnp.arange(0, DIM_HEAD, 2, dtype=jnp.float32)
            inv_freq = 1.0 / 10000.0 ** (half_idx / DIM_HEAD)
            t = jnp.arange(n, dtype=jnp.float32)
            freqs = t[:, None] * inv_freq[None, :]
            freqs = jnp.concatenate([freqs, freqs], axis=-1)
            base = (half_idx + 0.4 * DIM_HEAD) / (1.4 * DIM_HEAD)
            power = (t - n // 2) / float(WINDOW // 2)
            scale = base[None, :] ** power[:, None]
            scale = jnp.concatenate([scale, scale], axis=-1)
            cos, sin = (jnp.cos(freqs), jnp.sin(freqs))
            q = q * cos * scale + rotate_half(q) * sin * scale
            k = k * cos / scale + rotate_half(k) * sin / scale
            return (q, k)

        def local_attention(q, k, v):
            b, h, n, d = q.shape
            w = n // WINDOW
            bq = q.reshape(b, h, w, WINDOW, d) * QK_SCALE
            bk = k.reshape(b, h, w, WINDOW, d)
            bv = v.reshape(b, h, w, WINDOW, d)

            def look_around(t):
                p = jnp.pad(t, ((0, 0), (0, 0), (1, 0), (0, 0), (0, 0)))
                return jnp.concatenate([p[:, :, :w], p[:, :, 1:]], axis=3)
            bk, bv = (look_around(bk), look_around(bv))
            bt = jnp.arange(n).reshape(w, WINDOW)
            btp = jnp.pad(bt, ((1, 0), (0, 0)), constant_values=-1)
            btk = jnp.concatenate([btp[:w], btp[1:]], axis=1)
            sim = jnp.einsum('bhwid,bhwjd->bhwij', bq, bk)
            i = bt[:, :, None]
            j = btk[:, None, :]
            mask = (i < j) | (i > j + WINDOW) | (j == -1)
            sim = jnp.where(mask, -jnp.finfo(sim.dtype).max, sim)
            attn = jax.nn.softmax(sim, axis=-1)
            out = jnp.einsum('bhwij,bhwjd->bhwid', attn, bv)
            return out.reshape(b, h, n, d)

        def _layer(x, wqkv, qs, ksc, wo, lg, lb, w1, b1, w2, b2):
            b, n, _ = x.shape
            h = shift_token(x)
            qkv = h @ wqkv
            q, k, v = jnp.split(qkv, 3, axis=-1)
            to_heads = lambda t: t.reshape(b, n, HEADS, DIM_HEAD).transpose(0, 2, 1, 3)
            q, k, v = (to_heads(q), to_heads(k), to_heads(v))
            q = l2norm(q) * qs
            k = l2norm(k) * ksc
            q, k = rotary_xpos(q, k)
            o = local_attention(q, k, v)
            o = o.transpose(0, 2, 1, 3).reshape(b, n, INNER)
            x = x + o @ wo
            h = shift_token(x)
            mu = h.mean(-1, keepdims=True)
            var = h.var(-1, keepdims=True)
            h = (h - mu) / jnp.sqrt(var + 1e-05) * lg + lb
            h = h @ w1 + b1
            a, g = jnp.split(h, 2, axis=-1)
            h = a * jax.nn.gelu(g, approximate=False)
            x = x + h @ w2 + b2
            return x
        for l in range(DEPTH):
            x = _layer(x, wqkv[l], q_scale[l], k_scale[l], wo[l], ln_g[l], ln_b[l], w1[l], b1[l], w2[l], b2[l])
        return x

    def _L1_attn_ref(x, Wq, bq, Wk, bk, Wv, bv):
        import jax, jax.numpy as jnp
        import numpy as np
        import math
        B, S, D_IN, D_KQ, D_OUT = (4, 256, 128, 128, 128)
        Q = jnp.einsum('bsd,kd->bsk', x, Wq) + bq
        K = jnp.einsum('bsd,kd->bsk', x, Wk) + bk
        V = jnp.einsum('bsd,od->bso', x, Wv) + bv
        scale = 1.0 / math.sqrt(D_KQ)
        attn = jnp.einsum('bqk,bsk->bqs', Q, K) * scale
        s = attn.shape[-1]
        causal = jnp.tril(jnp.ones((s, s), dtype=bool))
        attn = jnp.where(causal[None, :, :], attn, -jnp.inf)
        attn = jax.nn.softmax(attn, axis=-1)
        Z = jnp.einsum('bqs,bso->bqo', attn, V)
        return Z

    def _L1_xattn_ref(inputs_q, inputs_kv, Wq, bq, Wk, bk, Wv, bv, Wo, bo):
        import jax, jax.numpy as jnp
        import numpy as np
        B, S, D = (2, 256, 128)
        H, HD = (16, 64)
        q = jnp.einsum('bsd,dhe->bshe', inputs_q, Wq) + bq
        k = jnp.einsum('bsd,dhe->bshe', inputs_kv, Wk) + bk
        v = jnp.einsum('bsd,dhe->bshe', inputs_kv, Wv) + bv
        q = q / jnp.sqrt(jnp.asarray(HD, dtype=q.dtype))
        scores = jnp.einsum('bqhd,bkhd->bhqk', q, k)
        weights = jax.nn.softmax(scores, axis=-1)
        ctx = jnp.einsum('bhqk,bkhd->bqhd', weights, v)
        out = jnp.einsum('bqhd,hde->bqe', ctx, Wo) + bo
        return out

    def _L1_ffn_ref(x, weights, scale, bias):
        import jax, jax.numpy as jnp
        import numpy as np
        MAX_VAL = 100.0
        w = (weights >= 0.0).astype(x.dtype) * 2.0 - 1.0
        y = jnp.einsum('bsi,oi->bso', x, w)
        y = y * scale + bias
        y = jnp.clip(y, -MAX_VAL, MAX_VAL)
        return y
    x = x + _L0_attn_ref(_layernorm(x, axis=-1), L0_attn_gamma, L0_attn_beta, L0_attn_W_in, L0_attn_conv_w, L0_attn_conv_b, L0_attn_W_xp, L0_attn_W_Bg, L0_attn_W_Cg, L0_attn_W_dt, L0_attn_b_dt, L0_attn_W_Bp, L0_attn_W_Cp, L0_attn_A, L0_attn_D_skip, L0_attn_W_out)
    x = x + _L0_xattn_ref(_layernorm(x, axis=-1), ctx_1024, ctx_1024, L0_xattn_w_q, L0_xattn_b_q, L0_xattn_w_k, L0_xattn_b_k, L0_xattn_w_v, L0_xattn_b_v, L0_xattn_w_0, L0_xattn_b_0)
    x = x + _L0_ffn_ref(_layernorm(x, axis=-1), L0_ffn_wqkv, L0_ffn_q_scale, L0_ffn_k_scale, L0_ffn_wo, L0_ffn_ln_g, L0_ffn_ln_b, L0_ffn_w1, L0_ffn_b1, L0_ffn_w2, L0_ffn_b2)
    x = x + _L1_attn_ref(_layernorm(x, axis=-1), L1_attn_Wq, L1_attn_bq, L1_attn_Wk, L1_attn_bk, L1_attn_Wv, L1_attn_bv)
    x = x + _L1_xattn_ref(_layernorm(x, axis=-1), ctx_1024, L1_xattn_Wq, L1_xattn_bq, L1_xattn_Wk, L1_xattn_bk, L1_xattn_Wv, L1_xattn_bv, L1_xattn_Wo, L1_xattn_bo)
    x = x + _L1_ffn_ref(_layernorm(x, axis=-1), L1_ffn_weights, L1_ffn_scale, L1_ffn_bias)
    return x

_drawn_inputs = setup_inputs


def setup_inputs(seed=0):
    import zlib

    import numpy as np

    out = dict(_drawn_inputs(seed))
    spreads = {'L0_attn_gamma': (1.0, 0.6),
     'L0_attn_beta': (0.0, 0.8),
     'L0_attn_conv_b': (0.0, 0.8),
     'L0_attn_b_dt': (0.0, 0.8),
     'L0_attn_D_skip': (1.0, 0.6),
     'L0_ffn_q_scale': (1.0, 0.6),
     'L0_ffn_k_scale': (1.0, 0.6),
     'L0_ffn_ln_g': (1.0, 0.6),
     'L0_ffn_ln_b': (0.0, 0.8),
     'L0_ffn_b1': (0.0, 0.8),
     'L0_ffn_b2': (0.0, 0.8),
     'L1_xattn_bq': (0.0, 2.0),
     'L1_xattn_bk': (0.0, 2.0),
     'L1_xattn_bv': (0.0, 0.8),
     'L1_xattn_bo': (0.0, 2.0),
     'L1_ffn_scale': (1.0, 0.2)}
    factors = {'L0_attn_W_in': 8.0,
     'L0_attn_conv_w': 8.0,
     'L0_attn_W_xp': 8.0,
     'L0_attn_W_Bg': 8.0,
     'L0_attn_W_Cg': 8.0,
     'L0_attn_W_dt': 8.0,
     'L0_attn_W_Bp': 8.0,
     'L0_attn_W_Cp': 8.0,
     'L0_attn_A': 8.0,
     'L0_attn_W_out': 8.0,
     'L0_xattn_b_q': 6.912,
     'L0_xattn_b_k': 64.0,
     'L0_ffn_wqkv': 5.2,
     'L0_ffn_wo': 5.272,
     'L0_ffn_w1': 8.0,
     'L0_ffn_w2': 8.0,
     'L1_attn_Wq': 49.189,
     'L1_attn_bq': 64.0,
     'L1_attn_Wk': 49.784,
     'L1_attn_bk': 64.0,
     'L1_attn_Wv': 13.549,
     'L1_attn_bv': 64.0,
     'L1_xattn_Wq': 3.966,
     'L1_xattn_Wk': 3.717}
    for name, (base, spread) in spreads.items():
        noise = np.random.default_rng([zlib.crc32(name.encode()), seed]).standard_normal(out[name].shape)
        drawn = base * np.exp(spread * noise) if base else spread * noise
        out[name] = jnp.asarray(drawn.astype(out[name].dtype))
    for name, factor in factors.items():
        out[name] = (out[name] * factor).astype(out[name].dtype)
    return out
```

```python
from contextlib import ExitStack

import concourse.bass as bass
from concourse import mybir

F32 = mybir.dt.float32
BF16 = mybir.dt.bfloat16
I32 = mybir.dt.int32
ALU = mybir.AluOpType
ACT = mybir.ActivationFunctionType
AX = mybir.AxisListType

P = 128
BANK = 512
EPS = 1e-5


def wait(eng, sem, value):
    if not isinstance(value, int) or value > 0:
        eng.wait_ge(sem, value)


class Order:

    def __init__(self, eng, sem):
        self.eng, self.sem, self.n = eng, sem, 0

    def done(self, ins):
        self.n += 1
        ins.then_inc(self.sem, 1)
        self.eng.wait_ge(self.sem, self.n)


class Stage:

    def __init__(self, nc, ctx, sems, name):
        self.nc, self.ctx, self.sems, self.name = nc, ctx, sems, name

    def sb(self, name, shape, dt=F32):
        return self.ctx.enter_context(self.nc.sbuf_tensor(f"{self.name}_{name}", shape, dt))

    def sem(self, name):
        return self.sems.new(f"{self.name}_{name}")


class Semaphores:

    def __init__(self, nc, ctx):
        self.nc, self.ctx, self.held = nc, ctx, []

    def new(self, name):
        self.held.append(self.ctx.enter_context(self.nc.semaphore(name)))
        return self.held[-1]

    def clear(self):
        with self.nc.Block() as block:
            @block.sync
            def _(sp):
                for sem in self.held:
                    sp.sem_clear(sem)


def column(ap):
    return ap.rearrange("(p o) -> p o", o=1)


def norm_vector(dve, order, src, dst, sq, st, var_ready, std_ready, count):
    n = src.shape[1]
    wide = [P, n, P]
    order.done(dve.tensor_reduce(st[:, 0, :], src, AX.X, ALU.add))
    order.done(dve.tensor_scalar(st[:, 0, :], st[:, 0, :], 1.0 / P, None, ALU.mult))
    order.done(dve.tensor_tensor(dst, src, st[:, 0, :].unsqueeze(2).to_broadcast(wide), ALU.subtract))
    order.done(dve.tensor_tensor(sq, dst, dst, ALU.mult))
    order.done(dve.tensor_reduce(st[:, 1, :], sq, AX.X, ALU.add))
    dve.tensor_scalar(st[:, 1, :], st[:, 1, :], 1.0 / P, EPS, ALU.mult, ALU.add).then_inc(var_ready, 1)
    dve.wait_ge(std_ready, count)
    order.done(dve.reciprocal(st[:, 2, :], st[:, 1, :]))
    order.done(dve.tensor_tensor(dst, dst, st[:, 2, :].unsqueeze(2).to_broadcast(wide), ALU.mult))


def norm_scalar(act, st, var_ready, std_ready, count):
    act.wait_ge(var_ready, count)
    act.activation(st[:, 1, :], st[:, 1, :], ACT.Sqrt).then_inc(std_ready, 1)


def load_stage(nc, g, d):
    with ExitStack() as ctx:
        s = Stage(nc, ctx, g.sems, "load")
        x_loaded = s.sem("x_loaded")
        zeroed, made = s.sem("zeroed"), s.sem("made")
        block = ctx.enter_context(nc.Block())

        @block.sync
        def _(sp):
            sp.dma_start(g.x[:, :, :], d["x"].rearrange("b (t p) c -> p (b t) c", p=P)).then_inc(x_loaded, 16)
            sp.wait_ge(x_loaded, 16)

        @block.gpsimd
        def _(pool):
            pool.memset(g.ident[:, :], 0.0).then_inc(zeroed, 1)
            pool.memset(g.identb[:, :], 0.0).then_inc(zeroed, 1)
            pool.memset(g.causal[:, :], 0.0).then_inc(zeroed, 1)
            pool.wait_ge(zeroed, 3)
            for m in (g.ident, g.identb):
                pool.affine_select(out=m[:, :], in_=m[:, :], compare_op=ALU.not_equal, fill=1.0, base=0,
                                   pattern=[[-1, P]], channel_multiplier=1).then_inc(made, 1)
            for col, n, first in ((0, P, 0), (P, 2 * P, P)):
                m = g.causal[:, col:col + n]
                pool.affine_select(out=m, in_=m, compare_op=ALU.is_ge, fill=MASKED, base=first,
                                   pattern=[[-1, n]], channel_multiplier=1).then_inc(made, 1)
            pool.wait_ge(made, 4)
            for col, n, first in ((0, P, 0), (P, 2 * P, P)):
                pool.affine_select(out=g.band[:, col:col + n], in_=g.causal[:, col:col + n], compare_op=ALU.is_ge,
                                   fill=MASKED, base=WINDOW - first, pattern=[[1, n]],
                                   channel_multiplier=-1).then_inc(made, 1)


MASKED = -1.0e25
WINDOW = 64


def scan_stage(nc, g, d):
    tokens = g.x.shape[1] * P
    T = tokens // P
    B, L = 8, tokens // 8
    with ExitStack() as ctx:
        s = Stage(nc, ctx, g.sems, "scan")
        h0 = s.sb("h0", [P, T, P])
        hn = s.sb("hn", [P, T, P])
        sq = s.sb("sq", [P, T, P])
        st = s.sb("st", [P, 3, T])
        hT = s.sb("hT", [P, tokens])
        xc = s.sb("xc", [P, tokens])
        xa = s.sb("xa", [P, tokens])
        zs = s.sb("zs", [P, tokens])
        low = s.sb("low", [112, tokens])
        v = s.sb("v", [P, tokens])
        e = s.sb("e", [P, tokens])
        u = s.sb("u", [P, tokens])
        small = s.sb("small", [P, tokens], I32)
        series = s.sb("series", [P, tokens])
        dA = s.sb("dA", [P, tokens])
        w_in = s.sb("w_in", [P, 2 * P])
        w_low = s.sb("w_low", [P, 112])
        w_up = s.sb("w_up", [112, P])
        w_out = s.sb("w_out", [P, P])
        conv = s.sb("conv", [P, 3])
        cols = s.sb("cols", [P, 6])
        gamma, beta, conv_b, b_dt, A, skip = (cols[:, i:i + 1] for i in range(6))
        loaded, gap_zeroed = s.sem("loaded"), s.sem("gap_zeroed")
        var_ready, std_ready = s.sem("var_ready"), s.sem("std_ready")
        hn_ready, hn_transposed, hT_ready = s.sem("hn_ready"), s.sem("hn_transposed"), s.sem("hT_ready")
        xb_ready, z_ready, zs_ready = s.sem("xb_ready"), s.sem("z_ready"), s.sem("zs_ready")
        xc_ready, xa_ready = s.sem("xc_ready"), s.sem("xa_ready")
        low_product, low_ready = s.sem("low_product"), s.sem("low_ready")
        v_product, bm_product, cm_product = s.sem("v_product"), s.sem("bm_product"), s.sem("cm_product")
        v_ready, e_ready, u_ready, log_ready = s.sem("v_ready"), s.sem("e_ready"), s.sem("u_ready"), s.sem("log_ready")
        delta_ready, dA_ready = s.sem("delta_ready"), s.sem("dA_ready")
        gated_ready, out_product = s.sem("gated_ready"), s.sem("out_product")
        dve_order, act_order = s.sem("dve_order"), s.sem("act_order")
        LOADS = 15
        ps = g.ps
        lo, hi = ps[:, 0:tokens], ps[:, tokens:2 * tokens]
        block = ctx.enter_context(nc.Block())

        @block.sync
        def _(sp):
            pairs = [(w_in[:, :], d["L0_attn_W_in"]), (w_out[:, :], d["L0_attn_W_out"])]
            pairs += [(c, column(d["L0_attn_" + n])) for c, n in (
                (gamma, "gamma"), (beta, "beta"), (conv_b, "conv_b"), (b_dt, "b_dt"), (A, "A"), (skip, "D_skip"))]
            for dst, src in pairs:
                sp.dma_start(dst, src).then_inc(loaded, 16)
            for k in range(3):
                sp.dma_start(conv[:, k:k + 1], d["L0_attn_conv_w"][k].rearrange("o c -> c o")).then_inc(loaded, 16)
            sp.dma_start(w_up[0:64, :], d["L0_attn_W_dt"]).then_inc(loaded, 16)
            sp.dma_start(w_up[64:80, :], d["L0_attn_W_Bp"]).then_inc(loaded, 16)
            sp.dma_start(w_up[96:112, :], d["L0_attn_W_Cp"]).then_inc(loaded, 16)
            sp.wait_ge(gap_zeroed, 1)
            sp.dma_start(w_low[:, 0:64], d["L0_attn_W_xp"]).then_inc(loaded, 16)
            sp.dma_start(w_low[:, 64:80], d["L0_attn_W_Bg"]).then_inc(loaded, 16)
            sp.dma_start(w_low[:, 96:112], d["L0_attn_W_Cg"]).then_inc(loaded, 16)

        @block.gpsimd
        def _(pool):
            pool.memset(w_low[:, :], 0.0).then_inc(gap_zeroed, 1)

        @block.vector
        def _(dve):
            order = Order(dve, dve_order)
            norm_vector(dve, order, g.x[:, :, :], h0[:, :, :], sq[:, :, :], st, var_ready, std_ready, 1)
            norm_vector(dve, order, h0[:, :, :], hn[:, :, :], sq[:, :, :], st, var_ready, std_ready, 2)
            order.done(dve.tensor_tensor(g.x[:, :, :], g.x[:, :, :], h0[:, :, :], ALU.add))
            dve.sem_inc(hn_ready, 1)
            dve.wait_ge(xb_ready, 1)
            dve.wait_ge(loaded, 16 * (LOADS + 2))
            order.done(dve.tensor_scalar(xc[:, :], hi, conv[:, 1:2], conv_b, ALU.mult, ALU.add))
            c3, x3 = xc[:, :].rearrange("p (b l) -> p b l", b=B), hi.rearrange("p (b l) -> p b l", b=B)
            order.done(dve.scalar_tensor_tensor(out=c3[:, :, 1:L], in0=x3[:, :, 0:L - 1], scalar=conv[:, 0:1],
                                                in1=c3[:, :, 1:L], op0=ALU.mult, op1=ALU.add))
            dve.scalar_tensor_tensor(out=c3[:, :, 0:L - 1], in0=x3[:, :, 1:L], scalar=conv[:, 2:3],
                                     in1=c3[:, :, 0:L - 1], op0=ALU.mult, op1=ALU.add).then_inc(xc_ready, 1)
            dve.wait_ge(v_product, 1)
            dve.tensor_scalar(v[:, :], lo, b_dt, None, ALU.add).then_inc(v_ready, 1)
            dve.wait_ge(e_ready, 1)
            order.done(dve.tensor_scalar(series[:, :], e[:, :], 1.0 / 3, -0.5, ALU.mult, ALU.add))
            order.done(dve.tensor_scalar(small[:, :], e[:, :], 2.0 ** -7, None, ALU.is_lt))
            order.done(dve.tensor_tensor(series[:, :], series[:, :], e[:, :], ALU.mult))
            order.done(dve.scalar_tensor_tensor(out=series[:, :], in0=series[:, :], scalar=1.0, in1=e[:, :],
                                                op0=ALU.add, op1=ALU.mult))
            dve.wait_ge(log_ready, 1)
            order.done(dve.copy_predicated(u[:, :], small[:, :], series[:, :]))
            dve.scalar_tensor_tensor(out=v[:, :], in0=v[:, :], scalar=0.0, in1=u[:, :], op0=ALU.max,
                                     op1=ALU.add).then_inc(delta_ready, 1)
            dve.wait_ge(delta_ready, 1)
            dve.wait_ge(bm_product, 1)
            order.done(dve.tensor_tensor(e[:, :], v[:, :], hi, ALU.mult))
            order.done(dve.tensor_tensor(e[:, :], e[:, :], xa[:, :], ALU.mult))
            dve.wait_ge(dA_ready, 1)
            for b in range(B):
                c = slice(b * L, (b + 1) * L)
                order.done(dve.tensor_tensor_scan(u[:, c], dA[:, c], e[:, c], 0.0, ALU.mult, ALU.add))
            dve.wait_ge(cm_product, 1)
            order.done(dve.tensor_tensor(u[:, :], u[:, :], lo, ALU.mult))
            order.done(dve.scalar_tensor_tensor(out=u[:, :], in0=xa[:, :], scalar=skip, in1=u[:, :],
                                                op0=ALU.mult, op1=ALU.add))
            dve.wait_ge(zs_ready, 1)
            dve.tensor_tensor(u[:, :], u[:, :], zs[:, :], ALU.mult).then_inc(gated_ready, 1)
            dve.wait_ge(out_product, 1)
            dve.tensor_tensor(g.x[:, :, :], g.x[:, :, :], hi.rearrange("p (t c) -> p t c", c=P), ALU.add)

        @block.scalar
        def _(act):
            order = Order(act, act_order)
            norm_scalar(act, st, var_ready, std_ready, 1)
            norm_scalar(act, st, var_ready, std_ready, 2)
            act.wait_ge(loaded, 16 * (LOADS + 2))
            act.wait_ge(hn_transposed, 1)
            act.activation(hT[:, :], lo, ACT.Identity, bias=beta, scale=gamma).then_inc(hT_ready, 1)
            act.wait_ge(z_ready, 1)
            act.activation(zs[:, :], lo, ACT.Silu).then_inc(zs_ready, 1)
            act.wait_ge(xc_ready, 1)
            act.activation(xa[:, :], xc[:, :], ACT.Silu).then_inc(xa_ready, 1)
            act.wait_ge(low_product, 1)
            act.activation(low[:, :], hi[0:112, :], ACT.Copy).then_inc(low_ready, 1)
            act.wait_ge(v_ready, 1)
            order.done(act.activation(e[:, :], v[:, :], ACT.Abs))
            act.activation(e[:, :], e[:, :], ACT.Exp, scale=-1.0).then_inc(e_ready, 1)
            act.wait_ge(e_ready, 1)
            act.activation(u[:, :], e[:, :], ACT.Ln, bias=1.0).then_inc(log_ready, 1)
            act.wait_ge(delta_ready, 1)
            act.activation(dA[:, :], v[:, :], ACT.Exp, scale=A).then_inc(dA_ready, 1)

        @block.tensor
        def _(pe):
            def product(base, lhsT, rhs, rows=P):
                for n in range(tokens // BANK):
                    c = slice(n * BANK, (n + 1) * BANK)
                    last = pe.matmul(ps[0:rows, base + n * BANK:base + (n + 1) * BANK], lhsT, rhs[:, c],
                                     start=True, stop=True)
                return last

            pe.wait_ge(hn_ready, 1)
            for t in range(T):
                last = pe.transpose(ps[:, t * P:(t + 1) * P], hn[:, t, :], g.ident[:, :])
            last.then_inc(hn_transposed, 1)
            pe.wait_ge(hT_ready, 1)
            product(tokens, w_in[:, 0:P], hT).then_inc(xb_ready, 1)
            product(0, w_in[:, P:2 * P], hT).then_inc(z_ready, 1)
            pe.wait_ge(xa_ready, 1)
            product(tokens, w_low[:, :], xa, 112).then_inc(low_product, 1)
            pe.wait_ge(low_ready, 1)
            pe.wait_ge(zs_ready, 1)
            product(0, w_up[0:64, :], low[0:64, :]).then_inc(v_product, 1)
            product(tokens, w_up[64:80, :], low[64:80, :]).then_inc(bm_product, 1)
            pe.wait_ge(v_ready, 1)
            product(0, w_up[96:112, :], low[96:112, :]).then_inc(cm_product, 1)
            pe.wait_ge(gated_ready, 1)
            for t in range(T):
                last = pe.matmul(ps[:, tokens + t * P:tokens + (t + 1) * P], u[:, t * P:(t + 1) * P], w_out[:, :],
                                 start=True, stop=True)
            last.then_inc(out_product, 1)


HEADS = 16
BATCHES = 8
TILES = 16
KEYS = 1601
KT = (KEYS + P - 1) // P
TAIL = KEYS - (KT - 1) * P
SPLIT = ((0, 401), (401, 400), (801, 400), (1201, 400))
GROUPS = ((0, 4), (4, 4), (8, 4), (12, 1))


def load_context(sp, d, b, dst, loaded):
    c = d["ctx_1024"][b]
    whole = (KT - 1) * P
    sp.dma_start(dst[:, 0:KT - 1, :], c[0:whole, :].rearrange("(t p) c -> p t c", p=P)).then_inc(loaded, 16)
    sp.dma_start(dst[0:TAIL, KT - 1, :], c[whole:KEYS, :]).then_inc(loaded, 16)


def context_stage(nc, g, d):
    with ExitStack() as ctx:
        s = Stage(nc, ctx, g.sems, "context")
        raw = [s.sb(f"raw{i}", [P, KT, P]) for i in range(2)]
        raw_loaded = [s.sem(f"raw_loaded{i}") for i in range(2)]
        transposed = [s.sem(f"transposed{i}") for i in range(2)]
        copied = [s.sem(f"copied{i}") for i in range(2)]
        block = ctx.enter_context(nc.Block())

        def bank(n):
            return g.ps[:, (n % 8) * BANK:(n % 8 + 1) * BANK]

        @block.sync
        def _(sp):
            for b in range(BATCHES):
                wait(sp, transposed[1], 2 * b - 2)
                load_context(sp, d, b, raw[b % 2], raw_loaded[b % 2])

        @block.tensor
        def _(pe):
            for b in range(BATCHES):
                pe.wait_ge(raw_loaded[b % 2], 32 * (b // 2 + 1))
                for j, (t0, n) in enumerate(GROUPS):
                    wait(pe, copied[j % 2], 2 * (b - 2) + j // 2 + 1)
                    for i in range(n):
                        rows = P if t0 + i < KT - 1 else TAIL
                        last = pe.transpose(bank(4 * b + j)[:, i * P:i * P + rows], raw[b % 2][0:rows, t0 + i, :],
                                            g.ident[0:rows, 0:rows])
                    last.then_inc(transposed[j % 2], 1)

        def copies(eng, side, copy):
            for b in range(BATCHES):
                for j in (side, side + 2):
                    t0, n = GROUPS[j]
                    cols = min(n * P, KEYS - t0 * P)
                    eng.wait_ge(transposed[side], 2 * b + j // 2 + 1)
                    copy(g.ctxT[:, b, t0 * P:t0 * P + cols], bank(4 * b + j)[:, 0:cols]).then_inc(copied[side], 1)

        @block.scalar
        def _(act):
            copies(act, 0, lambda o, i: act.activation(o, i, ACT.Copy))

        @block.vector
        def _(dve):
            copies(dve, 1, dve.tensor_copy)


def transpose_tokens(g, pe, src, base, done):
    for t in range(TILES):
        last = pe.transpose(g.ps[:, base + t * P:base + (t + 1) * P], src[:, t, :], g.ident[:, :])
    last.then_inc(done, 1)


def cross_stage(nc, g, d, name, q_name, k_name, v_name, o_name, scale, merged):
    def weight(n):
        low, up = f"{name}_w_{n}", f"{name}_W{n}"
        return d[low] if low in d else d[up]

    def bias(n):
        low, up = f"{name}_b_{n}", f"{name}_b{n}"
        ap = d[low] if low in d else d[up]
        return ap.rearrange("h e -> (h e)") if len(ap.shape) > 1 else ap

    def columns(ap):
        return ap.rearrange("c h e -> c (h e)") if len(ap.shape) > 2 else ap

    wq, wk, wv = (columns(weight(n)) for n in (q_name, k_name, v_name))
    wo = weight(o_name)
    wo = wo.rearrange("h e c -> (h e) c") if len(wo.shape) > 2 else wo
    with ExitStack() as ctx:
        so = Stage(nc, ctx, g.sems, name)
        A = so.sb("A", [P, HEADS, P + 1])
        B = so.sb("B", [P, HEADS, P])
        cb = so.sb("cb", [P, TILES, HEADS])
        hT = so.sb("hT", [P, TILES * P])
        biases = [bias(n) for n in (q_name, k_name, v_name, o_name)]
        fold_weights(nc, g, name, A, B, cb, hT, scale, merged, wq, wk, wv, wo, *biases)
        if merged:
            cross_heads(nc, g, d, name, A, B, cb, hT, g.x, P)
        else:
            dh = wq.shape[1] // HEADS
            heads_out = so.sb("heads_out", [P, TILES, HEADS * dh])
            cross_heads(nc, g, d, name, A, B, cb, hT, heads_out, dh)
            reshuffled_output(nc, g, name, heads_out, wo, biases[2], dh)


def reshuffled_output(nc, g, name, heads_out, wo, bv, dh):
    shuffle = nc.dram_tensor(name + "_shuffle", (BATCHES, HEADS, 2, P, dh), F32, kind="Internal").ap()
    with ExitStack() as ctx:
        s = Stage(nc, ctx, g.sems, name + "_out")
        rows = s.sb("rows", [P, TILES, P])
        rowsT = s.sb("rowsT", [P, TILES * P])
        wo_sb = s.sb("wo", [P, P])
        bv_rows = s.sb("bv_rows", [P, P])
        biased = s.sem("biased")
        spread, gathered, w_loaded = s.sem("spread"), s.sem("gathered"), s.sem("w_loaded")
        rows_transposed, rowsT_ready, product_done = s.sem("rows_transposed"), s.sem("rowsT_ready"), s.sem("product_done")
        block = ctx.enter_context(nc.Block())

        @block.sync
        def _(sp):
            sp.dma_start(bv_rows[:, :], bv.partition_broadcast(P)).then_inc(w_loaded, 16)
            sp.dma_start(wo_sb[:, :], wo).then_inc(w_loaded, 16)
            sp.wait_ge(biased, 1)
            for b in range(BATCHES):
                for q in range(2):
                    sp.dma_start(shuffle[b, :, q].rearrange("h p e -> p h e"),
                                 heads_out[:, 2 * b + q, :].rearrange("p (h e) -> p h e", e=dh)).then_inc(spread, 16)
            sp.wait_ge(spread, 16 * TILES)
            sp.dma_start(rows[:, :, :], shuffle.rearrange("b h q p e -> (b h q p e)").rearrange("(t p c) -> p t c", p=P, c=P))\
                .then_inc(gathered, 16)

        @block.tensor
        def _(pe):
            pe.wait_ge(gathered, 16)
            transpose_tokens(g, pe, rows, 0, rows_transposed)
            pe.wait_ge(rowsT_ready, 1)
            pe.wait_ge(w_loaded, 32)
            for t in range(TILES):
                last = pe.matmul(g.ps[:, (TILES + t) * P:(TILES + t + 1) * P], rowsT[:, t * P:(t + 1) * P], wo_sb[:, :],
                                 start=True, stop=True)
            last.then_inc(product_done, 1)

        @block.scalar
        def _(act):
            act.wait_ge(rows_transposed, 1)
            act.activation(rowsT[:, :], g.ps[:, 0:TILES * P], ACT.Copy).then_inc(rowsT_ready, 1)

        @block.vector
        def _(dve):
            dve.wait_ge(w_loaded, 32)
            dve.tensor_tensor(heads_out[:, :, :], heads_out[:, :, :],
                              bv_rows[:, :].unsqueeze(1).to_broadcast([P, TILES, P]), ALU.add).then_inc(biased, 1)
            dve.wait_ge(product_done, 1)
            dve.tensor_tensor(g.x[:, :, :], g.x[:, :, :],
                              g.ps[:, TILES * P:2 * TILES * P].rearrange("p (t c) -> p t c", c=P), ALU.add)


def fold_weights(nc, g, name, A, B, cb, hT, scale, merged, wq, wk, wv, wo, bq, bk, bv, bo):
    nb = wq.shape[1] // P
    per = HEADS // nb
    dh = P // per
    with ExitStack() as ctx:
        s = Stage(nc, ctx, g.sems, name + "_fold")
        hn = s.sb("hn", [P, TILES, P])
        sq = s.sb("sq", [P, TILES, P])
        st = s.sb("st", [P, 3, TILES])
        raw = s.sb("raw", [P, 3, nb * P])
        wT = s.sb("wT", [P, 3, nb, P])
        wo_sb = s.sb("wo", [P, nb, P])
        masked = s.sb("masked", [P, 2, HEADS, P])
        head_rows = s.sb("head_rows", [P, per])
        bcol = s.sb("bcol", [P, 3, nb])
        bmask = s.sb("bmask", [P, 2, nb, per])
        bwide = s.sb("bwide", [P, 2, nb, P])
        ones = s.sb("ones", [P, P])
        bo_rows = s.sb("bo_rows", [P, P])
        c_all = s.sb("c_all", [P, HEADS])
        c0 = s.sb("c0", [P, HEADS])
        orow = s.sb("orow", [P, P])
        loaded, rows_made = s.sem("loaded"), s.sem("rows_made")
        var_ready, std_ready = s.sem("var_ready"), s.sem("std_ready")
        hn_ready, hn_transposed, hT_ready = s.sem("hn_ready"), s.sem("hn_transposed"), s.sem("hT_ready")
        w_transposed, w_ready = s.sem("w_transposed"), s.sem("w_ready")
        masks_ready, a_product, a_copied = s.sem("masks_ready"), s.sem("a_product"), s.sem("a_copied")
        b_product, b_copied = s.sem("b_product"), s.sem("b_copied")
        bias_product, c_ready, cb_product = s.sem("bias_product"), s.sem("c_ready"), s.sem("cb_product")
        dve_order, pool_order = s.sem("dve_order"), s.sem("pool_order")
        ps = g.ps
        LOADS = 3 + 1 + 3 * nb + 1
        SUMS = 2 * BANK
        CB = 3 * BANK
        block = ctx.enter_context(nc.Block())

        @block.sync
        def _(sp):
            for i, w in enumerate((wq, wk, wv)):
                sp.dma_start(raw[:, i, :], w).then_inc(loaded, 16)
            sp.dma_start(wo_sb[:, :, :], wo.rearrange("(j p) c -> p j c", p=P)).then_inc(loaded, 16)
            for i, b in enumerate((bq, bk, bv)):
                for j in range(nb):
                    sp.dma_start(bcol[:, i, j:j + 1], column(b[j * P:(j + 1) * P])).then_inc(loaded, 16)
            sp.dma_start(bo_rows[:, :], bo.partition_broadcast(P)).then_inc(loaded, 16)

        @block.gpsimd
        def _(pool):
            order = Order(pool, pool_order)
            order.done(pool.memset(head_rows[:, :], 1.0))
            order.done(pool.memset(ones[:, :], 1.0))
            order.done(pool.affine_select(out=head_rows[:, :], in_=head_rows[:, :], compare_op=ALU.is_ge, fill=0.0,
                                          base=0, pattern=[[-dh, per]], channel_multiplier=1))
            pool.affine_select(out=head_rows[:, :], in_=head_rows[:, :], compare_op=ALU.is_ge, fill=0.0,
                               base=dh - 1, pattern=[[dh, per]], channel_multiplier=-1).then_inc(rows_made, 1)

        @block.vector
        def _(dve):
            order = Order(dve, dve_order)
            dve.wait_ge(rows_made, 1)
            dve.wait_ge(loaded, 16 * LOADS)
            for i in range(2):
                for j in range(nb):
                    order.done(dve.tensor_scalar(bmask[:, i, j, :], head_rows[:, :], bcol[:, i, j:j + 1], None,
                                                 ALU.mult))
                    order.done(dve.tensor_scalar(bwide[:, i, j, :], ones[:, :], bcol[:, 2 * i, j:j + 1], None,
                                                 ALU.mult))
            dve.wait_ge(w_ready, 1)
            for i in range(2):
                for r in range(per):
                    order.done(dve.tensor_scalar(masked[:, i, r:HEADS:per, :], wT[:, 2 * i, :, :],
                                                 head_rows[:, r:r + 1], None, ALU.mult))
            dve.sem_inc(masks_ready, 1)
            norm_vector(dve, order, g.x[:, :, :], hn[:, :, :], sq[:, :, :], st, var_ready, std_ready, 1)
            dve.sem_inc(hn_ready, 1)
            dve.wait_ge(b_product, 1)
            if merged:
                dve.tensor_copy(B[:, :, :], ps[:, 4 * BANK:8 * BANK].rearrange("p (h c) -> p h c", c=P))\
                    .then_inc(b_copied, 1)
            else:
                dve.tensor_copy(B[:, :, 0:dh], raw[:, 2, :].rearrange("p (h e) -> p h e", e=dh)).then_inc(b_copied, 1)
            dve.wait_ge(bias_product, 1)
            order.done(dve.tensor_scalar(A[:, :, P], ps[:, SUMS:SUMS + HEADS], scale, None, ALU.mult))
            order.done(dve.tensor_scalar(c_all[:, :], ps[:, SUMS + 16:SUMS + 32], scale, None, ALU.mult))
            order.done(dve.tensor_scalar(c0[:, :], ps[:, SUMS + 32:SUMS + 48], scale, None, ALU.mult))
            if merged:
                order.done(dve.tensor_tensor(orow[:, :], ps[:, SUMS + P:SUMS + 2 * P], bo_rows[:, :], ALU.add))
            else:
                order.done(dve.tensor_copy(orow[:, :], bo_rows[:, :]))
            dve.sem_inc(c_ready, 1)
            order.done(dve.tensor_tensor(g.x[:, :, :], g.x[:, :, :],
                                         orow[:, :].unsqueeze(1).to_broadcast([P, TILES, P]), ALU.add))
            dve.wait_ge(cb_product, 1)
            dve.tensor_tensor(cb[:, :, :], ps[:, CB:CB + TILES * HEADS].rearrange("p (t h) -> p t h", h=HEADS),
                              c0[:, :].unsqueeze(1).to_broadcast([P, TILES, HEADS]), ALU.add)

        @block.scalar
        def _(act):
            act.wait_ge(w_transposed, 1)
            act.activation(wT[:, :, :, :].rearrange("p k j c -> p (k j c)"), ps[:, 0:3 * nb * P], ACT.Copy)\
                .then_inc(w_ready, 1)
            norm_scalar(act, st, var_ready, std_ready, 1)
            act.wait_ge(a_product, 1)
            act.activation(A[:, :, 0:P], ps[:, 0:4 * BANK].rearrange("p (h c) -> p h c", c=P), ACT.Copy, scale=scale)\
                .then_inc(a_copied, 1)
            act.wait_ge(hn_transposed, 1)
            act.activation(hT[:, :], ps[:, 4 * BANK:8 * BANK], ACT.Copy).then_inc(hT_ready, 1)

        @block.tensor
        def _(pe):
            pe.wait_ge(loaded, 16 * LOADS)
            for i in range(3):
                for j in range(nb):
                    c = (i * nb + j) * P
                    last = pe.transpose(ps[:, c:c + P], raw[:, i, j * P:(j + 1) * P], g.ident[:, :])
            last.then_inc(w_transposed, 1)
            pe.wait_ge(masks_ready, 1)
            for h in range(HEADS):
                last = pe.matmul(ps[:, h * P:(h + 1) * P], masked[:, 0, h, :], wT[:, 1, h // per, :],
                                 start=True, stop=True)
            last.then_inc(a_product, 1)
            for h in range(HEADS):
                c = 4 * BANK + h * P
                last = pe.matmul(ps[:, c:c + P], masked[:, 1, h, :], wo_sb[:, h // per, :], start=True, stop=True)
            last.then_inc(b_product, 1)
            pe.wait_ge(a_copied, 1)
            for j in range(nb):
                c = SUMS + j * per
                pe.matmul(ps[:, c:c + per], wT[:, 1, j, :], bmask[:, 0, j, :], start=True, stop=True)
                pe.matmul(ps[:, c + 16:c + 16 + per], wT[:, 0, j, :], bmask[:, 1, j, :], start=True, stop=True)
                pe.matmul(ps[:, c + 32:c + 32 + per], bwide[:, 0, j, :], bmask[:, 1, j, :], start=True, stop=True)
            for j in range(nb):
                last = pe.matmul(ps[:, SUMS + P:SUMS + 2 * P], bwide[:, 1, j, :], wo_sb[:, j, :], start=(j == 0),
                                 stop=(j == nb - 1))
            last.then_inc(bias_product, 1)
            pe.wait_ge(hn_ready, 1)
            pe.wait_ge(b_copied, 1)
            transpose_tokens(g, pe, hn, 4 * BANK, hn_transposed)
            pe.wait_ge(hT_ready, 1)
            pe.wait_ge(c_ready, 1)
            for t in range(TILES):
                last = pe.matmul(ps[:, CB + t * HEADS:CB + (t + 1) * HEADS], hT[:, t * P:(t + 1) * P], c_all[:, :],
                                 start=True, stop=True)
            last.then_inc(cb_product, 1)


def cross_heads(nc, g, d, name, A, B, cb, hT, dest, width):
    with ExitStack() as ctx:
        s = Stage(nc, ctx, g.sems, name + "_heads")
        kv = [s.sb(f"context{i}", [P, KT, P]) for i in range(2)]
        a_head = s.sb("a_head", [P, P + 1])
        qT = [s.sb(f"qT{i}", [P, 2 * P]) for i in range(2)]
        probs = [s.sb(f"probs{i}", [P, KEYS]) for i in range(2)]
        pT = [s.sb(f"pT{i}", [P, KT, 2 * P]) for i in range(2)]
        mixed = s.sb("mixed", [P, 2 * P])
        peak = s.sb("peak", [P, 2, 3])
        shift = s.sb("shift", [P, 2])
        total = s.sb("total", [P, 2, 2, 2])
        inverse = s.sb("inverse", [P, 2, 2])
        kv_loaded = [s.sem(f"kv_loaded{i}") for i in range(2)]
        a_copied, q_product, q_ready = s.sem("a_copied"), s.sem("q_product"), s.sem("q_ready")
        scores_ready, parts_ready, peak_ready = s.sem("scores_ready"), s.sem("parts_ready"), s.sem("peak_ready")
        shift_ready, exp_done = s.sem("shift_ready"), s.sem("exp_done")
        transposed = [s.sem(f"transposed{i}") for i in range(2)]
        pT_copied = [s.sem(f"pT_copied{i}") for i in range(2)]
        mix_product, mix_ready = s.sem("mix_product"), s.sem("mix_ready")
        out_product, out_added = s.sem("out_product"), s.sem("out_added")
        sums_ready, inverse_ready = s.sem("sums_ready"), s.sem("inverse_ready")
        ps = g.ps
        score = ps[:, 0:4 * BANK].rearrange("p (k n) -> p k n", n=BANK)
        tbank = [ps[:, (4 + i) * BANK:(5 + i) * BANK] for i in range(2)]
        mix = ps[:, 6 * BANK:6 * BANK + 2 * P]
        q_ps = ps[:, 7 * BANK:7 * BANK + 2 * P]
        out_ps = ps[:, 7 * BANK + 2 * P:8 * BANK]
        xf = dest[:, :, :].rearrange("p t c -> p (t c)")
        cbf = cb[:, :, :].rearrange("p t h -> p (t h)")
        LAST = BATCHES * HEADS - 1
        block = ctx.enter_context(nc.Block())

        def walk(eng, step):
            def batch(b, slot, first):
                step(b, 0, 0, slot, 0 if first else 2)
                step(b, 1, 1, slot, 1 if first else 2)
                with eng.Fori(1, HEADS // 2) as pair:
                    for k in range(2):
                        step(b, pair * 2 + k, k, slot, 2)

            batch(0, 0, True)
            batch(1, 1, False)
            with eng.Fori(1, BATCHES // 2) as two:
                for slot in range(2):
                    batch(two * 2 + slot, slot, False)

        @block.sync
        def _(sp):
            for b in range(BATCHES):
                wait(sp, mix_product, HEADS * (b - 1))
                load_context(sp, d, b, kv[b % 2], kv_loaded[b % 2])

        @block.gpsimd
        def _(pool):
            with pool.Fori(0, BATCHES) as b:
                with pool.Fori(0, HEADS) as h:
                    pool.wait_ge(q_ready, b * HEADS + h)
                    pool.tensor_copy(a_head[:, :], A[:, :, :].rearrange("p h c -> p (h c)")[
                        :, bass.ds(h * (P + 1), P + 1)]).then_inc(a_copied, 1)

        @block.tensor
        def _(pe):
            def project(n, b):
                pe.wait_ge(a_copied, n + 1)
                wait(pe, out_added, n - 2)
                pe.matmul(q_ps, a_head[:, 0:P], hT[:, bass.ds(b * (2 * P), 2 * P)], start=True, stop=True)\
                    .then_inc(q_product, 1)

            def scores(n, b, k, q):
                u = n * 2 + q
                pe.wait_ge(q_ready, n + 1)
                for i, (c, w) in enumerate(SPLIT):
                    if i == 0:
                        wait(pe, exp_done, u * 2 - 1)
                    if i == 1:
                        wait(pe, exp_done, u * 2)
                    ins = pe.matmul(score[:, i, 0:w], qT[k][:, q * P:(q + 1) * P], g.ctxT[:, b, c:c + w],
                                    start=True, stop=True)
                    if i in (0, 3):
                        ins.then_inc(scores_ready, 1)

            def transposes(n, q):
                u = n * 2 + q
                pe.wait_ge(exp_done, u * 2 + 2)
                for j, (t0, w) in enumerate(GROUPS):
                    wait(pe, pT_copied[j % 2], u * 2 + j // 2)
                    for t in range(t0, t0 + w):
                        rows = P if t < KT - 1 else TAIL
                        ins = pe.transpose(tbank[j % 2][0:rows, (t - t0) * P:(t - t0 + 1) * P],
                                           probs[q][:, t * P:t * P + rows], g.ident[:, :])
                    ins.then_inc(transposed[j % 2], 1)

            def mix_tiles(n, k, slot, tiles):
                u = n * 2 + 1
                if tiles[0] == 0:
                    wait(pe, mix_ready, n)
                for t in tiles:
                    if t % 4 == 0:
                        j = t // 4
                        pe.wait_ge(pT_copied[j % 2], u * 2 + j // 2 + 1)
                    rows = P if t < KT - 1 else TAIL
                    ins = pe.matmul(mix, kv[slot][0:rows, t, :], pT[k][0:rows, t, :], start=(t == 0),
                                    stop=(t == KT - 1))
                if tiles[-1] == KT - 1:
                    ins.then_inc(mix_product, 1)

            def output(n, h):
                pe.wait_ge(mix_ready, n + 1)
                wait(pe, out_added, n)
                for q in range(2):
                    ins = pe.matmul(out_ps[:, q * P:q * P + width], mixed[:, q * P:(q + 1) * P],
                                    B[:, :, :].rearrange("p h c -> p (h c)")[:, bass.ds(h * P, width)],
                                    start=True, stop=True)
                ins.then_inc(out_product, 1)

            half = KT // 2 + 1

            def step(b, h, k, slot, before):
                n = b * HEADS + h
                if isinstance(h, int) and h == 1:
                    pe.wait_ge(kv_loaded[slot], (b - slot) * 16 + 32)
                past = 1 - slot if isinstance(h, int) and h == 0 else slot
                project(n, b)
                if before >= 1:
                    transposes(n - 1, 1)
                scores(n, b, k, 0)
                if before >= 2:
                    output(n - 2, (h - 2) % HEADS if isinstance(h, int) else h - 2)
                if before >= 1:
                    mix_tiles(n - 1, 1 - k, past, range(0, half))
                transposes(n, 0)
                scores(n, b, k, 1)
                if before >= 1:
                    mix_tiles(n - 1, 1 - k, past, range(half, KT))

            walk(pe, step)
            transposes(LAST, 1)
            output(LAST - 1, HEADS - 2)
            mix_tiles(LAST, 1, 1, range(0, KT))
            output(LAST, HEADS - 1)

        def copy_groups(eng, side, copy, n, k, q):
            u = n * 2 + q
            if q == 0:
                wait(eng, mix_product, n - 1)
            for j in (side, side + 2):
                t0, w = GROUPS[j]
                rows = P if j < 3 else TAIL
                eng.wait_ge(transposed[side], u * 2 + j // 2 + 1)
                copy(pT[k][0:rows, t0:t0 + w, q * P:(q + 1) * P],
                     tbank[side][0:rows, 0:w * P].rearrange("p (t c) -> p t c", c=P)).then_inc(pT_copied[side], 1)

        @block.scalar
        def _(act):
            def copy(o, i):
                return act.activation(o, i, ACT.Copy)

            def exps(n, k, q):
                u = n * 2 + q
                act.wait_ge(shift_ready, u + 1)
                wait(act, transposed[1], u * 2 - 2)
                wait(act, inverse_ready, n - 1)
                act.activation(probs[q][:, 0:401], score[:, 0, 0:401], ACT.Exp, bias=shift[:, q:q + 1],
                               accum_out=total[:, k, q, 0:1]).then_inc(exp_done, 1)
                act.activation(probs[q][:, 401:KEYS].rearrange("p (a n) -> p a n", n=400), score[:, 1:4, 0:400],
                               ACT.Exp, bias=shift[:, q:q + 1], accum_out=total[:, k, q, 1:2]).then_inc(exp_done, 1)

            def take_mix(n):
                act.wait_ge(mix_product, n + 1)
                wait(act, out_product, n)
                act.activation(mixed[:, :], mix, ACT.Copy).then_inc(mix_ready, 1)

            def step(b, h, k, slot, before):
                n = b * HEADS + h
                act.wait_ge(q_product, n + 1)
                act.activation(qT[k][:, :], q_ps, ACT.Identity, bias=a_head[:, P:P + 1]).then_inc(q_ready, 1)
                if before >= 1:
                    copy_groups(act, 0, copy, n - 1, 1 - k, 1)
                exps(n, k, 0)
                copy_groups(act, 0, copy, n, k, 0)
                exps(n, k, 1)
                if before >= 1:
                    take_mix(n - 1)

            walk(act, step)
            copy_groups(act, 0, copy, LAST, 1, 1)
            take_mix(LAST)

        @block.vector
        def _(dve):
            def shifts(b, h, n, q):
                u = n * 2 + q
                dve.wait_ge(scores_ready, u * 2 + 1)
                dve.tensor_reduce(peak[:, q, 0:1], score[:, 0, 0:401], AX.X, ALU.max)
                dve.wait_ge(scores_ready, u * 2 + 2)
                dve.tensor_reduce(peak[:, q, 1:2], score[:, 1:4, 0:400], AX.XY, ALU.max).then_inc(parts_ready, 1)
                cb_u = cbf[:, bass.ds((b * 2 + q) * HEADS + h, 1)]
                dve.wait_ge(parts_ready, u + 1)
                dve.scalar_tensor_tensor(out=peak[:, q, 2:3], in0=peak[:, q, 0:1], scalar=peak[:, q, 1:2], in1=cb_u,
                                         op0=ALU.max, op1=ALU.add).then_inc(peak_ready, 1)
                dve.wait_ge(peak_ready, u + 1)
                dve.tensor_tensor(shift[:, q:q + 1], cb_u, peak[:, q, 2:3], ALU.subtract).then_inc(shift_ready, 1)

            def inverses(n, k):
                dve.wait_ge(exp_done, n * 4 + 4)
                dve.tensor_tensor(inverse[:, k, :], total[:, k, :, 0], total[:, k, :, 1], ALU.add).then_inc(sums_ready, 1)
                dve.wait_ge(sums_ready, n + 1)
                dve.reciprocal(inverse[:, k, :], inverse[:, k, :]).then_inc(inverse_ready, 1)

            def add_output(n, k, b, h):
                dve.wait_ge(out_product, n + 1)
                dve.wait_ge(inverse_ready, n + 1)
                for q in range(2):
                    if width == P:
                        rows = xf[:, bass.ds((b * 2 + q) * P, P)]
                        ins = dve.scalar_tensor_tensor(out=rows, in0=out_ps[:, q * P:(q + 1) * P],
                                                       scalar=inverse[:, k, q:q + 1], in1=rows, op0=ALU.mult,
                                                       op1=ALU.add)
                    else:
                        ins = dve.tensor_scalar(xf[:, bass.ds((b * 2 + q) * P + h * width, width)],
                                                out_ps[:, q * P:q * P + width], inverse[:, k, q:q + 1], None, ALU.mult)
                ins.then_inc(out_added, 1)

            def step(b, h, k, slot, before):
                n = b * HEADS + h
                if before >= 1:
                    copy_groups(dve, 1, dve.tensor_copy, n - 1, 1 - k, 1)
                shifts(b, h, n, 0)
                if before >= 1:
                    inverses(n - 1, 1 - k)
                if before >= 2:
                    if isinstance(h, int):
                        add_output(n - 2, k, b - 1, (h - 2) % HEADS)
                    else:
                        add_output(n - 2, k, b, h - 2)
                copy_groups(dve, 1, dve.tensor_copy, n, k, 0)
                shifts(b, h, n, 1)

            walk(dve, step)
            copy_groups(dve, 1, dve.tensor_copy, LAST, 1, 1)
            inverses(LAST, 1)
            add_output(LAST - 1, 0, BATCHES - 1, HEADS - 2)
            add_output(LAST, 1, BATCHES - 1, HEADS - 1)


SLOTS = 8
SPAN = 3 * P


def slot_scores(pe, g, mask, i, q_tile, k_tiles):
    c = i * BANK
    pe.matmul(g.ps[:, c:c + SPAN], g.identb[:, :], mask[:, :], start=True, stop=False, skip_group_check=True)
    pe.matmul(g.ps[:, c:c + P], q_tile(0), k_tiles(1), start=False, stop=False, skip_group_check=True)
    return pe.matmul(g.ps[:, c + P:c + SPAN], q_tile(1), k_tiles(2), start=False, stop=True, skip_group_check=True)


def slot_peaks(dve, g, half, peaks):
    banks = g.ps[:, half * 4 * BANK:(half + 1) * 4 * BANK].rearrange("p (i n) -> p i n", n=BANK)
    s = slice(4 * half, 4 * half + 4)
    dve.tensor_reduce(peaks[:, 0, s], banks[:, :, 0:P], AX.X, ALU.max, negate=True)
    return dve.tensor_reduce(peaks[:, 1, s], banks[:, :, P:SPAN], AX.X, ALU.max, negate=True)


def slot_exps(act, g, i, probs, peaks, sums, scale):
    c = i * BANK
    act.activation(probs[:, i, 0:P], g.ps[:, c:c + P], ACT.Exp, bias=peaks[:, 0, i:i + 1], scale=scale(0),
                   accum_out=sums[:, 0, i:i + 1])
    return act.activation(probs[:, i, P:SPAN], g.ps[:, c + P:c + SPAN], ACT.Exp, bias=peaks[:, 1, i:i + 1],
                          scale=scale(1), accum_out=sums[:, 1, i:i + 1])


def slot_normalize(dve, half, probs, inverse):
    s = slice(4 * half, 4 * half + 4)
    dve.tensor_tensor(probs[:, s, 0:P], probs[:, s, 0:P], inverse[:, 0, s].unsqueeze(2).to_broadcast([P, 4, P]),
                      ALU.mult)
    return dve.tensor_tensor(probs[:, s, P:SPAN], probs[:, s, P:SPAN],
                             inverse[:, 1, s].unsqueeze(2).to_broadcast([P, 4, 2 * P]), ALU.mult)


def slot_transposes(pe, g, i, probs):
    c = (6 + i % 2) * BANK
    for j in range(3):
        ins = pe.transpose(g.ps[:, c + j * P:c + (j + 1) * P], probs[:, i, j * P:(j + 1) * P], g.ident[:, :])
    return ins


def slot_mix(pe, out, value, i, probsT, **tile):
    pe.matmul(out, value(0), probsT[:, i, 0:2 * P], start=True, stop=False, skip_group_check=True, **tile)
    return pe.matmul(out[:, P:2 * P], value(1), probsT[:, i, 2 * P:SPAN], start=False, stop=True,
                     skip_group_check=True, **tile)


LHEADS = 8
LDIM = 64
INNER = LHEADS * LDIM
SEQ = 2 * P
TOKENS = BATCHES * SEQ


def local_stage(nc, g, d):
    with ExitStack() as ctx:
        s = Stage(nc, ctx, g.sems, "local")
        yT = s.sb("yT", [P, TOKENS])
        norm_to_channels(nc, g, "local_norm", yT)
        for layer in range(2):
            local_attention(nc, g, d, yT, layer)
            local_mlp(nc, g, d, yT, layer)
        channels_to_x(nc, g, "local_end", yT)


def norm_to_channels(nc, g, name, dst):
    with ExitStack() as ctx:
        s = Stage(nc, ctx, g.sems, name)
        hn = s.sb("hn", [P, TILES, P])
        sq = s.sb("sq", [P, TILES, P])
        st = s.sb("st", [P, 3, TILES])
        var_ready, std_ready = s.sem("var_ready"), s.sem("std_ready")
        hn_ready, transposed, order_sem = s.sem("hn_ready"), s.sem("transposed"), s.sem("dve_order")
        block = ctx.enter_context(nc.Block())

        @block.vector
        def _(dve):
            order = Order(dve, order_sem)
            norm_vector(dve, order, g.x[:, :, :], hn[:, :, :], sq[:, :, :], st, var_ready, std_ready, 1)
            dve.sem_inc(hn_ready, 1)

        @block.scalar
        def _(act):
            norm_scalar(act, st, var_ready, std_ready, 1)
            act.wait_ge(transposed, 1)
            act.activation(dst[:, :], g.ps[:, 0:TOKENS], ACT.Copy)

        @block.tensor
        def _(pe):
            pe.wait_ge(hn_ready, 1)
            transpose_tokens(g, pe, hn, 0, transposed)


def channels_to_x(nc, g, name, src):
    with ExitStack() as ctx:
        s = Stage(nc, ctx, g.sems, name)
        transposed = s.sem("transposed")
        block = ctx.enter_context(nc.Block())

        @block.tensor
        def _(pe):
            for t in range(TILES):
                last = pe.transpose(g.ps[:, t * P:(t + 1) * P], src[:, t * P:(t + 1) * P], g.ident[:, :])
            last.then_inc(transposed, 1)

        @block.vector
        def _(dve):
            dve.wait_ge(transposed, 1)
            dve.tensor_tensor(g.x[:, :, :], g.x[:, :, :], g.ps[:, 0:TOKENS].rearrange("p (t c) -> p t c", c=P), ALU.add)


def local_attention(nc, g, d, yT, layer):
    with ExitStack() as ctx:
        s = Stage(nc, ctx, g.sems, f"local{layer}")
        wqkv = s.sb("wqkv", [P, 3 * INNER])
        wo = s.sb("wo", [P, INNER // P, P])
        rotary = s.sb("rotary", [P, 4, 2, LDIM])
        turned = s.sb("turned", [P, 4, 2, LDIM])
        scales = s.sb("scales", [P, 2, LDIM])
        shifted = s.sb("shifted", [P, SEQ])
        qk = s.sb("qk", [P, 4, LHEADS, LDIM])
        value = s.sb("value", [P, 2, INNER])
        squares = s.sb("squares", [P, 4, LHEADS, LDIM])
        norm = s.sb("norm", [P, 4, LHEADS])
        rnorm = s.sb("rnorm", [P, 4, LHEADS])
        q_gain = s.sb("q_gain", [P, 2, LHEADS])
        part = s.sb("part", [P, 4, LHEADS, LDIM])
        turn = s.sb("turn", [P, 4, LHEADS, LDIM])
        qT = s.sb("qT", [P, 4, SEQ])
        kT = s.sb("kT", [P, 4, SEQ])
        peaks = s.sb("peaks", [P, 2, SLOTS])
        shifts = s.sb("shifts", [P, 2, SLOTS])
        sums = s.sb("sums", [P, 2, SLOTS])
        inverse = s.sb("inverse", [P, 2, SLOTS])
        probs = s.sb("probs", [P, SLOTS, SPAN])
        probsT = s.sb("probsT", [P, SLOTS, SPAN])
        oT = s.sb("oT", [P, 4, SEQ])
        names = ("loaded edge_zeroed turned_ready shifted_ready qk_product v_product qk_ready squares_ready "
                 "squared_sums norm_ready gain_ready q_turned k_turned q_transposed k_transposed qT_ready kT_ready "
                 "v_ready scores_ready peaks_ready shifts_ready exp_done normalized mixed o_ready out_product "
                 "out_added dve_order k_part pool_order rnorm_ready q_part inverse_ready").split()
        m = {n: s.sem(n) for n in names}
        transposed = [s.sem(f"transposed{i}") for i in range(2)]
        probsT_copied = [s.sem(f"probsT_copied{i}") for i in range(2)]
        ps = g.ps
        block = ctx.enter_context(nc.Block())
        LOADS = 3 + 4

        @block.sync
        def _(sp):
            sp.dma_start(wqkv[:, :], d["L0_ffn_wqkv"][layer]).then_inc(m["loaded"], 16)
            sp.dma_start(wo[:, :, :], d["L0_ffn_wo"][layer].rearrange("(j p) c -> p j c", p=P)).then_inc(m["loaded"], 16)
            for i in range(4):
                sp.dma_start(rotary[:, i, :, :], d["rotary"][i].rearrange("(t p) e -> p t e", p=P)).then_inc(m["loaded"], 16)
            sp.dma_start(scales[:, 0, :], d["L0_ffn_q_scale"][layer].partition_broadcast(P)).then_inc(m["loaded"], 16)
            sp.dma_start(scales[:, 1, :], d["L0_ffn_k_scale"][layer].partition_broadcast(P)).then_inc(m["loaded"], 16)

        def walk(eng, front, attend):
            front(0)
            with eng.Fori(0, BATCHES - 1) as b:
                attend(b, True)
            attend(BATCHES - 1, False)

        @block.gpsimd
        def _(pool):
            order = Order(pool, m["pool_order"])
            order.done(pool.memset(shifted[64:P, 0:1], 0.0))
            pool.sem_inc(m["edge_zeroed"], 1)
            pool.wait_ge(m["loaded"], 16 * (LOADS + 1))
            half = LDIM // 2
            for i in range(2):
                full = scales[:, i, :].unsqueeze(1).to_broadcast([P, 2, LDIM])
                order.done(pool.tensor_tensor(turned[:, 2 * i], rotary[:, 2 * i], full, ALU.mult))
                for a, b in ((0, half), (half, 0)):
                    order.done(pool.tensor_tensor(turned[:, 2 * i + 1, :, a:a + half],
                                                  rotary[:, 2 * i + 1, :, a:a + half],
                                                  scales[:, i, b:b + half].unsqueeze(1).to_broadcast([P, 2, half]),
                                                  ALU.mult))
            pool.sem_inc(m["turned_ready"], 1)

            def front(b):
                pool.wait_ge(m["qk_ready"], b + 1)
                wait(pool, m["k_transposed"], b)
                k, t = qk[:, 2:4], turned[:, 2].unsqueeze(2)
                pool.tensor_tensor(turn[:, 2:4], k, t.to_broadcast([P, 2, LHEADS, LDIM]), ALU.mult)
                for a, c in ((0, half), (half, 0)):
                    ins = pool.tensor_tensor(part[:, 2:4, :, a:a + half], k[:, :, :, c:c + half],
                                             turned[:, 3, :, a:a + half].unsqueeze(2)
                                             .to_broadcast([P, 2, LHEADS, half]), ALU.mult)
                ins.then_inc(m["k_part"], 1)
                pool.wait_ge(m["k_part"], b * 2 + 1)
                pool.tensor_tensor(turn[:, 2:4], turn[:, 2:4], part[:, 2:4], ALU.add).then_inc(m["k_part"], 1)
                pool.wait_ge(m["k_part"], b * 2 + 2)
                pool.wait_ge(m["rnorm_ready"], b + 1)
                pool.tensor_tensor(turn[:, 2:4], turn[:, 2:4],
                                   rnorm[:, 2:4, :].unsqueeze(3).to_broadcast([P, 2, LHEADS, LDIM]), ALU.mult)\
                    .then_inc(m["k_turned"], 1)

            front(0)
            with pool.Fori(1, BATCHES) as b:
                front(b)

        @block.vector
        def _(dve):
            half = LDIM // 2
            dve.wait_ge(m["turned_ready"], 1)

            def front_norm(b):
                dve.wait_ge(m["squares_ready"], b + 1)
                dve.tensor_reduce(norm[:, :, :], squares[:, :, :, :], AX.X, ALU.add).then_inc(m["squared_sums"], 1)

            def front_turn(b):
                dve.wait_ge(m["qk_ready"], b + 1)
                wait(dve, m["q_transposed"], b)
                q = qk[:, 0:2]
                dve.tensor_tensor(turn[:, 0:2], q, turned[:, 0].unsqueeze(2).to_broadcast([P, 2, LHEADS, LDIM]),
                                  ALU.mult)
                for a, c in ((0, half), (half, 0)):
                    ins = dve.tensor_tensor(part[:, 0:2, :, a:a + half], q[:, :, :, c:c + half],
                                            turned[:, 1, :, a:a + half].unsqueeze(2)
                                            .to_broadcast([P, 2, LHEADS, half]), ALU.mult)
                ins.then_inc(m["q_part"], 1)
                dve.wait_ge(m["q_part"], b + 1)
                dve.tensor_tensor(turn[:, 0:2], turn[:, 0:2], part[:, 0:2], ALU.add).then_inc(m["q_turned"], 1)
                dve.wait_ge(m["norm_ready"], b + 1)
                dve.tensor_scalar(norm[:, :, :], norm[:, :, :], 1e-12, None, ALU.max).then_inc(m["dve_order"], 1)
                dve.wait_ge(m["dve_order"], b * 2 + 1)
                dve.reciprocal(rnorm[:, :, :], norm[:, :, :]).then_inc(m["rnorm_ready"], 1)
                dve.wait_ge(m["rnorm_ready"], b + 1)
                dve.tensor_scalar(q_gain[:, :, :], rnorm[:, 0:2, :], 8.0, None, ALU.mult).then_inc(m["dve_order"], 1)
                dve.wait_ge(m["dve_order"], b * 2 + 2)

            def front_keys(b):
                dve.wait_ge(m["k_transposed"], b + 1)
                dve.tensor_copy(kT[:, :, :], ps[:, 2 * BANK:4 * BANK].rearrange("p (j n) -> p j n", n=SEQ))\
                    .then_inc(m["kT_ready"], 1)

            def attend(b, more):
                for half_ in range(2):
                    dve.wait_ge(m["scores_ready"], b * 2 + half_ + 1)
                    slot_peaks(dve, g, half_, peaks).then_inc(m["peaks_ready"], 1)
                dve.wait_ge(m["peaks_ready"], b * 2 + 2)
                dve.tensor_tensor(shifts[:, :, :], peaks[:, :, :], q_gain[:, :, :], ALU.mult)\
                    .then_inc(m["shifts_ready"], 1)
                for half_ in range(2):
                    dve.wait_ge(m["exp_done"], b * 2 + half_ + 1)
                    h = slice(4 * half_, 4 * half_ + 4)
                    dve.reciprocal(inverse[:, :, h], sums[:, :, h]).then_inc(m["inverse_ready"], 1)
                    dve.wait_ge(m["inverse_ready"], b * 2 + half_ + 1)
                    slot_normalize(dve, half_, probs, inverse).then_inc(m["normalized"], 1)
                if more:
                    front_norm(b + 1)
                for i in range(1, SLOTS, 2):
                    dve.wait_ge(transposed[1], b * 4 + i // 2 + 1)
                    dve.tensor_copy(probsT[:, i, :], ps[:, 7 * BANK:7 * BANK + SPAN]).then_inc(probsT_copied[1], 1)
                if more:
                    front_turn(b + 1)
                dve.wait_ge(m["out_product"], b + 1)
                cols = yT[:, bass.ds(b * SEQ, SEQ)]
                dve.tensor_tensor(cols, cols, ps[:, 2 * BANK:2 * BANK + SEQ], ALU.add).then_inc(m["out_added"], 1)
                if more:
                    front_keys(b + 1)

            def front(b):
                front_norm(b)
                front_turn(b)
                front_keys(b)

            walk(dve, front, attend)

        @block.scalar
        def _(act):
            def front_shift(b):
                wait(act, m["v_product"], b)
                act.activation(shifted[0:64, :], yT[0:64, bass.ds(b * SEQ, SEQ)], ACT.Copy)
                act.activation(shifted[64:P, 1:SEQ], yT[64:P, bass.ds(b * SEQ, SEQ - 1)], ACT.Copy)\
                    .then_inc(m["shifted_ready"], 1)

            def front_take(b):
                act.wait_ge(m["qk_product"], b + 1)
                wait(act, m["k_turned"], b)
                wait(act, m["q_turned"], b)
                act.activation(qk[:, :, :, :].rearrange("p i h e -> p (i h e)"), ps[:, 0:4 * BANK], ACT.Copy)\
                    .then_inc(m["qk_ready"], 1)
                act.wait_ge(m["qk_ready"], b + 1)
                act.activation(squares[:, :, :, :], qk[:, :, :, :], ACT.Square).then_inc(m["squares_ready"], 1)

            def front_sqrt(b):
                act.wait_ge(m["squared_sums"], b + 1)
                act.activation(norm[:, :, :], norm[:, :, :], ACT.Sqrt).then_inc(m["norm_ready"], 1)

            def front_value(b):
                act.wait_ge(m["v_product"], b + 1)
                wait(act, m["mixed"], b)
                act.activation(value[:, :, :].rearrange("p t n -> p (t n)"), ps[:, 4 * BANK:6 * BANK], ACT.Copy)\
                    .then_inc(m["v_ready"], 1)

            def front_queries(b):
                act.wait_ge(m["q_transposed"], b + 1)
                act.activation(qT[:, :, :].rearrange("p j n -> p (j n)"), ps[:, 0:2 * BANK], ACT.Copy)\
                    .then_inc(m["qT_ready"], 1)

            def attend(b, more):
                if more:
                    front_shift(b + 1)
                act.wait_ge(m["shifts_ready"], b + 1)
                for i in range(SLOTS):
                    ins = slot_exps(act, g, i, probs, shifts, sums, lambda t: q_gain[:, t, i:i + 1])
                    if i % 4 == 3:
                        ins.then_inc(m["exp_done"], 1)
                if more:
                    front_take(b + 1)
                for i in range(0, SLOTS, 2):
                    act.wait_ge(transposed[0], b * 4 + i // 2 + 1)
                    act.activation(probsT[:, i, :], ps[:, 6 * BANK:6 * BANK + SPAN], ACT.Copy)\
                        .then_inc(probsT_copied[0], 1)
                if more:
                    front_sqrt(b + 1)
                act.wait_ge(m["mixed"], b + 1)
                act.activation(oT[:, :, :].rearrange("p j n -> p (j n)"), ps[:, 0:2 * BANK], ACT.Copy)\
                    .then_inc(m["o_ready"], 1)
                if more:
                    front_value(b + 1)
                    front_queries(b + 1)

            def front(b):
                front_shift(b)
                front_take(b)
                front_sqrt(b)
                front_value(b)
                front_queries(b)

            walk(act, front, attend)

        @block.tensor
        def _(pe):
            pe.wait_ge(m["loaded"], 16 * (LOADS + 1))
            pe.wait_ge(m["edge_zeroed"], 1)

            def front_project(b):
                pe.wait_ge(m["shifted_ready"], b + 1)
                wait(pe, m["exp_done"], b * 2)
                for i in range(6):
                    j, t = i // 2, i % 2
                    ins = pe.matmul(ps[:, i * BANK:(i + 1) * BANK], shifted[:, t * P:(t + 1) * P],
                                    wqkv[:, j * INNER:(j + 1) * INNER], start=True, stop=True)
                    if i == 3:
                        ins.then_inc(m["qk_product"], 1)
                ins.then_inc(m["v_product"], 1)

            def front_transposes(b):
                wait(pe, m["o_ready"], b)
                wait(pe, m["out_added"], b)
                for i, name in ((0, "q"), (1, "k")):
                    pe.wait_ge(m[name + "_turned"], b + 1)
                    if i == 0:
                        pe.wait_ge(m["qk_ready"], b + 1)
                    for j in range(4):
                        for t in range(2):
                            c = 2 * i * BANK + j * SEQ + t * P
                            ins = pe.transpose(ps[:, c:c + P],
                                               turn[:, 2 * i + t, 2 * j:2 * j + 2, :].rearrange("p h e -> p (h e)"),
                                               g.ident[:, :])
                    ins.then_inc(m[name + "_transposed"], 1)

            def attend(b, more):
                pe.wait_ge(m["qT_ready"], b + 1)
                pe.wait_ge(m["kT_ready"], b + 1)
                pe.wait_ge(m["v_ready"], b + 1)
                wait(pe, probsT_copied[0], b * 4)
                wait(pe, probsT_copied[1], b * 4)
                for i in range(SLOTS):
                    j, rows = i // 2, slice(64 * (i % 2), 64 * (i % 2) + 64)
                    ins = slot_scores(pe, g, g.band, i, lambda t: qT[rows, j, t * P:(t + 1) * P],
                                      lambda n: kT[rows, j, 0:n * P])
                    if i % 4 == 3:
                        ins.then_inc(m["scores_ready"], 1)
                if more:
                    front_project(b + 1)
                else:
                    pe.wait_ge(m["exp_done"], b * 2 + 2)
                for i in range(SLOTS):
                    if i % 4 == 0:
                        pe.wait_ge(m["normalized"], b * 2 + i // 4 + 1)
                    if i >= 2:
                        pe.wait_ge(probsT_copied[i % 2], b * 4 + i // 2)
                    slot_transposes(pe, g, i, probs).then_inc(transposed[i % 2], 1)
                if more:
                    pe.wait_ge(m["qk_ready"], b + 2)
                for i in range(SLOTS):
                    if i % 2 == 0:
                        for side in range(2):
                            pe.wait_ge(probsT_copied[side], b * 4 + i // 2 + 1)
                    j, r = i // 2, i % 2
                    ins = slot_mix(pe, ps[64 * r:64 * r + 64, j * SEQ:(j + 1) * SEQ],
                                   lambda kt: value[:, kt, i * LDIM:(i + 1) * LDIM], i, probsT)
                ins.then_inc(m["mixed"], 1)
                pe.wait_ge(m["o_ready"], b + 1)
                for j in range(4):
                    ins = pe.matmul(ps[:, 2 * BANK:2 * BANK + SEQ], wo[:, j, :], oT[:, j, :], start=(j == 0),
                                    stop=(j == 3))
                ins.then_inc(m["out_product"], 1)
                if more:
                    front_transposes(b + 1)

            def front(b):
                front_project(b)
                front_transposes(b)

            walk(pe, front, attend)


def local_mlp(nc, g, d, yT, layer):
    hid = d["L0_ffn_w2"].shape[1]
    chunks = [(c, min(P, hid - c)) for c in range(0, hid, P)]
    with ExitStack() as ctx:
        s = Stage(nc, ctx, g.sems, f"mlp{layer}")
        w1 = s.sb("w1", [P, 2 * hid])
        w2 = s.sb("w2", [P, len(chunks), P])
        b1 = s.sb("b1", [P, 2, len(chunks)])
        cols = s.sb("cols", [P, 3])
        gain, offset, b2 = (cols[:, i:i + 1] for i in range(3))
        mean_of = s.sb("mean_of", [P, P])
        h = s.sb("h", [P, TOKENS])
        sq = s.sb("sq", [P, TOKENS])
        gate = s.sb("gate", [P, 2, TOKENS])
        hidden = s.sb("hidden", [P, len(chunks), TOKENS])
        names = ("loaded constants shifted_ready mean_product centred squared var_product var_ready std_ready h_ready "
                 "gate_product gate_ready a_product hidden_ready out_product dve_order pool_order scaled").split()
        m = {n: s.sem(n) for n in names}
        ps = g.ps
        lo, hi = ps[:, 0:TOKENS], ps[:, TOKENS:2 * TOKENS]
        loads = 1 + len(chunks) * 3 + 3
        block = ctx.enter_context(nc.Block())

        @block.sync
        def _(sp):
            sp.dma_start(w1[:, :], d["L0_ffn_w1"][layer]).then_inc(m["loaded"], 16)
            for j, (c, n) in enumerate(chunks):
                sp.dma_start(w2[0:n, j, :], d["L0_ffn_w2"][layer][c:c + n, :]).then_inc(m["loaded"], 16)
                for k in range(2):
                    sp.dma_start(b1[0:n, k, j:j + 1], column(d["L0_ffn_b1"][layer][k * hid + c:k * hid + c + n]))\
                        .then_inc(m["loaded"], 16)
            for c, name in ((gain, "ln_g"), (offset, "ln_b"), (b2, "b2")):
                sp.dma_start(c, column(d["L0_ffn_" + name][layer])).then_inc(m["loaded"], 16)

        @block.gpsimd
        def _(pool):
            order = Order(pool, m["pool_order"])
            order.done(pool.memset(mean_of[:, :], 1.0 / P))
            pool.sem_inc(m["constants"], 1)
            h3, y3 = (a.rearrange("p (b l) -> p b l", l=SEQ) for a in (h[:, :], yT[:, :]))
            order.done(pool.memset(h3[64:P, :, 0:1], 0.0))
            pool.tensor_copy(h3[64:P, :, 1:SEQ], y3[64:P, :, 0:SEQ - 1]).then_inc(m["shifted_ready"], 1)

        @block.vector
        def _(dve):
            order = Order(dve, m["dve_order"])
            dve.tensor_copy(h[0:64, :], yT[0:64, :]).then_inc(m["shifted_ready"], 1)
            dve.wait_ge(m["mean_product"], 1)
            dve.tensor_tensor(h[:, :], h[:, :], lo, ALU.subtract).then_inc(m["centred"], 1)
            dve.wait_ge(m["var_product"], 1)
            dve.tensor_scalar(sq[:, :], hi, EPS, None, ALU.add).then_inc(m["var_ready"], 1)
            dve.wait_ge(m["std_ready"], 1)
            order.done(dve.reciprocal(sq[:, :], sq[:, :]))
            dve.tensor_tensor(h[:, :], h[:, :], sq[:, :], ALU.mult).then_inc(m["scaled"], 1)
            for j, (c, n) in enumerate(chunks):
                dve.wait_ge(m["gate_ready"], j + 1)
                dve.wait_ge(m["a_product"], j + 1)
                dve.scalar_tensor_tensor(out=hidden[0:n, j, :], in0=hi[0:n, :], scalar=b1[0:n, 0, j:j + 1],
                                         in1=gate[0:n, j % 2, :], op0=ALU.add, op1=ALU.mult)\
                    .then_inc(m["hidden_ready"], 1)
            dve.wait_ge(m["out_product"], 1)
            dve.scalar_tensor_tensor(out=yT[:, :], in0=lo, scalar=b2, in1=yT[:, :], op0=ALU.add, op1=ALU.add)

        @block.scalar
        def _(act):
            act.wait_ge(m["centred"], 1)
            act.activation(sq[:, :], h[:, :], ACT.Square).then_inc(m["squared"], 1)
            act.wait_ge(m["var_ready"], 1)
            act.activation(sq[:, :], sq[:, :], ACT.Sqrt).then_inc(m["std_ready"], 1)
            act.wait_ge(m["scaled"], 1)
            act.wait_ge(m["loaded"], 16 * loads)
            act.activation(h[:, :], h[:, :], ACT.Identity, bias=offset, scale=gain).then_inc(m["h_ready"], 1)
            for j, (c, n) in enumerate(chunks):
                act.wait_ge(m["gate_product"], j + 1)
                wait(act, m["hidden_ready"], j - 1)
                act.activation(gate[0:n, j % 2, :], lo[0:n, :], ACT.Gelu, bias=b1[0:n, 1, j:j + 1])\
                    .then_inc(m["gate_ready"], 1)

        @block.tensor
        def _(pe):
            def product(base, lhsT, rhs, rows=P, start=True, stop=True, n=None):
                for k in range(TOKENS // BANK):
                    last = pe.matmul(ps[0:rows, base + k * BANK:base + (k + 1) * BANK], lhsT,
                                     rhs[:, k * BANK:(k + 1) * BANK], start=start, stop=stop)
                return last

            pe.wait_ge(m["constants"], 1)
            pe.wait_ge(m["shifted_ready"], 2)
            product(0, mean_of[:, :], h).then_inc(m["mean_product"], 1)
            pe.wait_ge(m["squared"], 1)
            product(TOKENS, mean_of[:, :], sq).then_inc(m["var_product"], 1)
            pe.wait_ge(m["loaded"], 16 * loads)
            pe.wait_ge(m["h_ready"], 1)
            for j, (c, n) in enumerate(chunks):
                wait(pe, m["gate_ready"], j)
                product(0, w1[:, hid + c:hid + c + n], h, n).then_inc(m["gate_product"], 1)
                wait(pe, m["hidden_ready"], j)
                product(TOKENS, w1[:, c:c + n], h, n).then_inc(m["a_product"], 1)
            pe.wait_ge(m["gate_ready"], len(chunks))
            for k in range(TOKENS // BANK):
                for j, (c, n) in enumerate(chunks):
                    if k == 0:
                        pe.wait_ge(m["hidden_ready"], j + 1)
                    last = pe.matmul(ps[:, k * BANK:(k + 1) * BANK], w2[0:n, j, :],
                                     hidden[0:n, j, k * BANK:(k + 1) * BANK], start=(j == 0),
                                     stop=(j == len(chunks) - 1))
            last.then_inc(m["out_product"], 1)


def causal_stage(nc, g, d):
    with ExitStack() as outer:
        so = Stage(nc, outer, g.sems, "causal")
        hT = so.sb("hT", [P, TOKENS])
        norm_to_channels(nc, g, "causal_norm", hT)
        causal_attention(nc, g, d, hT)


def causal_attention(nc, g, d, hT):
    with ExitStack() as ctx:
        s = Stage(nc, ctx, g.sems, "causal_attn")
        raw = s.sb("raw", [P, 3, P])
        wT = s.sb("wT", [P, 3, P])
        bcol = s.sb("bcol", [P, 3])
        qT = s.sb("qT", [P, TOKENS])
        kT = s.sb("kT", [P, TOKENS])
        value = s.sb("value", [P, TILES, P])
        peaks = s.sb("peaks", [P, 2, SLOTS])
        sums = s.sb("sums", [P, 2, SLOTS])
        inverse = s.sb("inverse", [P, 2, SLOTS])
        probs = s.sb("probs", [P, SLOTS, SPAN])
        probsT = s.sb("probsT", [P, SLOTS, SPAN])
        oT = s.sb("oT", [P, TOKENS])
        names = ("loaded w_transposed w_ready q_product k_product v_product q_ready k_ready v_ready scores_ready "
                 "peaks_ready exp_done normalized mixed o_ready o_transposed inverse_ready").split()
        m = {n: s.sem(n) for n in names}
        transposed = [s.sem(f"transposed{i}") for i in range(2)]
        probsT_copied = [s.sem(f"probsT_copied{i}") for i in range(2)]
        ps = g.ps
        lo, hi = ps[:, 0:TOKENS], ps[:, TOKENS:2 * TOKENS]
        block = ctx.enter_context(nc.Block())

        @block.sync
        def _(sp):
            for i, n in enumerate("qkv"):
                sp.dma_start(raw[:, i, :], d["L1_attn_W" + n]).then_inc(m["loaded"], 16)
                sp.dma_start(bcol[:, i:i + 1], column(d["L1_attn_b" + n])).then_inc(m["loaded"], 16)

        @block.tensor
        def _(pe):
            pe.wait_ge(m["loaded"], 96)
            for i in range(3):
                last = pe.transpose(ps[:, i * P:(i + 1) * P], raw[:, i, :], g.ident[:, :])
            last.then_inc(m["w_transposed"], 1)
            pe.wait_ge(m["w_ready"], 1)
            for base, i, done in ((0, 0, "q_product"), (TOKENS, 1, "k_product")):
                for k in range(TOKENS // BANK):
                    last = pe.matmul(ps[:, base + k * BANK:base + (k + 1) * BANK], wT[:, i, :],
                                     hT[:, k * BANK:(k + 1) * BANK], start=True, stop=True)
                last.then_inc(m[done], 1)
            pe.wait_ge(m["q_ready"], 1)
            for t in range(TILES):
                last = pe.matmul(ps[:, t * P:(t + 1) * P], hT[:, t * P:(t + 1) * P], wT[:, 2, :], start=True, stop=True)
            last.then_inc(m["v_product"], 1)
            pe.wait_ge(m["k_ready"], 1)
            pe.wait_ge(m["v_ready"], 1)
            for b in range(BATCHES):
                c = b * SEQ
                ins = slot_scores(pe, g, g.causal, b, lambda t: qT[:, c + t * P:c + (t + 1) * P],
                                  lambda n: kT[:, c:c + n * P])
                if b % 4 == 3:
                    ins.then_inc(m["scores_ready"], 1)
            pe.wait_ge(m["exp_done"], 2)
            for b in range(BATCHES):
                if b % 4 == 0:
                    pe.wait_ge(m["normalized"], b // 4 + 1)
                if b >= 2:
                    pe.wait_ge(probsT_copied[b % 2], b // 2)
                slot_transposes(pe, g, b, probs).then_inc(transposed[b % 2], 1)
            for b in range(BATCHES):
                pe.wait_ge(probsT_copied[b % 2], b // 2 + 1)
                last = slot_mix(pe, ps[:, b * SEQ:(b + 1) * SEQ], lambda kt: value[:, 2 * b + kt, :], b, probsT)
            last.then_inc(m["mixed"], 1)
            pe.wait_ge(m["o_ready"], 1)
            for t in range(TILES):
                last = pe.transpose(ps[:, TOKENS + t * P:TOKENS + (t + 1) * P], oT[:, t * P:(t + 1) * P], g.ident[:, :])
            last.then_inc(m["o_transposed"], 1)

        @block.scalar
        def _(act):
            act.wait_ge(m["w_transposed"], 1)
            act.activation(wT[:, :, :].rearrange("p i c -> p (i c)"), ps[:, 0:3 * P], ACT.Copy).then_inc(m["w_ready"], 1)
            act.wait_ge(m["loaded"], 96)
            act.wait_ge(m["k_product"], 1)
            act.activation(kT[:, :], hi, ACT.Identity, bias=bcol[:, 1:2]).then_inc(m["k_ready"], 1)
            act.wait_ge(m["v_product"], 1)
            act.activation(value[:, :, :].rearrange("p t c -> p (t c)"), lo, ACT.Copy).then_inc(m["v_ready"], 1)
            for b in range(BATCHES):
                if b % 4 == 0:
                    act.wait_ge(m["peaks_ready"], b // 4 + 1)
                ins = slot_exps(act, g, b, probs, peaks, sums, lambda t: 1.0)
                if b % 4 == 3:
                    ins.then_inc(m["exp_done"], 1)
            for b in range(0, BATCHES, 2):
                act.wait_ge(transposed[0], b // 2 + 1)
                act.activation(probsT[:, b, :], ps[:, 6 * BANK:6 * BANK + SPAN], ACT.Copy).then_inc(probsT_copied[0], 1)
            act.wait_ge(m["mixed"], 1)
            act.activation(oT[:, :], lo, ACT.Identity, bias=bcol[:, 2:3]).then_inc(m["o_ready"], 1)

        @block.vector
        def _(dve):
            dve.wait_ge(m["loaded"], 96)
            dve.wait_ge(m["q_product"], 1)
            dve.tensor_scalar(qT[:, :], lo, bcol[:, 0:1], float(P) ** -0.5, ALU.add, ALU.mult).then_inc(m["q_ready"], 1)
            for half in range(2):
                dve.wait_ge(m["scores_ready"], half + 1)
                slot_peaks(dve, g, half, peaks).then_inc(m["peaks_ready"], 1)
            for half in range(2):
                dve.wait_ge(m["exp_done"], half + 1)
                h = slice(4 * half, 4 * half + 4)
                dve.reciprocal(inverse[:, :, h], sums[:, :, h]).then_inc(m["inverse_ready"], 1)
                dve.wait_ge(m["inverse_ready"], half + 1)
                slot_normalize(dve, half, probs, inverse).then_inc(m["normalized"], 1)
            for b in range(1, BATCHES, 2):
                dve.wait_ge(transposed[1], b // 2 + 1)
                dve.tensor_copy(probsT[:, b, :], ps[:, 7 * BANK:7 * BANK + SPAN]).then_inc(probsT_copied[1], 1)
            dve.wait_ge(m["o_transposed"], 1)
            dve.tensor_tensor(g.x[:, :, :], g.x[:, :, :], hi.rearrange("p (t c) -> p t c", c=P), ALU.add)


LIMIT = 100.0


def binary_stage(nc, g, d):
    with ExitStack() as outer:
        so = Stage(nc, outer, g.sems, "binary")
        hT = so.sb("hT", [P, TOKENS])
        norm_to_channels(nc, g, "binary_norm", hT)
        binary_product(nc, g, d, hT)


def binary_product(nc, g, d, hT):
    with ExitStack() as ctx:
        s = Stage(nc, ctx, g.sems, "binary_product")
        w = s.sb("w", [P, P])
        wT = s.sb("wT", [P, P])
        scale = s.sb("scale", [P, P])
        bias = s.sb("bias", [P, P])
        y = s.sb("y", [P, TILES, P])
        loaded, signs, w_transposed, w_ready = s.sem("loaded"), s.sem("signs"), s.sem("w_transposed"), s.sem("w_ready")
        product_done, dve_order = s.sem("product_done"), s.sem("dve_order")
        block = ctx.enter_context(nc.Block())
        wide = [P, TILES, P]

        @block.sync
        def _(sp):
            sp.dma_start(w[:, :], d["L1_ffn_weights"]).then_inc(loaded, 16)
            sp.dma_start(scale[:, :], d["L1_ffn_scale"].partition_broadcast(P)).then_inc(loaded, 16)
            sp.dma_start(bias[:, :], d["L1_ffn_bias"].partition_broadcast(P)).then_inc(loaded, 16)

        @block.vector
        def _(dve):
            order = Order(dve, dve_order)
            dve.wait_ge(loaded, 48)
            order.done(dve.tensor_scalar(w[:, :], w[:, :], 0.0, 2.0, ALU.is_ge, ALU.mult))
            dve.tensor_scalar(w[:, :], w[:, :], 1.0, None, ALU.subtract).then_inc(signs, 1)
            dve.wait_ge(product_done, 1)
            order.done(dve.tensor_tensor(y[:, :, :], g.ps[:, 0:TOKENS].rearrange("p (t c) -> p t c", c=P),
                                         scale[:, :].unsqueeze(1).to_broadcast(wide), ALU.mult))
            order.done(dve.tensor_tensor(y[:, :, :], y[:, :, :], bias[:, :].unsqueeze(1).to_broadcast(wide), ALU.add))
            order.done(dve.tensor_scalar(y[:, :, :], y[:, :, :], -LIMIT, LIMIT, ALU.max, ALU.min))
            dve.tensor_tensor(g.x[:, :, :], g.x[:, :, :], y[:, :, :], ALU.add)

        @block.scalar
        def _(act):
            act.wait_ge(w_transposed, 1)
            act.activation(wT[:, :], g.ps[:, 0:P], ACT.Copy).then_inc(w_ready, 1)

        @block.tensor
        def _(pe):
            pe.wait_ge(signs, 1)
            pe.transpose(g.ps[:, 0:P], w[:, :], g.ident[:, :]).then_inc(w_transposed, 1)
            pe.wait_ge(w_ready, 1)
            for t in range(TILES):
                last = pe.matmul(g.ps[:, t * P:(t + 1) * P], hT[:, t * P:(t + 1) * P], wT[:, :], start=True, stop=True)
            last.then_inc(product_done, 1)


class Globals:
    pass


def build(nc, d, out, stop=99):
    g = Globals()
    with ExitStack() as ctx:
        g.x = ctx.enter_context(nc.sbuf_tensor("x_residual", [P, 16, P], F32))
        g.ident = ctx.enter_context(nc.sbuf_tensor("ident", [P, P], F32))
        g.identb = ctx.enter_context(nc.sbuf_tensor("identb", [P, P], BF16))
        g.causal = ctx.enter_context(nc.sbuf_tensor("causal_mask", [P, 3 * P], BF16))
        g.band = ctx.enter_context(nc.sbuf_tensor("band_mask", [P, 3 * P], BF16))
        g.ps = ctx.enter_context(nc.psum_tensor("banks", [P, 8 * BANK], F32))
        g.ctxT = ctx.enter_context(nc.sbuf_tensor("contextT", [P, BATCHES, KEYS], F32))
        stages = [load_stage, context_stage, scan_stage,
                  lambda *a: cross_stage(*a, "L0_xattn", "q", "k", "v", "0", 8 ** -0.5, False),
                  local_stage, causal_stage,
                  lambda *a: cross_stage(*a, "L1_xattn", "q", "k", "v", "o", 64 ** -0.5, True),
                  binary_stage]
        for i, f in enumerate(stages):
            if i <= stop:
                with ExitStack() as sem_ctx:
                    g.sems = Semaphores(nc, sem_ctx)
                    f(nc, g, d)
                    g.sems.clear()
        stored = ctx.enter_context(nc.semaphore("stored"))
        block = ctx.enter_context(nc.Block())

        @block.sync
        def _(sp):
            sp.dma_start(out.rearrange("b (t p) c -> p (b t) c", p=P), g.x[:, :, :]).then_inc(stored, 16)
            sp.wait_ge(stored, 16)


def rotary_tables():
    import numpy as np
    f = np.float32
    half = np.arange(0, LDIM, 2, dtype=f)
    inv_freq = (f(1.0) / np.power(f(10000.0), half / f(LDIM))).astype(f)
    t = np.arange(SEQ, dtype=f)
    freqs = np.tile(t[:, None] * inv_freq[None, :], (1, 2)).astype(f)
    base = ((half + f(0.4 * LDIM)) / f(1.4 * LDIM)).astype(f)
    power = ((t - SEQ // 2) / f(WINDOW // 2)).astype(f)
    scale = np.tile(np.power(base[None, :], power[:, None]), (1, 2)).astype(f)
    sign = np.where(np.arange(LDIM) < LDIM // 2, f(-1.0), f(1.0))
    cos, sin = np.cos(freqs), np.sin(freqs) * sign
    return np.stack([cos * scale, sin * scale, cos / scale, sin / scale]).astype(f)


def kernel(**inputs):
    import numpy as np
    from concourse import bacc
    from concourse.bass_utils import run_bass_kernel_spmd

    nc = bacc.Bacc("TRN2", target_bir_lowering=False, num_devices=1)
    arrays, d = {}, {}
    for name, a in list(inputs.items()) + [("rotary", rotary_tables())]:
        a = np.ascontiguousarray(a)
        arrays[f"in_{name}_dram"] = a
        d[name] = nc.dram_tensor(f"in_{name}_dram", a.shape, mybir.dt.from_np(a.dtype), kind="ExternalInput").ap()
    out = nc.dram_tensor("out_0_dram", inputs["x"].shape, F32, kind="ExternalOutput").ap()
    build(nc, d, out)
    r = run_bass_kernel_spmd(nc, [arrays], core_ids=[0])
    return r.results[0]["out_0_dram"]
```

```python
from contextlib import ExitStack

import concourse.bass as bass
from concourse import mybir

F32 = mybir.dt.float32
BF16 = mybir.dt.bfloat16
I32 = mybir.dt.int32
ALU = mybir.AluOpType
ACT = mybir.ActivationFunctionType
AX = mybir.AxisListType

P = 128
BANK = 512
EPS = 1e-5


def wait(eng, sem, value):
    if not isinstance(value, int) or value > 0:
        eng.wait_ge(sem, value)


class Order:

    def __init__(self, eng, sem):
        self.eng, self.sem, self.n = eng, sem, 0

    def done(self, ins):
        self.n += 1
        ins.then_inc(self.sem, 1)
        self.eng.wait_ge(self.sem, self.n)


class Stage:

    def __init__(self, nc, ctx, sems, name):
        self.nc, self.ctx, self.sems, self.name = nc, ctx, sems, name

    def sb(self, name, shape, dt=F32):
        return self.ctx.enter_context(self.nc.sbuf_tensor(f"{self.name}_{name}", shape, dt))

    def sem(self, name):
        return self.sems.new(f"{self.name}_{name}")


class Semaphores:

    def __init__(self, nc, ctx):
        self.nc, self.ctx, self.held = nc, ctx, []

    def new(self, name):
        self.held.append(self.ctx.enter_context(self.nc.semaphore(name)))
        return self.held[-1]

    def clear(self):
        with self.nc.Block() as block:
            @block.sync
            def _(sp):
                for sem in self.held:
                    sp.sem_clear(sem)


def column(ap):
    return ap.rearrange("(p o) -> p o", o=1)


def norm_vector(dve, order, src, dst, sq, st, var_ready, std_ready, count):
    n = src.shape[1]
    wide = [P, n, P]
    order.done(dve.tensor_reduce(st[:, 0, :], src, AX.X, ALU.add))
    order.done(dve.tensor_scalar(st[:, 0, :], st[:, 0, :], 1.0 / P, None, ALU.mult))
    order.done(dve.tensor_tensor(dst, src, st[:, 0, :].unsqueeze(2).to_broadcast(wide), ALU.subtract))
    order.done(dve.tensor_tensor(sq, dst, dst, ALU.mult))
    order.done(dve.tensor_reduce(st[:, 1, :], sq, AX.X, ALU.add))
    dve.tensor_scalar(st[:, 1, :], st[:, 1, :], 1.0 / P, EPS, ALU.mult, ALU.add).then_inc(var_ready, 1)
    dve.wait_ge(std_ready, count)
    order.done(dve.reciprocal(st[:, 2, :], st[:, 1, :]))
    order.done(dve.tensor_tensor(dst, dst, st[:, 2, :].unsqueeze(2).to_broadcast(wide), ALU.mult))


def norm_scalar(act, st, var_ready, std_ready, count):
    act.wait_ge(var_ready, count)
    act.activation(st[:, 1, :], st[:, 1, :], ACT.Sqrt).then_inc(std_ready, 1)


def load_stage(nc, g, d):
    with ExitStack() as ctx:
        s = Stage(nc, ctx, g.sems, "load")
        x_loaded = s.sem("x_loaded")
        zeroed, made = s.sem("zeroed"), s.sem("made")
        block = ctx.enter_context(nc.Block())

        @block.sync
        def _(sp):
            sp.dma_start(g.x[:, :, :], d["x"].rearrange("b (t p) c -> p (b t) c", p=P)).then_inc(x_loaded, 16)
            sp.wait_ge(x_loaded, 16)

        @block.gpsimd
        def _(pool):
            pool.memset(g.ident[:, :], 0.0).then_inc(zeroed, 1)
            pool.memset(g.identb[:, :], 0.0).then_inc(zeroed, 1)
            pool.memset(g.causal[:, :], 0.0).then_inc(zeroed, 1)
            pool.wait_ge(zeroed, 3)
            for m in (g.ident, g.identb):
                pool.affine_select(out=m[:, :], in_=m[:, :], compare_op=ALU.not_equal, fill=1.0, base=0,
                                   pattern=[[-1, P]], channel_multiplier=1).then_inc(made, 1)
            for col, n, first in ((0, P, 0), (P, 2 * P, P)):
                m = g.causal[:, col:col + n]
                pool.affine_select(out=m, in_=m, compare_op=ALU.is_ge, fill=MASKED, base=first,
                                   pattern=[[-1, n]], channel_multiplier=1).then_inc(made, 1)
            pool.wait_ge(made, 4)
            for col, n, first in ((0, P, 0), (P, 2 * P, P)):
                pool.affine_select(out=g.band[:, col:col + n], in_=g.causal[:, col:col + n], compare_op=ALU.is_ge,
                                   fill=MASKED, base=WINDOW - first, pattern=[[1, n]],
                                   channel_multiplier=-1).then_inc(made, 1)


MASKED = -1.0e25
WINDOW = 64


def scan_stage(nc, g, d):
    tokens = g.x.shape[1] * P
    T = tokens // P
    B, L = 8, tokens // 8
    with ExitStack() as ctx:
        s = Stage(nc, ctx, g.sems, "scan")
        h0 = s.sb("h0", [P, T, P])
        hn = s.sb("hn", [P, T, P])
        sq = s.sb("sq", [P, T, P])
        st = s.sb("st", [P, 3, T])
        hT = s.sb("hT", [P, tokens])
        xc = s.sb("xc", [P, tokens])
        xa = s.sb("xa", [P, tokens])
        zs = s.sb("zs", [P, tokens])
        low = s.sb("low", [112, tokens])
        v = s.sb("v", [P, tokens])
        e = s.sb("e", [P, tokens])
        u = s.sb("u", [P, tokens])
        small = s.sb("small", [P, tokens], I32)
        series = s.sb("series", [P, tokens])
        dA = s.sb("dA", [P, tokens])
        w_in = s.sb("w_in", [P, 2 * P])
        w_low = s.sb("w_low", [P, 112])
        w_up = s.sb("w_up", [112, P])
        w_out = s.sb("w_out", [P, P])
        conv = s.sb("conv", [P, 3])
        cols = s.sb("cols", [P, 6])
        gamma, beta, conv_b, b_dt, A, skip = (cols[:, i:i + 1] for i in range(6))
        loaded, gap_zeroed = s.sem("loaded"), s.sem("gap_zeroed")
        var_ready, std_ready = s.sem("var_ready"), s.sem("std_ready")
        hn_ready, hn_transposed, hT_ready = s.sem("hn_ready"), s.sem("hn_transposed"), s.sem("hT_ready")
        xb_ready, z_ready, zs_ready = s.sem("xb_ready"), s.sem("z_ready"), s.sem("zs_ready")
        xc_ready, xa_ready = s.sem("xc_ready"), s.sem("xa_ready")
        low_product, low_ready = s.sem("low_product"), s.sem("low_ready")
        v_product, bm_product, cm_product = s.sem("v_product"), s.sem("bm_product"), s.sem("cm_product")
        v_ready, e_ready, u_ready, log_ready = s.sem("v_ready"), s.sem("e_ready"), s.sem("u_ready"), s.sem("log_ready")
        delta_ready, dA_ready = s.sem("delta_ready"), s.sem("dA_ready")
        gated_ready, out_product = s.sem("gated_ready"), s.sem("out_product")
        dve_order, act_order = s.sem("dve_order"), s.sem("act_order")
        LOADS = 15
        ps = g.ps
        lo, hi = ps[:, 0:tokens], ps[:, tokens:2 * tokens]
        block = ctx.enter_context(nc.Block())

        @block.sync
        def _(sp):
            pairs = [(w_in[:, :], d["L0_attn_W_in"]), (w_out[:, :], d["L0_attn_W_out"])]
            pairs += [(c, column(d["L0_attn_" + n])) for c, n in (
                (gamma, "gamma"), (beta, "beta"), (conv_b, "conv_b"), (b_dt, "b_dt"), (A, "A"), (skip, "D_skip"))]
            for dst, src in pairs:
                sp.dma_start(dst, src).then_inc(loaded, 16)
            for k in range(3):
                sp.dma_start(conv[:, k:k + 1], d["L0_attn_conv_w"][k].rearrange("o c -> c o")).then_inc(loaded, 16)
            sp.dma_start(w_up[0:64, :], d["L0_attn_W_dt"]).then_inc(loaded, 16)
            sp.dma_start(w_up[64:80, :], d["L0_attn_W_Bp"]).then_inc(loaded, 16)
            sp.dma_start(w_up[96:112, :], d["L0_attn_W_Cp"]).then_inc(loaded, 16)
            sp.wait_ge(gap_zeroed, 1)
            sp.dma_start(w_low[:, 0:64], d["L0_attn_W_xp"]).then_inc(loaded, 16)
            sp.dma_start(w_low[:, 64:80], d["L0_attn_W_Bg"]).then_inc(loaded, 16)
            sp.dma_start(w_low[:, 96:112], d["L0_attn_W_Cg"]).then_inc(loaded, 16)

        @block.gpsimd
        def _(pool):
            pool.memset(w_low[:, :], 0.0).then_inc(gap_zeroed, 1)

        @block.vector
        def _(dve):
            order = Order(dve, dve_order)
            norm_vector(dve, order, g.x[:, :, :], h0[:, :, :], sq[:, :, :], st, var_ready, std_ready, 1)
            norm_vector(dve, order, h0[:, :, :], hn[:, :, :], sq[:, :, :], st, var_ready, std_ready, 2)
            order.done(dve.tensor_tensor(g.x[:, :, :], g.x[:, :, :], h0[:, :, :], ALU.add))
            dve.sem_inc(hn_ready, 1)
            dve.wait_ge(xb_ready, 1)
            dve.wait_ge(loaded, 16 * (LOADS + 2))
            order.done(dve.tensor_scalar(xc[:, :], hi, conv[:, 1:2], conv_b, ALU.mult, ALU.add))
            c3, x3 = xc[:, :].rearrange("p (b l) -> p b l", b=B), hi.rearrange("p (b l) -> p b l", b=B)
            order.done(dve.scalar_tensor_tensor(out=c3[:, :, 1:L], in0=x3[:, :, 0:L - 1], scalar=conv[:, 0:1],
                                                in1=c3[:, :, 1:L], op0=ALU.mult, op1=ALU.add))
            dve.scalar_tensor_tensor(out=c3[:, :, 0:L - 1], in0=x3[:, :, 1:L], scalar=conv[:, 2:3],
                                     in1=c3[:, :, 0:L - 1], op0=ALU.mult, op1=ALU.add).then_inc(xc_ready, 1)
            dve.wait_ge(v_product, 1)
            dve.tensor_scalar(v[:, :], lo, b_dt, None, ALU.add).then_inc(v_ready, 1)
            dve.wait_ge(e_ready, 1)
            order.done(dve.tensor_scalar(series[:, :], e[:, :], 1.0 / 3, -0.5, ALU.mult, ALU.add))
            order.done(dve.tensor_scalar(small[:, :], e[:, :], 2.0 ** -7, None, ALU.is_lt))
            order.done(dve.tensor_tensor(series[:, :], series[:, :], e[:, :], ALU.mult))
            order.done(dve.scalar_tensor_tensor(out=series[:, :], in0=series[:, :], scalar=1.0, in1=e[:, :],
                                                op0=ALU.add, op1=ALU.mult))
            dve.wait_ge(log_ready, 1)
            order.done(dve.copy_predicated(u[:, :], small[:, :], series[:, :]))
            dve.scalar_tensor_tensor(out=v[:, :], in0=v[:, :], scalar=0.0, in1=u[:, :], op0=ALU.max,
                                     op1=ALU.add).then_inc(delta_ready, 1)
            dve.wait_ge(delta_ready, 1)
            dve.wait_ge(bm_product, 1)
            order.done(dve.tensor_tensor(e[:, :], v[:, :], hi, ALU.mult))
            order.done(dve.tensor_tensor(e[:, :], e[:, :], xa[:, :], ALU.mult))
            dve.wait_ge(dA_ready, 1)
            for b in range(B):
                c = slice(b * L, (b + 1) * L)
                order.done(dve.tensor_tensor_scan(u[:, c], dA[:, c], e[:, c], 0.0, ALU.mult, ALU.add))
            dve.wait_ge(cm_product, 1)
            order.done(dve.tensor_tensor(u[:, :], u[:, :], lo, ALU.mult))
            order.done(dve.scalar_tensor_tensor(out=u[:, :], in0=xa[:, :], scalar=skip, in1=u[:, :],
                                                op0=ALU.mult, op1=ALU.add))
            dve.wait_ge(zs_ready, 1)
            dve.tensor_tensor(u[:, :], u[:, :], zs[:, :], ALU.mult).then_inc(gated_ready, 1)
            dve.wait_ge(out_product, 1)
            dve.tensor_tensor(g.x[:, :, :], g.x[:, :, :], hi.rearrange("p (t c) -> p t c", c=P), ALU.add)

        @block.scalar
        def _(act):
            order = Order(act, act_order)
            norm_scalar(act, st, var_ready, std_ready, 1)
            norm_scalar(act, st, var_ready, std_ready, 2)
            act.wait_ge(loaded, 16 * (LOADS + 2))
            act.wait_ge(hn_transposed, 1)
            act.activation(hT[:, :], lo, ACT.Identity, bias=beta, scale=gamma).then_inc(hT_ready, 1)
            act.wait_ge(z_ready, 1)
            act.activation(zs[:, :], lo, ACT.Silu).then_inc(zs_ready, 1)
            act.wait_ge(xc_ready, 1)
            act.activation(xa[:, :], xc[:, :], ACT.Silu).then_inc(xa_ready, 1)
            act.wait_ge(low_product, 1)
            act.activation(low[:, :], hi[0:112, :], ACT.Copy).then_inc(low_ready, 1)
            act.wait_ge(v_ready, 1)
            order.done(act.activation(e[:, :], v[:, :], ACT.Abs))
            act.activation(e[:, :], e[:, :], ACT.Exp, scale=-1.0).then_inc(e_ready, 1)
            act.wait_ge(e_ready, 1)
            act.activation(u[:, :], e[:, :], ACT.Ln, bias=1.0).then_inc(log_ready, 1)
            act.wait_ge(delta_ready, 1)
            act.activation(dA[:, :], v[:, :], ACT.Exp, scale=A).then_inc(dA_ready, 1)

        @block.tensor
        def _(pe):
            def product(base, lhsT, rhs, rows=P):
                for n in range(tokens // BANK):
                    c = slice(n * BANK, (n + 1) * BANK)
                    last = pe.matmul(ps[0:rows, base + n * BANK:base + (n + 1) * BANK], lhsT, rhs[:, c],
                                     start=True, stop=True)
                return last

            pe.wait_ge(hn_ready, 1)
            for t in range(T):
                last = pe.transpose(ps[:, t * P:(t + 1) * P], hn[:, t, :], g.ident[:, :])
            last.then_inc(hn_transposed, 1)
            pe.wait_ge(hT_ready, 1)
            product(tokens, w_in[:, 0:P], hT).then_inc(xb_ready, 1)
            product(0, w_in[:, P:2 * P], hT).then_inc(z_ready, 1)
            pe.wait_ge(xa_ready, 1)
            product(tokens, w_low[:, :], xa, 112).then_inc(low_product, 1)
            pe.wait_ge(low_ready, 1)
            pe.wait_ge(zs_ready, 1)
            product(0, w_up[0:64, :], low[0:64, :]).then_inc(v_product, 1)
            product(tokens, w_up[64:80, :], low[64:80, :]).then_inc(bm_product, 1)
            pe.wait_ge(v_ready, 1)
            product(0, w_up[96:112, :], low[96:112, :]).then_inc(cm_product, 1)
            pe.wait_ge(gated_ready, 1)
            for t in range(T):
                last = pe.matmul(ps[:, tokens + t * P:tokens + (t + 1) * P], u[:, t * P:(t + 1) * P], w_out[:, :],
                                 start=True, stop=True)
            last.then_inc(out_product, 1)


HEADS = 16
BATCHES = 8
TILES = 16
KEYS = 1601
KT = (KEYS + P - 1) // P
TAIL = KEYS - (KT - 1) * P
SPLIT = ((0, 401), (401, 400), (801, 400), (1201, 400))
GROUPS = ((0, 4), (4, 4), (8, 4), (12, 1))


def load_context(sp, d, b, dst, loaded):
    c = d["ctx_1024"][b]
    whole = (KT - 1) * P
    sp.dma_start(dst[:, 0:KT - 1, :], c[0:whole, :].rearrange("(t p) c -> p t c", p=P)).then_inc(loaded, 16)
    sp.dma_start(dst[0:TAIL, KT - 1, :], c[whole:KEYS, :]).then_inc(loaded, 16)


def context_stage(nc, g, d):
    with ExitStack() as ctx:
        s = Stage(nc, ctx, g.sems, "context")
        raw = [s.sb(f"raw{i}", [P, KT, P]) for i in range(2)]
        raw_loaded = [s.sem(f"raw_loaded{i}") for i in range(2)]
        transposed = [s.sem(f"transposed{i}") for i in range(2)]
        copied = [s.sem(f"copied{i}") for i in range(2)]
        block = ctx.enter_context(nc.Block())

        def bank(n):
            return g.ps[:, (n % 8) * BANK:(n % 8 + 1) * BANK]

        @block.sync
        def _(sp):
            for b in range(BATCHES):
                wait(sp, transposed[1], 2 * b - 2)
                load_context(sp, d, b, raw[b % 2], raw_loaded[b % 2])

        @block.tensor
        def _(pe):
            for b in range(BATCHES):
                pe.wait_ge(raw_loaded[b % 2], 32 * (b // 2 + 1))
                for j, (t0, n) in enumerate(GROUPS):
                    wait(pe, copied[j % 2], 2 * (b - 2) + j // 2 + 1)
                    for i in range(n):
                        rows = P if t0 + i < KT - 1 else TAIL
                        last = pe.transpose(bank(4 * b + j)[:, i * P:i * P + rows], raw[b % 2][0:rows, t0 + i, :],
                                            g.ident[0:rows, 0:rows])
                    last.then_inc(transposed[j % 2], 1)

        def copies(eng, side, copy):
            for b in range(BATCHES):
                for j in (side, side + 2):
                    t0, n = GROUPS[j]
                    cols = min(n * P, KEYS - t0 * P)
                    eng.wait_ge(transposed[side], 2 * b + j // 2 + 1)
                    copy(g.ctxT[:, b, t0 * P:t0 * P + cols], bank(4 * b + j)[:, 0:cols]).then_inc(copied[side], 1)

        @block.scalar
        def _(act):
            copies(act, 0, lambda o, i: act.activation(o, i, ACT.Copy))

        @block.vector
        def _(dve):
            copies(dve, 1, dve.tensor_copy)


def transpose_tokens(g, pe, src, base, done):
    for t in range(TILES):
        last = pe.transpose(g.ps[:, base + t * P:base + (t + 1) * P], src[:, t, :], g.ident[:, :])
    last.then_inc(done, 1)


def cross_stage(nc, g, d, name, scale):
    wq, wk, wv = (d[f"{name}_W{n}"].rearrange("c h e -> c (h e)") for n in "qkv")
    bq, bk, bv = (d[f"{name}_b{n}"].rearrange("h e -> (h e)") for n in "qkv")
    wo = d[name + "_Wo"].rearrange("h e c -> (h e) c")
    with ExitStack() as ctx:
        so = Stage(nc, ctx, g.sems, name)
        A = so.sb("A", [P, HEADS, P + 1])
        B = so.sb("B", [P, HEADS, P])
        cb = so.sb("cb", [P, TILES, HEADS])
        hT = so.sb("hT", [P, TILES * P])
        fold_weights(nc, g, name, A, B, cb, hT, scale, wq, wk, wv, wo, bq, bk, bv, d[name + "_bo"])
        cross_heads(nc, g, d, name, A, B, cb, hT)


def fold_weights(nc, g, name, A, B, cb, hT, scale, wq, wk, wv, wo, bq, bk, bv, bo):
    nb = wq.shape[1] // P
    per = HEADS // nb
    dh = P // per
    with ExitStack() as ctx:
        s = Stage(nc, ctx, g.sems, name + "_fold")
        hn = s.sb("hn", [P, TILES, P])
        sq = s.sb("sq", [P, TILES, P])
        st = s.sb("st", [P, 3, TILES])
        raw = s.sb("raw", [P, 3, nb * P])
        wT = s.sb("wT", [P, 3, nb, P])
        wo_sb = s.sb("wo", [P, nb, P])
        masked = s.sb("masked", [P, 2, HEADS, P])
        head_rows = s.sb("head_rows", [P, per])
        bcol = s.sb("bcol", [P, 3, nb])
        bmask = s.sb("bmask", [P, 2, nb, per])
        bwide = s.sb("bwide", [P, 2, nb, P])
        ones = s.sb("ones", [P, P])
        bo_rows = s.sb("bo_rows", [P, P])
        c_all = s.sb("c_all", [P, HEADS])
        c0 = s.sb("c0", [P, HEADS])
        orow = s.sb("orow", [P, P])
        loaded, rows_made = s.sem("loaded"), s.sem("rows_made")
        var_ready, std_ready = s.sem("var_ready"), s.sem("std_ready")
        hn_ready, hn_transposed, hT_ready = s.sem("hn_ready"), s.sem("hn_transposed"), s.sem("hT_ready")
        w_transposed, w_ready = s.sem("w_transposed"), s.sem("w_ready")
        masks_ready, a_product, a_copied = s.sem("masks_ready"), s.sem("a_product"), s.sem("a_copied")
        b_product, b_copied = s.sem("b_product"), s.sem("b_copied")
        bias_product, c_ready, cb_product = s.sem("bias_product"), s.sem("c_ready"), s.sem("cb_product")
        dve_order, pool_order = s.sem("dve_order"), s.sem("pool_order")
        ps = g.ps
        LOADS = 3 + 1 + 3 * nb + 1
        SUMS = 2 * BANK
        CB = 3 * BANK
        block = ctx.enter_context(nc.Block())

        @block.sync
        def _(sp):
            for i, w in enumerate((wq, wk, wv)):
                sp.dma_start(raw[:, i, :], w).then_inc(loaded, 16)
            sp.dma_start(wo_sb[:, :, :], wo.rearrange("(j p) c -> p j c", p=P)).then_inc(loaded, 16)
            for i, b in enumerate((bq, bk, bv)):
                for j in range(nb):
                    sp.dma_start(bcol[:, i, j:j + 1], column(b[j * P:(j + 1) * P])).then_inc(loaded, 16)
            sp.dma_start(bo_rows[:, :], bo.partition_broadcast(P)).then_inc(loaded, 16)

        @block.gpsimd
        def _(pool):
            order = Order(pool, pool_order)
            order.done(pool.memset(head_rows[:, :], 1.0))
            order.done(pool.memset(ones[:, :], 1.0))
            order.done(pool.affine_select(out=head_rows[:, :], in_=head_rows[:, :], compare_op=ALU.is_ge, fill=0.0,
                                          base=0, pattern=[[-dh, per]], channel_multiplier=1))
            pool.affine_select(out=head_rows[:, :], in_=head_rows[:, :], compare_op=ALU.is_ge, fill=0.0,
                               base=dh - 1, pattern=[[dh, per]], channel_multiplier=-1).then_inc(rows_made, 1)

        @block.vector
        def _(dve):
            order = Order(dve, dve_order)
            dve.wait_ge(rows_made, 1)
            dve.wait_ge(loaded, 16 * LOADS)
            for i in range(2):
                for j in range(nb):
                    order.done(dve.tensor_scalar(bmask[:, i, j, :], head_rows[:, :], bcol[:, i, j:j + 1], None,
                                                 ALU.mult))
                    order.done(dve.tensor_scalar(bwide[:, i, j, :], ones[:, :], bcol[:, 2 * i, j:j + 1], None,
                                                 ALU.mult))
            dve.wait_ge(w_ready, 1)
            for i in range(2):
                for r in range(per):
                    order.done(dve.tensor_scalar(masked[:, i, r:HEADS:per, :], wT[:, 2 * i, :, :],
                                                 head_rows[:, r:r + 1], None, ALU.mult))
            dve.sem_inc(masks_ready, 1)
            norm_vector(dve, order, g.x[:, :, :], hn[:, :, :], sq[:, :, :], st, var_ready, std_ready, 1)
            dve.sem_inc(hn_ready, 1)
            dve.wait_ge(b_product, 1)
            dve.tensor_copy(B[:, :, :], ps[:, 4 * BANK:8 * BANK].rearrange("p (h c) -> p h c", c=P))\
                .then_inc(b_copied, 1)
            dve.wait_ge(bias_product, 1)
            order.done(dve.tensor_scalar(A[:, :, P], ps[:, SUMS:SUMS + HEADS], scale, None, ALU.mult))
            order.done(dve.tensor_scalar(c_all[:, :], ps[:, SUMS + 16:SUMS + 32], scale, None, ALU.mult))
            order.done(dve.tensor_scalar(c0[:, :], ps[:, SUMS + 32:SUMS + 48], scale, None, ALU.mult))
            order.done(dve.tensor_tensor(orow[:, :], ps[:, SUMS + P:SUMS + 2 * P], bo_rows[:, :], ALU.add))
            dve.sem_inc(c_ready, 1)
            order.done(dve.tensor_tensor(g.x[:, :, :], g.x[:, :, :],
                                         orow[:, :].unsqueeze(1).to_broadcast([P, TILES, P]), ALU.add))
            dve.wait_ge(cb_product, 1)
            dve.tensor_tensor(cb[:, :, :], ps[:, CB:CB + TILES * HEADS].rearrange("p (t h) -> p t h", h=HEADS),
                              c0[:, :].unsqueeze(1).to_broadcast([P, TILES, HEADS]), ALU.add)

        @block.scalar
        def _(act):
            act.wait_ge(w_transposed, 1)
            act.activation(wT[:, :, :, :].rearrange("p k j c -> p (k j c)"), ps[:, 0:3 * nb * P], ACT.Copy)\
                .then_inc(w_ready, 1)
            norm_scalar(act, st, var_ready, std_ready, 1)
            act.wait_ge(a_product, 1)
            act.activation(A[:, :, 0:P], ps[:, 0:4 * BANK].rearrange("p (h c) -> p h c", c=P), ACT.Copy, scale=scale)\
                .then_inc(a_copied, 1)
            act.wait_ge(hn_transposed, 1)
            act.activation(hT[:, :], ps[:, 4 * BANK:8 * BANK], ACT.Copy).then_inc(hT_ready, 1)

        @block.tensor
        def _(pe):
            pe.wait_ge(loaded, 16 * LOADS)
            for i in range(3):
                for j in range(nb):
                    c = (i * nb + j) * P
                    last = pe.transpose(ps[:, c:c + P], raw[:, i, j * P:(j + 1) * P], g.ident[:, :])
            last.then_inc(w_transposed, 1)
            pe.wait_ge(masks_ready, 1)
            for h in range(HEADS):
                last = pe.matmul(ps[:, h * P:(h + 1) * P], masked[:, 0, h, :], wT[:, 1, h // per, :],
                                 start=True, stop=True)
            last.then_inc(a_product, 1)
            for h in range(HEADS):
                c = 4 * BANK + h * P
                last = pe.matmul(ps[:, c:c + P], masked[:, 1, h, :], wo_sb[:, h // per, :], start=True, stop=True)
            last.then_inc(b_product, 1)
            pe.wait_ge(a_copied, 1)
            for j in range(nb):
                c = SUMS + j * per
                pe.matmul(ps[:, c:c + per], wT[:, 1, j, :], bmask[:, 0, j, :], start=True, stop=True)
                pe.matmul(ps[:, c + 16:c + 16 + per], wT[:, 0, j, :], bmask[:, 1, j, :], start=True, stop=True)
                pe.matmul(ps[:, c + 32:c + 32 + per], bwide[:, 0, j, :], bmask[:, 1, j, :], start=True, stop=True)
            for j in range(nb):
                last = pe.matmul(ps[:, SUMS + P:SUMS + 2 * P], bwide[:, 1, j, :], wo_sb[:, j, :], start=(j == 0),
                                 stop=(j == nb - 1))
            last.then_inc(bias_product, 1)
            pe.wait_ge(hn_ready, 1)
            pe.wait_ge(b_copied, 1)
            transpose_tokens(g, pe, hn, 4 * BANK, hn_transposed)
            pe.wait_ge(hT_ready, 1)
            pe.wait_ge(c_ready, 1)
            for t in range(TILES):
                last = pe.matmul(ps[:, CB + t * HEADS:CB + (t + 1) * HEADS], hT[:, t * P:(t + 1) * P], c_all[:, :],
                                 start=True, stop=True)
            last.then_inc(cb_product, 1)


def cross_heads(nc, g, d, name, A, B, cb, hT):
    with ExitStack() as ctx:
        s = Stage(nc, ctx, g.sems, name + "_heads")
        kv = [s.sb(f"context{i}", [P, KT, P]) for i in range(2)]
        a_head = s.sb("a_head", [P, P + 1])
        qT = [s.sb(f"qT{i}", [P, 2 * P]) for i in range(2)]
        probs = [s.sb(f"probs{i}", [P, KEYS]) for i in range(2)]
        pT = [s.sb(f"pT{i}", [P, KT, 2 * P]) for i in range(2)]
        mixed = s.sb("mixed", [P, 2 * P])
        peak = s.sb("peak", [P, 2, 3])
        shift = s.sb("shift", [P, 2])
        total = s.sb("total", [P, 2, 2, 2])
        inverse = s.sb("inverse", [P, 2, 2])
        kv_loaded = [s.sem(f"kv_loaded{i}") for i in range(2)]
        a_copied, q_product, q_ready = s.sem("a_copied"), s.sem("q_product"), s.sem("q_ready")
        scores_ready, parts_ready, peak_ready = s.sem("scores_ready"), s.sem("parts_ready"), s.sem("peak_ready")
        shift_ready, exp_done = s.sem("shift_ready"), s.sem("exp_done")
        transposed = [s.sem(f"transposed{i}") for i in range(2)]
        pT_copied = [s.sem(f"pT_copied{i}") for i in range(2)]
        mix_product, mix_ready = s.sem("mix_product"), s.sem("mix_ready")
        out_product, out_added = s.sem("out_product"), s.sem("out_added")
        sums_ready, inverse_ready = s.sem("sums_ready"), s.sem("inverse_ready")
        ps = g.ps
        score = ps[:, 0:4 * BANK].rearrange("p (k n) -> p k n", n=BANK)
        tbank = [ps[:, (4 + i) * BANK:(5 + i) * BANK] for i in range(2)]
        mix = ps[:, 6 * BANK:6 * BANK + 2 * P]
        q_ps = ps[:, 7 * BANK:7 * BANK + 2 * P]
        out_ps = ps[:, 7 * BANK + 2 * P:8 * BANK]
        xf = g.x[:, :, :].rearrange("p t c -> p (t c)")
        cbf = cb[:, :, :].rearrange("p t h -> p (t h)")
        LAST = BATCHES * HEADS - 1
        QUARTER = KEYS // 4
        EARLY = KT // 2
        block = ctx.enter_context(nc.Block())

        def walk(eng, step):
            def batch(b, slot, first):
                step(b, 0, 0, slot, 0 if first else 2)
                step(b, 1, 1, slot, 1 if first else 2)
                with eng.Fori(1, HEADS // 2) as pair:
                    for k in range(2):
                        step(b, pair * 2 + k, k, slot, 2)

            batch(0, 0, True)
            batch(1, 1, False)
            with eng.Fori(1, BATCHES // 2) as two:
                for slot in range(2):
                    batch(two * 2 + slot, slot, False)

        def earlier(b, h, back):
            if isinstance(h, int) and h < back:
                return b - 1, h - back + HEADS
            return b, h - back

        def slot_of(h, slot, back):
            return 1 - slot if isinstance(h, int) and h < back else slot

        @block.sync
        def _(sp):
            for b in range(BATCHES):
                wait(sp, mix_product, HEADS * (b - 1))
                load_context(sp, d, b, kv[b % 2], kv_loaded[b % 2])

        @block.gpsimd
        def _(pool):
            with pool.Fori(0, BATCHES) as b:
                with pool.Fori(0, HEADS) as h:
                    pool.wait_ge(q_ready, b * HEADS + h)
                    pool.tensor_copy(a_head[:, :], A[:, :, :].rearrange("p h c -> p (h c)")[
                        :, bass.ds(h * (P + 1), P + 1)]).then_inc(a_copied, 1)

        @block.tensor
        def _(pe):
            def project(n, b):
                pe.wait_ge(a_copied, n + 1)
                wait(pe, out_added, n - 2)
                pe.matmul(q_ps, a_head[:, 0:P], hT[:, bass.ds(b * (2 * P), 2 * P)], start=True, stop=True)\
                    .then_inc(q_product, 1)

            def scores(n, b, k, q):
                u = n * 2 + q
                pe.wait_ge(q_ready, n + 1)
                for i, (bank, width) in enumerate(((3, QUARTER + 1), (2, QUARTER + 1), (0, QUARTER), (1, QUARTER))):
                    if i == 0:
                        wait(pe, exp_done, u * 2 - 1)
                    if i == 1:
                        wait(pe, exp_done, u * 2)
                    ins = pe.matmul(score[:, bank, 0:width], qT[k][:, q * P:(q + 1) * P],
                                    g.ctxT[:, b, bank * QUARTER:bank * QUARTER + width], start=True, stop=True)
                    if i % 2 == 1:
                        ins.then_inc(scores_ready, 1)

            def transposes(n, q, groups):
                u = n * 2 + q
                pe.wait_ge(exp_done, u * 2 + 2)
                for j in groups:
                    t0, w = GROUPS[j]
                    wait(pe, pT_copied[j % 2], u * 2 + j // 2)
                    for t in range(t0, t0 + w):
                        rows = P if t < KT - 1 else TAIL
                        ins = pe.transpose(tbank[j % 2][0:rows, (t - t0) * P:(t - t0 + 1) * P],
                                           probs[q][:, t * P:t * P + rows], g.ident[:, :])
                    ins.then_inc(transposed[j % 2], 1)

            def mix_tiles(n, k, slot, tiles):
                u = n * 2 + 1
                if tiles[0] == 0:
                    wait(pe, mix_ready, n)
                for t in tiles:
                    if t % 4 == 0 or t == tiles[0]:
                        j = t // 4
                        pe.wait_ge(pT_copied[j % 2], u * 2 + j // 2 + 1)
                    rows = P if t < KT - 1 else TAIL
                    ins = pe.matmul(mix, kv[slot][0:rows, t, :], pT[k][0:rows, t, :], start=(t == 0),
                                    stop=(t == KT - 1))
                if tiles[-1] == KT - 1:
                    ins.then_inc(mix_product, 1)

            def output(n, h):
                pe.wait_ge(mix_ready, n + 1)
                wait(pe, out_added, n)
                for q in range(2):
                    ins = pe.matmul(out_ps[:, q * P:(q + 1) * P], mixed[:, q * P:(q + 1) * P],
                                    B[:, :, :].rearrange("p h c -> p (h c)")[:, bass.ds(h * P, P)],
                                    start=True, stop=True)
                ins.then_inc(out_product, 1)

            def step(b, h, k, slot, before):
                n = b * HEADS + h
                if isinstance(h, int) and h == 1:
                    pe.wait_ge(kv_loaded[slot], (b - slot) * 16 + 32)
                project(n, b)
                if before >= 2:
                    mix_tiles(n - 2, k, slot_of(h, slot, 2), range(EARLY, EARLY + 2))
                scores(n, b, k, 0)
                if before >= 1:
                    transposes(n - 1, 1, (0, 1))
                if before >= 2:
                    mix_tiles(n - 2, k, slot_of(h, slot, 2), range(EARLY + 2, EARLY + 4))
                if before >= 1:
                    transposes(n - 1, 1, (2,))
                if before >= 2:
                    mix_tiles(n - 2, k, slot_of(h, slot, 2), range(EARLY + 4, KT))
                if before >= 1:
                    transposes(n - 1, 1, (3,))
                scores(n, b, k, 1)
                transposes(n, 0, (0, 1))
                if before >= 1:
                    mix_tiles(n - 1, 1 - k, slot_of(h, slot, 1), range(0, 2))
                transposes(n, 0, (2,))
                if before >= 2:
                    output(n - 2, earlier(b, h, 2)[1])
                if before >= 1:
                    mix_tiles(n - 1, 1 - k, slot_of(h, slot, 1), range(2, EARLY))
                transposes(n, 0, (3,))

            walk(pe, step)
            mix_tiles(LAST - 1, 0, 1, range(EARLY, KT))
            transposes(LAST, 1, range(4))
            output(LAST - 1, HEADS - 2)
            mix_tiles(LAST, 1, 1, range(0, KT))
            output(LAST, HEADS - 1)

        def copy_groups(eng, side, copy, n, k, q, which=(0, 1)):
            u = n * 2 + q
            if q == 0:
                wait(eng, mix_product, n - 1)
            for j in (side + 2 * i for i in which):
                t0, w = GROUPS[j]
                rows = P if j < 3 else TAIL
                eng.wait_ge(transposed[side], u * 2 + j // 2 + 1)
                copy(pT[k][0:rows, t0:t0 + w, q * P:(q + 1) * P],
                     tbank[side][0:rows, 0:w * P].rearrange("p (t c) -> p t c", c=P)).then_inc(pT_copied[side], 1)

        @block.scalar
        def _(act):
            def copy(o, i):
                return act.activation(o, i, ACT.Copy)

            def exps(n, k, q):
                u = n * 2 + q
                act.wait_ge(shift_ready, u + 1)
                wait(act, transposed[1], u * 2 - 2)
                wait(act, inverse_ready, n - 1)
                act.activation(probs[q][:, 3 * QUARTER:KEYS], score[:, 3, 0:QUARTER + 1], ACT.Exp,
                               bias=shift[:, q:q + 1], accum_out=total[:, k, q, 0:1]).then_inc(exp_done, 1)
                act.activation(probs[q][:, 0:3 * QUARTER].rearrange("p (a n) -> p a n", n=QUARTER),
                               score[:, 0:3, 0:QUARTER], ACT.Exp, bias=shift[:, q:q + 1],
                               accum_out=total[:, k, q, 1:2]).then_inc(exp_done, 1)

            def take_mix(n):
                act.wait_ge(mix_product, n + 1)
                wait(act, out_product, n)
                act.activation(mixed[:, :], mix, ACT.Copy).then_inc(mix_ready, 1)

            def step(b, h, k, slot, before):
                n = b * HEADS + h
                act.wait_ge(q_product, n + 1)
                act.activation(qT[k][:, :], q_ps, ACT.Identity, bias=a_head[:, P:P + 1]).then_inc(q_ready, 1)
                if before >= 1:
                    copy_groups(act, 0, copy, n - 1, 1 - k, 1, (0,))
                exps(n, k, 0)
                if before >= 1:
                    copy_groups(act, 0, copy, n - 1, 1 - k, 1, (1,))
                if before >= 2:
                    take_mix(n - 2)
                copy_groups(act, 0, copy, n, k, 0, (0,))
                exps(n, k, 1)
                copy_groups(act, 0, copy, n, k, 0, (1,))

            walk(act, step)
            take_mix(LAST - 1)
            copy_groups(act, 0, copy, LAST, 1, 1)
            take_mix(LAST)

        @block.vector
        def _(dve):
            def shifts(b, h, n, q):
                u = n * 2 + q
                dve.wait_ge(scores_ready, u * 2 + 1)
                dve.tensor_reduce(peak[:, q, 0:1], score[:, 2:4, 0:QUARTER + 1], AX.XY, ALU.max)
                dve.wait_ge(scores_ready, u * 2 + 2)
                dve.tensor_reduce(peak[:, q, 1:2], score[:, 0:2, 0:QUARTER], AX.XY, ALU.max).then_inc(parts_ready, 1)
                cb_u = cbf[:, bass.ds((b * 2 + q) * HEADS + h, 1)]
                dve.wait_ge(parts_ready, u + 1)
                dve.scalar_tensor_tensor(out=peak[:, q, 2:3], in0=peak[:, q, 0:1], scalar=peak[:, q, 1:2], in1=cb_u,
                                         op0=ALU.max, op1=ALU.add).then_inc(peak_ready, 1)
                dve.wait_ge(peak_ready, u + 1)
                dve.tensor_tensor(shift[:, q:q + 1], cb_u, peak[:, q, 2:3], ALU.subtract).then_inc(shift_ready, 1)

            def inverses(n, k):
                dve.wait_ge(exp_done, n * 4 + 4)
                dve.tensor_tensor(inverse[:, k, :], total[:, k, :, 0], total[:, k, :, 1], ALU.add).then_inc(sums_ready, 1)
                dve.wait_ge(sums_ready, n + 1)
                dve.reciprocal(inverse[:, k, :], inverse[:, k, :]).then_inc(inverse_ready, 1)

            def add_output(n, k, b):
                dve.wait_ge(out_product, n + 1)
                dve.wait_ge(inverse_ready, n + 1)
                for q in range(2):
                    rows = xf[:, bass.ds((b * 2 + q) * P, P)]
                    ins = dve.scalar_tensor_tensor(out=rows, in0=out_ps[:, q * P:(q + 1) * P],
                                                   scalar=inverse[:, k, q:q + 1], in1=rows, op0=ALU.mult, op1=ALU.add)
                ins.then_inc(out_added, 1)

            def step(b, h, k, slot, before):
                n = b * HEADS + h
                shifts(b, h, n, 0)
                if before >= 1:
                    inverses(n - 1, 1 - k)
                    copy_groups(dve, 1, dve.tensor_copy, n - 1, 1 - k, 1)
                shifts(b, h, n, 1)
                copy_groups(dve, 1, dve.tensor_copy, n, k, 0, (0,))
                if before >= 2:
                    add_output(n - 2, k, earlier(b, h, 2)[0])
                copy_groups(dve, 1, dve.tensor_copy, n, k, 0, (1,))

            walk(dve, step)
            dve.wait_ge(out_added, LAST - 1)
            inverses(LAST, 1)
            copy_groups(dve, 1, dve.tensor_copy, LAST, 1, 1)
            add_output(LAST - 1, 0, BATCHES - 1)
            add_output(LAST, 1, BATCHES - 1)


PRODUCTS = 6
SHIFT_ROWS = 3
PAIR = 2 * 2 * P
QUADS = HEADS // 4
WINDOW_KEYS = KEYS // 4 + 1
CHUNKS = 16
LAG = 2
SCORE_RING = 2
PROBS_RING = 4


def narrow_cross_stage(nc, g, d, name, scale):
    dh = P // HEADS
    qd = nc.dram_tensor(name + "_queries", (3, P, TILES * P), BF16, kind="Internal").ap()
    kd = nc.dram_tensor(name + "_keys", (3, BATCHES, P, KEYS), BF16, kind="Internal").ap()
    vd = nc.dram_tensor(name + "_values", (BATCHES, P, KT * HEADS * (dh + 1)), F32, kind="Internal").ap()
    narrow_queries(nc, g, d, name, qd, scale)
    narrow_keys(nc, g, d, name, kd, vd, dh)
    with ExitStack() as ctx:
        so = Stage(nc, ctx, g.sems, name)
        heads_out = so.sb("heads_out", [P, TILES, P])
        narrow_heads(nc, g, name, qd, kd, vd, heads_out, dh)
        reshuffled_output(nc, g, name, heads_out, d[name + "_w_0"], d[name + "_b_v"], dh)


def narrow_queries(nc, g, d, name, qd, scale):
    with ExitStack() as ctx:
        s = Stage(nc, ctx, g.sems, name + "_q")
        hn = s.sb("hn", [P, TILES, P])
        sq = s.sb("sq", [P, TILES, P])
        st = s.sb("st", [P, 3, TILES])
        hT = s.sb("hT", [P, TILES * P])
        q = s.sb("q", [P, TILES * P])
        rest = s.sb("rest", [P, TILES * P])
        parts = s.sb("parts", [P, 3, TILES * P], BF16)
        wq = s.sb("wq", [P, P])
        bq = s.sb("bq", [P, 1])
        b0_rows = s.sb("b0_rows", [P, P])
        loaded, var_ready, std_ready = s.sem("loaded"), s.sem("var_ready"), s.sem("std_ready")
        hn_ready, hn_transposed, hT_ready = s.sem("hn_ready"), s.sem("hn_transposed"), s.sem("hT_ready")
        q_product, parts_ready, stored = s.sem("q_product"), s.sem("parts_ready"), s.sem("stored")
        dve_order = s.sem("dve_order")
        block = ctx.enter_context(nc.Block())

        @block.sync
        def _(sp):
            sp.dma_start(wq[:, :], d[name + "_w_q"]).then_inc(loaded, 16)
            sp.dma_start(bq[:, :], column(d[name + "_b_q"])).then_inc(loaded, 16)
            sp.dma_start(b0_rows[:, :], d[name + "_b_0"].partition_broadcast(P)).then_inc(loaded, 16)
            for i in range(3):
                sp.wait_ge(parts_ready, i + 1)
                sp.dma_start(qd[i], parts[:, i, :]).then_inc(stored, 16)
            sp.wait_ge(stored, 3 * 16)

        @block.vector
        def _(dve):
            order = Order(dve, dve_order)
            norm_vector(dve, order, g.x[:, :, :], hn[:, :, :], sq[:, :, :], st, var_ready, std_ready, 1)
            dve.sem_inc(hn_ready, 1)
            dve.wait_ge(loaded, 3 * 16)
            order.done(dve.tensor_tensor(g.x[:, :, :], g.x[:, :, :],
                                         b0_rows[:, :].unsqueeze(1).to_broadcast([P, TILES, P]), ALU.add))
            dve.wait_ge(q_product, 1)
            order.done(dve.tensor_scalar(q[:, :], g.ps[:, 0:4 * BANK], bq[:, 0:1], scale, ALU.add, ALU.mult))
            order.done(dve.tensor_copy(parts[:, 0, :], q[:, :]))
            dve.sem_inc(parts_ready, 1)
            order.done(dve.tensor_tensor(rest[:, :], q[:, :], parts[:, 0, :], ALU.subtract))
            order.done(dve.tensor_copy(parts[:, 1, :], rest[:, :]))
            dve.sem_inc(parts_ready, 1)
            dve.tensor_tensor(parts[:, 2, :], rest[:, :], parts[:, 1, :], ALU.subtract).then_inc(parts_ready, 1)

        @block.scalar
        def _(act):
            norm_scalar(act, st, var_ready, std_ready, 1)
            act.wait_ge(hn_transposed, 1)
            act.activation(hT[:, :], g.ps[:, 4 * BANK:8 * BANK], ACT.Copy).then_inc(hT_ready, 1)

        @block.tensor
        def _(pe):
            pe.wait_ge(hn_ready, 1)
            transpose_tokens(g, pe, hn, 4 * BANK, hn_transposed)
            pe.wait_ge(hT_ready, 1)
            pe.wait_ge(loaded, 3 * 16)
            for i in range(4):
                last = pe.matmul(g.ps[:, i * BANK:(i + 1) * BANK], wq[:, :], hT[:, i * BANK:(i + 1) * BANK],
                                 start=True, stop=True)
            last.then_inc(q_product, 1)


def narrow_keys(nc, g, d, name, kd, vd, dh):
    with ExitStack() as ctx:
        s = Stage(nc, ctx, g.sems, name + "_kv")
        wk = s.sb("wk", [P, P])
        wv = s.sb("wv", [P, P])
        bk = s.sb("bk", [P, 1])
        keys = [s.sb(f"keys{i}", [P, KEYS]) for i in range(2)]
        rest = [s.sb(f"rest{i}", [P, KEYS]) for i in range(2)]
        parts = [s.sb(f"parts{i}", [P, 3, KEYS], BF16) for i in range(2)]
        values = [s.sb(f"values{i}", [P, KT, HEADS, dh + 1]) for i in range(2)]
        loaded, ones_made = s.sem("loaded"), s.sem("ones_made")
        k_product, k_ready, high_ready = s.sem("k_product"), s.sem("k_ready"), s.sem("high_ready")
        rest_ready, middle_ready, parts_ready = s.sem("rest_ready"), s.sem("middle_ready"), s.sem("parts_ready")
        v_product, v_ready = s.sem("v_product"), s.sem("v_ready")
        k_stored = [s.sem(f"k_stored{i}") for i in range(2)]
        v_stored = [s.sem(f"v_stored{i}") for i in range(2)]
        ps = g.ps
        V = 4 * BANK
        whole = KT - 1
        block = ctx.enter_context(nc.Block())

        @block.sync
        def _(sp):
            sp.dma_start(wk[:, :], d[name + "_w_k"]).then_inc(loaded, 16)
            sp.dma_start(wv[:, :], d[name + "_w_v"]).then_inc(loaded, 16)
            sp.dma_start(bk[:, :], column(d[name + "_b_k"])).then_inc(loaded, 16)
            for b in range(BATCHES):
                k = b % 2
                sp.wait_ge(v_ready, b + 1)
                sp.dma_start(vd[b], values[k][:, :, :, :].rearrange("p t h e -> p (t h e)")).then_inc(v_stored[k], 16)
                sp.wait_ge(parts_ready, b + 1)
                sp.dma_start(kd[:, b].rearrange("i p n -> p i n"), parts[k][:, :, :]).then_inc(k_stored[k], 16)
            for k in range(2):
                sp.wait_ge(v_stored[k], 16 * BATCHES // 2)
                sp.wait_ge(k_stored[k], 16 * BATCHES // 2)

        @block.gpsimd
        def _(pool):
            for k in range(2):
                pool.memset(values[k][:, :, :, :], 1.0).then_inc(ones_made, 1)
            for b in range(BATCHES):
                k = b % 2
                pool.wait_ge(high_ready, b + 1)
                wait(pool, parts_ready, b - 1)
                pool.tensor_tensor(rest[k][:, :], keys[k][:, :], parts[k][:, 0, :], ALU.subtract)\
                    .then_inc(rest_ready, 1)

        @block.vector
        def _(dve):
            for b in range(BATCHES):
                k = b % 2
                dve.wait_ge(k_ready, b + 1)
                wait(dve, k_stored[k], 16 * (b // 2))
                dve.tensor_copy(parts[k][:, 0, :], keys[k][:, :]).then_inc(high_ready, 1)
                dve.wait_ge(rest_ready, b + 1)
                dve.tensor_copy(parts[k][:, 1, :], rest[k][:, :]).then_inc(middle_ready, 1)
                dve.wait_ge(middle_ready, b + 1)
                dve.tensor_tensor(parts[k][:, 2, :], rest[k][:, :], parts[k][:, 1, :], ALU.subtract)\
                    .then_inc(parts_ready, 1)

        @block.scalar
        def _(act):
            act.wait_ge(loaded, 3 * 16)
            act.wait_ge(ones_made, 2)
            for b in range(BATCHES):
                k = b % 2
                act.wait_ge(k_product, b + 1)
                wait(act, rest_ready, b - 1)
                act.activation(keys[k][:, 0:401], ps[:, 0:401], ACT.Identity, bias=bk[:, 0:1])
                act.activation(keys[k][:, 401:KEYS].rearrange("p (a n) -> p a n", n=400),
                               ps[:, BANK:4 * BANK].rearrange("p (a n) -> p a n", n=BANK)[:, :, 0:400], ACT.Identity,
                               bias=bk[:, 0:1]).then_inc(k_ready, 1)
                act.wait_ge(v_product, b + 1)
                wait(act, v_stored[k], 16 * (b // 2))
                act.activation(values[k][:, 0:whole, :, 0:dh],
                               ps[:, V:V + whole * P].rearrange("p (t h e) -> p t h e", h=HEADS, e=dh), ACT.Copy)
                act.activation(values[k][0:TAIL, whole, :, 0:dh],
                               ps[0:TAIL, V + whole * P:V + KT * P].rearrange("p (h e) -> p h e", e=dh), ACT.Copy)\
                    .then_inc(v_ready, 1)

        @block.tensor
        def _(pe):
            pe.wait_ge(loaded, 3 * 16)
            for b in range(BATCHES):
                wait(pe, k_ready, b)
                for i, (c, w) in enumerate(SPLIT):
                    last = pe.matmul(ps[:, i * BANK:i * BANK + w], wk[:, :], g.ctxT[:, b, c:c + w], start=True, stop=True)
                last.then_inc(k_product, 1)
                wait(pe, v_ready, b)
                for t in range(KT):
                    rows = P if t < whole else TAIL
                    last = pe.matmul(ps[0:rows, V + t * P:V + (t + 1) * P], g.ctxT[:, b, t * P:t * P + rows], wv[:, :],
                                     start=True, stop=True)
                last.then_inc(v_product, 1)


def narrow_heads(nc, g, name, qd, kd, vd, heads_out, dh):
    with ExitStack() as ctx:
        s = Stage(nc, ctx, g.sems, name + "_heads")
        kstack = [s.sb(f"kstack{j}", [P, 2, KEYS], BF16) for j in range(QUADS)]
        qstack = [s.sb(f"qstack{j}", [P, 2, PAIR], BF16) for j in range(QUADS)]
        values = [s.sb(f"values{j}", [P, KT, 4, dh + 1]) for j in range(QUADS)]
        probsT = [s.sb(f"probsT{i}", [P, 2, PAIR]) for i in range(PROBS_RING)]
        peaks = [s.sb(f"peaks{i}", [P, 4, 2]) for i in range(2)]
        peak = s.sb("peak", [P, 4])
        rest = s.sb("rest", [P, 4])
        lows = [s.sb(f"lows{i}", [P, 2, P], BF16) for i in range(2)]
        mixed = s.sb("mixed", [P, 2 * P])
        zeros = s.sb("zeros", [P, 2, PAIR], BF16)
        inverse = s.sb("inverse", [P, 2, 4])
        cleared = s.sem("cleared")
        loaded = [s.sem(f"loaded{j}") for j in range(QUADS)]
        chunk_ready, chunk_taken = s.sem("chunk_ready"), s.sem("chunk_taken")
        lows_ready, rows_product = s.sem("lows_ready"), s.sem("rows_product")
        upper_copied, lower_copied = s.sem("upper_copied"), s.sem("lower_copied")
        score_ready, exp_done, tile_mixed = s.sem("score_ready"), s.sem("exp_done"), s.sem("tile_mixed")
        mix_copied, mix_turned, mix_divided = s.sem("mix_copied"), s.sem("mix_turned"), s.sem("mix_divided")
        max_step, inverse_ready = s.sem("max_step"), s.sem("inverse_ready")
        bank_cleared = s.sem("bank_cleared")
        ps = g.ps
        half = [ps[:, 2 * i * BANK:(2 * i + 2) * BANK].rearrange("p (a n) -> p a n", n=BANK) for i in range(2)]
        score = [ps[:, (4 + i) * BANK:(5 + i) * BANK] for i in range(SCORE_RING)]
        mix = ps[:, 7 * BANK:7 * BANK + 2 * P]
        side = ps[:, 6 * BANK:6 * BANK + 2 * P]
        LOADS = 2 + 2 * 2 * 3 * 2 + 1
        QN = BATCHES * QUADS
        STEPS = 2 * KT
        out_f = heads_out[:, :, :].rearrange("p t c -> p (t c)")
        kf = kd.rearrange("i b r n -> i (b r) n")
        vf = vd.rearrange("b p (t h e) -> (b p) t (h e)", t=KT, h=HEADS)
        block = ctx.enter_context(nc.Block())

        def walk(eng, stream):
            for j in range(QUADS):
                stream(0, j)
            with eng.Fori(1, BATCHES - 1) as b:
                for j in range(QUADS):
                    stream(b, j)
            for j in range(QUADS):
                stream(BATCHES - 1, j)

        def is_last(b, j, ahead):
            return isinstance(b, int) and b * QUADS + j + ahead >= QN

        def clear(eng, js):
            for j in js:
                eng.memset(qstack[j][:, :, :], 0.0).then_inc(cleared, 1)
                eng.memset(kstack[j][:, :, :], 1.0).then_inc(cleared, 1)

        @block.gpsimd
        def _(pool):
            pool.memset(zeros[:, :, :], 0.0).then_inc(cleared, 1)
            for i in range(2):
                pool.memset(lows[i][:, :, :], 0.0).then_inc(cleared, 1)
            clear(pool, (2,))

        @block.sync
        def _(sp):
            sp.wait_ge(cleared, 2 * QUADS + 3)

            def stream(b, j):
                n = b * QUADS + j
                if not (isinstance(b, int) and b == 0):
                    sp.wait_ge(tile_mixed, (n - QUADS + 1) * KT)
                for i in range(2):
                    sp.dma_start(qstack[j][64 * i:64 * i + SHIFT_ROWS, :, :], zeros[64 * i:64 * i + SHIFT_ROWS, :, :])\
                        .then_inc(loaded[j], 16)
                for r in range(2):
                    for i in range(2):
                        h = 4 * j + 2 * r + i
                        row = 64 * i + SHIFT_ROWS
                        for part, copies in ((0, 3), (1, 2), (2, 1)):
                            rows = copies * dh
                            sp.dma_start(kstack[j][row:row + rows, r, :],
                                         kf[part:part + 1, bass.ds(b * P + h * dh, dh), :].to_broadcast([copies, dh, KEYS]))\
                                .then_inc(loaded[j], 16)
                            sp.dma_start(qstack[j][row:row + rows, r, i * 2 * P:(i + 1) * 2 * P],
                                         qd[0:copies, h * dh:(h + 1) * dh, bass.ds(b * (2 * P), 2 * P)])\
                                .then_inc(loaded[j], 16)
                            row += rows
                sp.dma_start(values[j][:, :, :, :].rearrange("p t h e -> p t (h e)"),
                             vf[bass.ds(b * P, P), :, 4 * j * (dh + 1):4 * (j + 1) * (dh + 1)]).then_inc(loaded[j], 16)

            walk(sp, stream)

        @block.tensor
        def _(pe):
            def chunk(m, j, r, c):
                i, q, side_half = c // 4, c // 2 % 2, c % 2
                wait(pe, chunk_taken, m * 8 + c - 1)
                for a in range(2):
                    k0 = (2 * side_half + a) * (WINDOW_KEYS - 1)
                    ins = pe.matmul(half[c % 2][:, a, 0:WINDOW_KEYS], qstack[j][:, r, (2 * i + q) * P:(2 * i + q + 1) * P],
                                    kstack[j][:, r, k0:k0 + WINDOW_KEYS], start=True, stop=True)
                ins.then_inc(chunk_ready, 1)

            def first_loads(b, j):
                pe.wait_ge(loaded[j], (b + 1) * (16 * LOADS))

            def mix_tile(n, j, t):
                if t == 0:
                    wait(pe, mix_copied, n)
                pe.wait_ge(exp_done, n * STEPS + 2 * t + 2)
                rows_ = P if t < KT - 1 else TAIL
                for h in range(4):
                    ins = pe.matmul(mix[32 * h:32 * h + dh + 1, :], values[j][0:rows_, t, h, :],
                                    probsT[(j * KT + t) % PROBS_RING][0:rows_, h // 2, (h % 2) * 2 * P:(h % 2 + 1) * 2 * P],
                                    start=(t == 0), stop=(t == KT - 1), tile_position=(0, 32 * h))
                ins.then_inc(tile_mixed, 1)

            def turn(n):
                pe.wait_ge(mix_copied, n + 1)
                wait(pe, mix_divided, n)
                for q in range(2):
                    ins = pe.transpose(side[:, q * P:(q + 1) * P], mixed[:, q * P:(q + 1) * P], g.ident[:, :])
                ins.then_inc(mix_turned, 1)

            def stream(b, j):
                n = b * QUADS + j
                taken = 0
                for t in range(KT):
                    for r in range(2):
                        i = 2 * t + r
                        if t == 0:
                            pe.wait_ge(upper_copied, n * 2 + r + 1)
                            pe.wait_ge(lower_copied, n * 2 + r + 1)
                        wait(pe, exp_done, n * STEPS + i - SCORE_RING + 1)
                        rows_ = P if t < KT - 1 else TAIL
                        pe.matmul(score[i % SCORE_RING][0:rows_, :], kstack[j][:, r, t * P:t * P + rows_], qstack[j][:, r, :],
                                  start=True, stop=True).then_inc(score_ready, 1)
                        if r == 0 or t in (2, 6, 10):
                            if taken < 8 and not is_last(b, j, 1):
                                chunk(2 * n + 3, (j + 1) % QUADS, 1, taken)
                            if taken >= 8 and not is_last(b, j, 2):
                                if taken == 8:
                                    first_loads(b + (j + 2) // QUADS, (j + 2) % QUADS)
                                chunk(2 * n + 4, (j + 2) % QUADS, 0, taken - 8)
                            taken += 1
                    if t >= LAG:
                        mix_tile(n, j, t - LAG)
                    elif not (isinstance(b, int) and n == 0):
                        mix_tile(n - 1, (j - 1) % QUADS, KT - LAG + t)
                    if t == 2 and not (isinstance(b, int) and n == 0):
                        turn(n - 1)
                    if t == 4 and not is_last(b, j, 1):
                        wait(pe, mix_divided, n)
                        rows_at(2 * n + 2, 0)
                    if t == 9 and not is_last(b, j, 1):
                        pe.wait_ge(upper_copied, 2 * n + 3)
                        pe.wait_ge(lower_copied, 2 * n + 3)
                        rows_at(2 * n + 3, 1)

            def rows_at(m, parity):
                pe.wait_ge(lows_ready, m + 1)
                for q in range(2):
                    ins = pe.matmul(side[:, q * P:(q + 1) * P], lows[parity][:, q, :], g.identb[:, :], start=True, stop=True)
                ins.then_inc(rows_product, 1)

            pe.wait_ge(bank_cleared, 1)
            first_loads(0, 0)
            for c in range(8):
                chunk(0, 0, 0, c)
            for c in range(8):
                chunk(1, 0, 1, c)
            rows_at(0, 0)
            first_loads(0, 1)
            for c in range(8):
                chunk(2, 1, 0, c)
            pe.wait_ge(upper_copied, 1)
            pe.wait_ge(lower_copied, 1)
            rows_at(1, 1)
            walk(pe, stream)
            for t in range(KT - LAG, KT):
                mix_tile(QN - 1, QUADS - 1, t)
            turn(QN - 1)

        @block.scalar
        def _(act):
            def copy_lower(m, j, r):
                act.wait_ge(rows_product, m + 1)
                act.activation(qstack[j][64:64 + SHIFT_ROWS, r, 2 * P:4 * P], side[64:64 + SHIFT_ROWS, :], ACT.Copy)\
                    .then_inc(lower_copied, 1)

            def copy_mix(n):
                act.wait_ge(tile_mixed, (n + 1) * KT)
                wait(act, mix_turned, n)
                act.activation(mixed[:, :], mix, ACT.Copy).then_inc(mix_copied, 1)

            def stream(b, j):
                n = b * QUADS + j
                for t in range(KT):
                    for r in range(2):
                        i = 2 * t + r
                        rows_ = P if t < KT - 1 else TAIL
                        act.wait_ge(score_ready, n * STEPS + i + 1)
                        if r == 0:
                            wait(act, tile_mixed, n * KT + t - PROBS_RING + 1)
                        act.activation(probsT[(j * KT + t) % PROBS_RING][0:rows_, r, :], score[i % SCORE_RING][0:rows_, :], ACT.Exp)\
                            .then_inc(exp_done, 1)
                    if t == 1 and not (isinstance(b, int) and n == 0):
                        copy_mix(n - 1)
                    if t == 5 and not is_last(b, j, 1):
                        copy_lower(2 * n + 2, (j + 1) % QUADS, 0)
                    if t == 10 and not is_last(b, j, 1):
                        copy_lower(2 * n + 3, (j + 1) % QUADS, 1)

            copy_lower(0, 0, 0)
            copy_lower(1, 0, 1)
            walk(act, stream)
            copy_mix(QN - 1)

        @block.vector
        def _(dve):
            clear(dve, (0, 1, 3))
            dve.memset(mix, 0.0).then_inc(bank_cleared, 1)

            def chunk(m, parity, c):
                i, q = c // 4, c // 2 % 2
                dve.wait_ge(chunk_ready, m * 8 + c + 1)
                dve.tensor_reduce(peaks[parity][:, 2 * q + i, c % 2:c % 2 + 1], half[c % 2][:, :, 0:WINDOW_KEYS], AX.XY,
                                  ALU.max).then_inc(chunk_taken, 1)

            def maxima(m, parity):
                dve.wait_ge(chunk_taken, m * 8 + 8)
                wait(dve, rows_product, m - 1)
                low = lows[parity]
                pk = peak[:, :].rearrange("p (q i) -> p q i", i=2)
                rs = rest[:, :].rearrange("p (q i) -> p q i", i=2)

                def part(i):
                    return low[:, :, i:P:64]

                dve.tensor_tensor(peak[:, :], peaks[parity][:, :, 0], peaks[parity][:, :, 1], ALU.max).then_inc(max_step, 1)
                dve.wait_ge(max_step, m * 4 + 1)
                dve.tensor_scalar(part(0), pk, -1.0, None, ALU.mult).then_inc(max_step, 1)
                dve.wait_ge(max_step, m * 4 + 2)
                dve.scalar_tensor_tensor(out=rs, in0=pk, scalar=-1.0, in1=part(0), op0=ALU.mult, op1=ALU.subtract)\
                    .then_inc(max_step, 1)
                dve.wait_ge(max_step, m * 4 + 3)
                dve.tensor_copy(part(1), rs).then_inc(max_step, 1)
                dve.wait_ge(max_step, m * 4 + 4)
                dve.tensor_tensor(part(2), rs, part(1), ALU.subtract).then_inc(lows_ready, 1)

            def copy_upper(m, j, r):
                dve.wait_ge(rows_product, m + 1)
                dve.tensor_copy(qstack[j][0:SHIFT_ROWS, r, 0:2 * P], side[0:SHIFT_ROWS, :]).then_inc(upper_copied, 1)

            def divide(n, b, j):
                dve.wait_ge(mix_turned, n + 1)
                turned = side.rearrange("p (q h e) -> p q h e", q=2, h=4)
                dve.reciprocal(inverse[:, :, :], turned[:, :, :, dh]).then_inc(inverse_ready, 1)
                dve.wait_ge(inverse_ready, n + 1)
                for q in range(2):
                    ins = dve.tensor_tensor(
                        out_f[:, bass.ds((b * 2 + q) * P + 4 * j * dh, 4 * dh)].rearrange("p (h e) -> p h e", e=dh),
                        turned[:, q, :, 0:dh], inverse[:, q, :].unsqueeze(2).to_broadcast([P, 4, dh]), ALU.mult)
                ins.then_inc(mix_divided, 1)

            def stream(b, j):
                n = b * QUADS + j
                for c in range(CHUNKS):
                    if c < 8 and not is_last(b, j, 1):
                        chunk(2 * n + 3, 1, c)
                    if c >= 8 and not is_last(b, j, 2):
                        chunk(2 * n + 4, 0, c - 8)
                    if c == 4 and not (isinstance(b, int) and n == 0):
                        divide(n - 1, b if j else b - 1, (j - 1) % QUADS)
                    if c == 8 and not is_last(b, j, 1):
                        copy_upper(2 * n + 2, (j + 1) % QUADS, 0)
                    if c == 7 and not is_last(b, j, 1):
                        maxima(2 * n + 3, 1)
                    if c == 13 and not is_last(b, j, 1):
                        copy_upper(2 * n + 3, (j + 1) % QUADS, 1)
                    if c == 15 and not is_last(b, j, 2):
                        maxima(2 * n + 4, 0)

            for c in range(8):
                chunk(0, 0, c)
            maxima(0, 0)
            for c in range(8):
                chunk(1, 1, c)
            copy_upper(0, 0, 0)
            maxima(1, 1)
            for c in range(8):
                chunk(2, 0, c)
            copy_upper(1, 0, 1)
            maxima(2, 0)
            walk(dve, stream)
            divide(QN - 1, BATCHES - 1, QUADS - 1)


def reshuffled_output(nc, g, name, heads_out, wo, bv, dh):
    shuffle = nc.dram_tensor(name + "_shuffle", (BATCHES, HEADS, 2, P, dh), F32, kind="Internal").ap()
    with ExitStack() as ctx:
        s = Stage(nc, ctx, g.sems, name + "_out")
        rows = s.sb("rows", [P, TILES, P])
        rowsT = s.sb("rowsT", [P, TILES * P])
        wo_sb = s.sb("wo", [P, P])
        bv_rows = s.sb("bv_rows", [P, P])
        biased = s.sem("biased")
        spread, gathered, w_loaded = s.sem("spread"), s.sem("gathered"), s.sem("w_loaded")
        rows_transposed, rowsT_ready, product_done = s.sem("rows_transposed"), s.sem("rowsT_ready"), s.sem("product_done")
        block = ctx.enter_context(nc.Block())

        @block.sync
        def _(sp):
            sp.dma_start(bv_rows[:, :], bv.partition_broadcast(P)).then_inc(w_loaded, 16)
            sp.dma_start(wo_sb[:, :], wo).then_inc(w_loaded, 16)
            sp.wait_ge(biased, 1)
            for b in range(BATCHES):
                for q in range(2):
                    sp.dma_start(shuffle[b, :, q].rearrange("h p e -> p h e"),
                                 heads_out[:, 2 * b + q, :].rearrange("p (h e) -> p h e", e=dh)).then_inc(spread, 16)
            sp.wait_ge(spread, 16 * TILES)
            sp.dma_start(rows[:, :, :], shuffle.rearrange("b h q p e -> (b h q p e)").rearrange("(t p c) -> p t c", p=P, c=P))\
                .then_inc(gathered, 16)

        @block.tensor
        def _(pe):
            pe.wait_ge(gathered, 16)
            transpose_tokens(g, pe, rows, 0, rows_transposed)
            pe.wait_ge(rowsT_ready, 1)
            pe.wait_ge(w_loaded, 32)
            for t in range(TILES):
                last = pe.matmul(g.ps[:, (TILES + t) * P:(TILES + t + 1) * P], rowsT[:, t * P:(t + 1) * P], wo_sb[:, :],
                                 start=True, stop=True)
            last.then_inc(product_done, 1)

        @block.scalar
        def _(act):
            act.wait_ge(rows_transposed, 1)
            act.activation(rowsT[:, :], g.ps[:, 0:TILES * P], ACT.Copy).then_inc(rowsT_ready, 1)

        @block.vector
        def _(dve):
            dve.wait_ge(w_loaded, 32)
            dve.tensor_tensor(heads_out[:, :, :], heads_out[:, :, :],
                              bv_rows[:, :].unsqueeze(1).to_broadcast([P, TILES, P]), ALU.add).then_inc(biased, 1)
            dve.wait_ge(product_done, 1)
            dve.tensor_tensor(g.x[:, :, :], g.x[:, :, :],
                              g.ps[:, TILES * P:2 * TILES * P].rearrange("p (t c) -> p t c", c=P), ALU.add)


SLOTS = 8
SPAN = 3 * P


def slot_scores(pe, g, mask, i, q_tile, k_tiles):
    c = i * BANK
    pe.matmul(g.ps[:, c:c + SPAN], g.identb[:, :], mask[:, :], start=True, stop=False, skip_group_check=True)
    pe.matmul(g.ps[:, c:c + P], q_tile(0), k_tiles(1), start=False, stop=False, skip_group_check=True)
    return pe.matmul(g.ps[:, c + P:c + SPAN], q_tile(1), k_tiles(2), start=False, stop=True, skip_group_check=True)


def slot_peaks(dve, g, half, peaks):
    banks = g.ps[:, half * 4 * BANK:(half + 1) * 4 * BANK].rearrange("p (i n) -> p i n", n=BANK)
    s = slice(4 * half, 4 * half + 4)
    dve.tensor_reduce(peaks[:, 0, s], banks[:, :, 0:P], AX.X, ALU.max, negate=True)
    return dve.tensor_reduce(peaks[:, 1, s], banks[:, :, P:SPAN], AX.X, ALU.max, negate=True)


def slot_exps(act, g, i, probs, peaks, sums, scale):
    c = i * BANK
    act.activation(probs[:, i, 0:P], g.ps[:, c:c + P], ACT.Exp, bias=peaks[:, 0, i:i + 1], scale=scale(0),
                   accum_out=sums[:, 0, i:i + 1])
    return act.activation(probs[:, i, P:SPAN], g.ps[:, c + P:c + SPAN], ACT.Exp, bias=peaks[:, 1, i:i + 1],
                          scale=scale(1), accum_out=sums[:, 1, i:i + 1])


def slot_normalize(dve, half, probs, inverse):
    s = slice(4 * half, 4 * half + 4)
    dve.tensor_tensor(probs[:, s, 0:P], probs[:, s, 0:P], inverse[:, 0, s].unsqueeze(2).to_broadcast([P, 4, P]),
                      ALU.mult)
    return dve.tensor_tensor(probs[:, s, P:SPAN], probs[:, s, P:SPAN],
                             inverse[:, 1, s].unsqueeze(2).to_broadcast([P, 4, 2 * P]), ALU.mult)


def slot_transposes(pe, g, i, probs):
    c = (6 + i % 2) * BANK
    for j in range(3):
        ins = pe.transpose(g.ps[:, c + j * P:c + (j + 1) * P], probs[:, i, j * P:(j + 1) * P], g.ident[:, :])
    return ins


def slot_mix(pe, out, value, i, probsT, **tile):
    pe.matmul(out, value(0), probsT[:, i, 0:2 * P], start=True, stop=False, skip_group_check=True, **tile)
    return pe.matmul(out[:, P:2 * P], value(1), probsT[:, i, 2 * P:SPAN], start=False, stop=True,
                     skip_group_check=True, **tile)


LHEADS = 8
LDIM = 64
INNER = LHEADS * LDIM
SEQ = 2 * P
TOKENS = BATCHES * SEQ


def local_stage(nc, g, d):
    with ExitStack() as ctx:
        s = Stage(nc, ctx, g.sems, "local")
        yT = s.sb("yT", [P, TOKENS])
        norm_to_channels(nc, g, "local_norm", yT)
        for layer in range(2):
            local_attention(nc, g, d, yT, layer)
            local_mlp(nc, g, d, yT, layer)
        channels_to_x(nc, g, "local_end", yT)


def norm_to_channels(nc, g, name, dst):
    with ExitStack() as ctx:
        s = Stage(nc, ctx, g.sems, name)
        hn = s.sb("hn", [P, TILES, P])
        sq = s.sb("sq", [P, TILES, P])
        st = s.sb("st", [P, 3, TILES])
        var_ready, std_ready = s.sem("var_ready"), s.sem("std_ready")
        hn_ready, transposed, order_sem = s.sem("hn_ready"), s.sem("transposed"), s.sem("dve_order")
        block = ctx.enter_context(nc.Block())

        @block.vector
        def _(dve):
            order = Order(dve, order_sem)
            norm_vector(dve, order, g.x[:, :, :], hn[:, :, :], sq[:, :, :], st, var_ready, std_ready, 1)
            dve.sem_inc(hn_ready, 1)

        @block.scalar
        def _(act):
            norm_scalar(act, st, var_ready, std_ready, 1)
            act.wait_ge(transposed, 1)
            act.activation(dst[:, :], g.ps[:, 0:TOKENS], ACT.Copy)

        @block.tensor
        def _(pe):
            pe.wait_ge(hn_ready, 1)
            transpose_tokens(g, pe, hn, 0, transposed)


def channels_to_x(nc, g, name, src):
    with ExitStack() as ctx:
        s = Stage(nc, ctx, g.sems, name)
        transposed = s.sem("transposed")
        block = ctx.enter_context(nc.Block())

        @block.tensor
        def _(pe):
            for t in range(TILES):
                last = pe.transpose(g.ps[:, t * P:(t + 1) * P], src[:, t * P:(t + 1) * P], g.ident[:, :])
            last.then_inc(transposed, 1)

        @block.vector
        def _(dve):
            dve.wait_ge(transposed, 1)
            dve.tensor_tensor(g.x[:, :, :], g.x[:, :, :], g.ps[:, 0:TOKENS].rearrange("p (t c) -> p t c", c=P), ALU.add)


def local_attention(nc, g, d, yT, layer):
    with ExitStack() as ctx:
        s = Stage(nc, ctx, g.sems, f"local{layer}")
        wqkv = s.sb("wqkv", [P, 3 * INNER])
        wo = s.sb("wo", [P, INNER // P, P])
        rotary = s.sb("rotary", [P, 4, 2, LDIM])
        turned = s.sb("turned", [P, 4, 2, LDIM])
        scales = s.sb("scales", [P, 2, LDIM])
        shifted = s.sb("shifted", [P, SEQ])
        qk = s.sb("qk", [P, 4, LHEADS, LDIM])
        value = s.sb("value", [P, 2, INNER])
        squares = s.sb("squares", [P, 4, LHEADS, LDIM])
        norm = s.sb("norm", [P, 4, LHEADS])
        rnorm = s.sb("rnorm", [P, 4, LHEADS])
        q_gain = s.sb("q_gain", [P, 2, LHEADS])
        part = s.sb("part", [P, 4, LHEADS, LDIM])
        turn = s.sb("turn", [P, 4, LHEADS, LDIM])
        qT = s.sb("qT", [P, 4, SEQ])
        kT = s.sb("kT", [P, 4, SEQ])
        peaks = s.sb("peaks", [P, 2, SLOTS])
        shifts = s.sb("shifts", [P, 2, SLOTS])
        sums = s.sb("sums", [P, 2, SLOTS])
        inverse = s.sb("inverse", [P, 2, SLOTS])
        probs = s.sb("probs", [P, SLOTS, SPAN])
        probsT = s.sb("probsT", [P, SLOTS, SPAN])
        oT = s.sb("oT", [P, 4, SEQ])
        names = ("loaded edge_zeroed turned_ready shifted_ready qk_product v_product qk_ready squares_ready "
                 "squared_sums norm_ready gain_ready q_turned k_turned q_transposed k_transposed qT_ready kT_ready "
                 "v_ready scores_ready peaks_ready shifts_ready exp_done normalized mixed o_ready out_product "
                 "out_added dve_order k_part pool_order rnorm_ready q_part inverse_ready").split()
        m = {n: s.sem(n) for n in names}
        transposed = [s.sem(f"transposed{i}") for i in range(2)]
        probsT_copied = [s.sem(f"probsT_copied{i}") for i in range(2)]
        ps = g.ps
        block = ctx.enter_context(nc.Block())
        LOADS = 3 + 4

        @block.sync
        def _(sp):
            sp.dma_start(wqkv[:, :], d["L0_ffn_wqkv"][layer]).then_inc(m["loaded"], 16)
            sp.dma_start(wo[:, :, :], d["L0_ffn_wo"][layer].rearrange("(j p) c -> p j c", p=P)).then_inc(m["loaded"], 16)
            for i in range(4):
                sp.dma_start(rotary[:, i, :, :], d["rotary"][i].rearrange("(t p) e -> p t e", p=P)).then_inc(m["loaded"], 16)
            sp.dma_start(scales[:, 0, :], d["L0_ffn_q_scale"][layer].partition_broadcast(P)).then_inc(m["loaded"], 16)
            sp.dma_start(scales[:, 1, :], d["L0_ffn_k_scale"][layer].partition_broadcast(P)).then_inc(m["loaded"], 16)

        def walk(eng, front, attend):
            front(0)
            with eng.Fori(0, BATCHES - 1) as b:
                attend(b, True)
            attend(BATCHES - 1, False)

        @block.gpsimd
        def _(pool):
            order = Order(pool, m["pool_order"])
            order.done(pool.memset(shifted[64:P, 0:1], 0.0))
            pool.sem_inc(m["edge_zeroed"], 1)
            pool.wait_ge(m["loaded"], 16 * (LOADS + 1))
            half = LDIM // 2
            for i in range(2):
                full = scales[:, i, :].unsqueeze(1).to_broadcast([P, 2, LDIM])
                order.done(pool.tensor_tensor(turned[:, 2 * i], rotary[:, 2 * i], full, ALU.mult))
                for a, b in ((0, half), (half, 0)):
                    order.done(pool.tensor_tensor(turned[:, 2 * i + 1, :, a:a + half],
                                                  rotary[:, 2 * i + 1, :, a:a + half],
                                                  scales[:, i, b:b + half].unsqueeze(1).to_broadcast([P, 2, half]),
                                                  ALU.mult))
            pool.sem_inc(m["turned_ready"], 1)

            def front(b):
                pool.wait_ge(m["qk_ready"], b + 1)
                wait(pool, m["k_transposed"], b)
                k, t = qk[:, 2:4], turned[:, 2].unsqueeze(2)
                pool.tensor_tensor(turn[:, 2:4], k, t.to_broadcast([P, 2, LHEADS, LDIM]), ALU.mult)
                for a, c in ((0, half), (half, 0)):
                    ins = pool.tensor_tensor(part[:, 2:4, :, a:a + half], k[:, :, :, c:c + half],
                                             turned[:, 3, :, a:a + half].unsqueeze(2)
                                             .to_broadcast([P, 2, LHEADS, half]), ALU.mult)
                ins.then_inc(m["k_part"], 1)
                pool.wait_ge(m["k_part"], b * 2 + 1)
                pool.tensor_tensor(turn[:, 2:4], turn[:, 2:4], part[:, 2:4], ALU.add).then_inc(m["k_part"], 1)
                pool.wait_ge(m["k_part"], b * 2 + 2)
                pool.wait_ge(m["rnorm_ready"], b + 1)
                pool.tensor_tensor(turn[:, 2:4], turn[:, 2:4],
                                   rnorm[:, 2:4, :].unsqueeze(3).to_broadcast([P, 2, LHEADS, LDIM]), ALU.mult)\
                    .then_inc(m["k_turned"], 1)

            front(0)
            with pool.Fori(1, BATCHES) as b:
                front(b)

        @block.vector
        def _(dve):
            half = LDIM // 2
            dve.wait_ge(m["turned_ready"], 1)

            def front_norm(b):
                dve.wait_ge(m["squares_ready"], b + 1)
                dve.tensor_reduce(norm[:, :, :], squares[:, :, :, :], AX.X, ALU.add).then_inc(m["squared_sums"], 1)

            def front_turn(b):
                dve.wait_ge(m["qk_ready"], b + 1)
                wait(dve, m["q_transposed"], b)
                q = qk[:, 0:2]
                dve.tensor_tensor(turn[:, 0:2], q, turned[:, 0].unsqueeze(2).to_broadcast([P, 2, LHEADS, LDIM]),
                                  ALU.mult)
                for a, c in ((0, half), (half, 0)):
                    ins = dve.tensor_tensor(part[:, 0:2, :, a:a + half], q[:, :, :, c:c + half],
                                            turned[:, 1, :, a:a + half].unsqueeze(2)
                                            .to_broadcast([P, 2, LHEADS, half]), ALU.mult)
                ins.then_inc(m["q_part"], 1)
                dve.wait_ge(m["q_part"], b + 1)
                dve.tensor_tensor(turn[:, 0:2], turn[:, 0:2], part[:, 0:2], ALU.add).then_inc(m["q_turned"], 1)
                dve.wait_ge(m["norm_ready"], b + 1)
                dve.tensor_scalar(norm[:, :, :], norm[:, :, :], 1e-12, None, ALU.max).then_inc(m["dve_order"], 1)
                dve.wait_ge(m["dve_order"], b * 2 + 1)
                dve.reciprocal(rnorm[:, :, :], norm[:, :, :]).then_inc(m["rnorm_ready"], 1)
                dve.wait_ge(m["rnorm_ready"], b + 1)
                dve.tensor_scalar(q_gain[:, :, :], rnorm[:, 0:2, :], 8.0, None, ALU.mult).then_inc(m["dve_order"], 1)
                dve.wait_ge(m["dve_order"], b * 2 + 2)

            def front_keys(b):
                dve.wait_ge(m["k_transposed"], b + 1)
                dve.tensor_copy(kT[:, :, :], ps[:, 2 * BANK:4 * BANK].rearrange("p (j n) -> p j n", n=SEQ))\
                    .then_inc(m["kT_ready"], 1)

            def attend(b, more):
                for half_ in range(2):
                    dve.wait_ge(m["scores_ready"], b * 2 + half_ + 1)
                    slot_peaks(dve, g, half_, peaks).then_inc(m["peaks_ready"], 1)
                dve.wait_ge(m["peaks_ready"], b * 2 + 2)
                dve.tensor_tensor(shifts[:, :, :], peaks[:, :, :], q_gain[:, :, :], ALU.mult)\
                    .then_inc(m["shifts_ready"], 1)
                for half_ in range(2):
                    dve.wait_ge(m["exp_done"], b * 2 + half_ + 1)
                    h = slice(4 * half_, 4 * half_ + 4)
                    dve.reciprocal(inverse[:, :, h], sums[:, :, h]).then_inc(m["inverse_ready"], 1)
                    dve.wait_ge(m["inverse_ready"], b * 2 + half_ + 1)
                    slot_normalize(dve, half_, probs, inverse).then_inc(m["normalized"], 1)
                if more:
                    front_norm(b + 1)
                for i in range(1, SLOTS, 2):
                    dve.wait_ge(transposed[1], b * 4 + i // 2 + 1)
                    dve.tensor_copy(probsT[:, i, :], ps[:, 7 * BANK:7 * BANK + SPAN]).then_inc(probsT_copied[1], 1)
                if more:
                    front_turn(b + 1)
                dve.wait_ge(m["out_product"], b + 1)
                cols = yT[:, bass.ds(b * SEQ, SEQ)]
                dve.tensor_tensor(cols, cols, ps[:, 2 * BANK:2 * BANK + SEQ], ALU.add).then_inc(m["out_added"], 1)
                if more:
                    front_keys(b + 1)

            def front(b):
                front_norm(b)
                front_turn(b)
                front_keys(b)

            walk(dve, front, attend)

        @block.scalar
        def _(act):
            def front_shift(b):
                wait(act, m["v_product"], b)
                act.activation(shifted[0:64, :], yT[0:64, bass.ds(b * SEQ, SEQ)], ACT.Copy)
                act.activation(shifted[64:P, 1:SEQ], yT[64:P, bass.ds(b * SEQ, SEQ - 1)], ACT.Copy)\
                    .then_inc(m["shifted_ready"], 1)

            def front_take(b):
                act.wait_ge(m["qk_product"], b + 1)
                wait(act, m["k_turned"], b)
                wait(act, m["q_turned"], b)
                act.activation(qk[:, :, :, :].rearrange("p i h e -> p (i h e)"), ps[:, 0:4 * BANK], ACT.Copy)\
                    .then_inc(m["qk_ready"], 1)
                act.wait_ge(m["qk_ready"], b + 1)
                act.activation(squares[:, :, :, :], qk[:, :, :, :], ACT.Square).then_inc(m["squares_ready"], 1)

            def front_sqrt(b):
                act.wait_ge(m["squared_sums"], b + 1)
                act.activation(norm[:, :, :], norm[:, :, :], ACT.Sqrt).then_inc(m["norm_ready"], 1)

            def front_value(b):
                act.wait_ge(m["v_product"], b + 1)
                wait(act, m["mixed"], b)
                act.activation(value[:, :, :].rearrange("p t n -> p (t n)"), ps[:, 4 * BANK:6 * BANK], ACT.Copy)\
                    .then_inc(m["v_ready"], 1)

            def front_queries(b):
                act.wait_ge(m["q_transposed"], b + 1)
                act.activation(qT[:, :, :].rearrange("p j n -> p (j n)"), ps[:, 0:2 * BANK], ACT.Copy)\
                    .then_inc(m["qT_ready"], 1)

            def attend(b, more):
                if more:
                    front_shift(b + 1)
                act.wait_ge(m["shifts_ready"], b + 1)
                for i in range(SLOTS):
                    ins = slot_exps(act, g, i, probs, shifts, sums, lambda t: q_gain[:, t, i:i + 1])
                    if i % 4 == 3:
                        ins.then_inc(m["exp_done"], 1)
                if more:
                    front_take(b + 1)
                for i in range(0, SLOTS, 2):
                    act.wait_ge(transposed[0], b * 4 + i // 2 + 1)
                    act.activation(probsT[:, i, :], ps[:, 6 * BANK:6 * BANK + SPAN], ACT.Copy)\
                        .then_inc(probsT_copied[0], 1)
                if more:
                    front_sqrt(b + 1)
                act.wait_ge(m["mixed"], b + 1)
                act.activation(oT[:, :, :].rearrange("p j n -> p (j n)"), ps[:, 0:2 * BANK], ACT.Copy)\
                    .then_inc(m["o_ready"], 1)
                if more:
                    front_value(b + 1)
                    front_queries(b + 1)

            def front(b):
                front_shift(b)
                front_take(b)
                front_sqrt(b)
                front_value(b)
                front_queries(b)

            walk(act, front, attend)

        @block.tensor
        def _(pe):
            pe.wait_ge(m["loaded"], 16 * (LOADS + 1))
            pe.wait_ge(m["edge_zeroed"], 1)

            def front_project(b):
                pe.wait_ge(m["shifted_ready"], b + 1)
                wait(pe, m["exp_done"], b * 2)
                for i in range(6):
                    j, t = i // 2, i % 2
                    ins = pe.matmul(ps[:, i * BANK:(i + 1) * BANK], shifted[:, t * P:(t + 1) * P],
                                    wqkv[:, j * INNER:(j + 1) * INNER], start=True, stop=True)
                    if i == 3:
                        ins.then_inc(m["qk_product"], 1)
                ins.then_inc(m["v_product"], 1)

            def front_transposes(b):
                wait(pe, m["o_ready"], b)
                wait(pe, m["out_added"], b)
                for i, name in ((0, "q"), (1, "k")):
                    pe.wait_ge(m[name + "_turned"], b + 1)
                    if i == 0:
                        pe.wait_ge(m["qk_ready"], b + 1)
                    for j in range(4):
                        for t in range(2):
                            c = 2 * i * BANK + j * SEQ + t * P
                            ins = pe.transpose(ps[:, c:c + P],
                                               turn[:, 2 * i + t, 2 * j:2 * j + 2, :].rearrange("p h e -> p (h e)"),
                                               g.ident[:, :])
                    ins.then_inc(m[name + "_transposed"], 1)

            def attend(b, more):
                pe.wait_ge(m["qT_ready"], b + 1)
                pe.wait_ge(m["kT_ready"], b + 1)
                pe.wait_ge(m["v_ready"], b + 1)
                wait(pe, probsT_copied[0], b * 4)
                wait(pe, probsT_copied[1], b * 4)
                for i in range(SLOTS):
                    j, rows = i // 2, slice(64 * (i % 2), 64 * (i % 2) + 64)
                    ins = slot_scores(pe, g, g.band, i, lambda t: qT[rows, j, t * P:(t + 1) * P],
                                      lambda n: kT[rows, j, 0:n * P])
                    if i % 4 == 3:
                        ins.then_inc(m["scores_ready"], 1)
                if more:
                    front_project(b + 1)
                else:
                    pe.wait_ge(m["exp_done"], b * 2 + 2)
                for i in range(SLOTS):
                    if i % 4 == 0:
                        pe.wait_ge(m["normalized"], b * 2 + i // 4 + 1)
                    if i >= 2:
                        pe.wait_ge(probsT_copied[i % 2], b * 4 + i // 2)
                    slot_transposes(pe, g, i, probs).then_inc(transposed[i % 2], 1)
                if more:
                    pe.wait_ge(m["qk_ready"], b + 2)
                for i in range(SLOTS):
                    if i % 2 == 0:
                        for side in range(2):
                            pe.wait_ge(probsT_copied[side], b * 4 + i // 2 + 1)
                    j, r = i // 2, i % 2
                    ins = slot_mix(pe, ps[64 * r:64 * r + 64, j * SEQ:(j + 1) * SEQ],
                                   lambda kt: value[:, kt, i * LDIM:(i + 1) * LDIM], i, probsT)
                ins.then_inc(m["mixed"], 1)
                pe.wait_ge(m["o_ready"], b + 1)
                for j in range(4):
                    ins = pe.matmul(ps[:, 2 * BANK:2 * BANK + SEQ], wo[:, j, :], oT[:, j, :], start=(j == 0),
                                    stop=(j == 3))
                ins.then_inc(m["out_product"], 1)
                if more:
                    front_transposes(b + 1)

            def front(b):
                front_project(b)
                front_transposes(b)

            walk(pe, front, attend)


def local_mlp(nc, g, d, yT, layer):
    hid = d["L0_ffn_w2"].shape[1]
    chunks = [(c, min(P, hid - c)) for c in range(0, hid, P)]
    with ExitStack() as ctx:
        s = Stage(nc, ctx, g.sems, f"mlp{layer}")
        w1 = s.sb("w1", [P, 2 * hid])
        w2 = s.sb("w2", [P, len(chunks), P])
        b1 = s.sb("b1", [P, 2, len(chunks)])
        cols = s.sb("cols", [P, 3])
        gain, offset, b2 = (cols[:, i:i + 1] for i in range(3))
        mean_of = s.sb("mean_of", [P, P])
        h = s.sb("h", [P, TOKENS])
        sq = s.sb("sq", [P, TOKENS])
        gate = s.sb("gate", [P, 2, TOKENS])
        hidden = s.sb("hidden", [P, len(chunks), TOKENS])
        names = ("loaded constants shifted_ready mean_product centred squared var_product var_ready std_ready h_ready "
                 "gate_product gate_ready a_product hidden_ready out_product dve_order pool_order scaled").split()
        m = {n: s.sem(n) for n in names}
        ps = g.ps
        lo, hi = ps[:, 0:TOKENS], ps[:, TOKENS:2 * TOKENS]
        loads = 1 + len(chunks) * 3 + 3
        block = ctx.enter_context(nc.Block())

        @block.sync
        def _(sp):
            sp.dma_start(w1[:, :], d["L0_ffn_w1"][layer]).then_inc(m["loaded"], 16)
            for j, (c, n) in enumerate(chunks):
                sp.dma_start(w2[0:n, j, :], d["L0_ffn_w2"][layer][c:c + n, :]).then_inc(m["loaded"], 16)
                for k in range(2):
                    sp.dma_start(b1[0:n, k, j:j + 1], column(d["L0_ffn_b1"][layer][k * hid + c:k * hid + c + n]))\
                        .then_inc(m["loaded"], 16)
            for c, name in ((gain, "ln_g"), (offset, "ln_b"), (b2, "b2")):
                sp.dma_start(c, column(d["L0_ffn_" + name][layer])).then_inc(m["loaded"], 16)

        @block.gpsimd
        def _(pool):
            order = Order(pool, m["pool_order"])
            order.done(pool.memset(mean_of[:, :], 1.0 / P))
            pool.sem_inc(m["constants"], 1)
            h3, y3 = (a.rearrange("p (b l) -> p b l", l=SEQ) for a in (h[:, :], yT[:, :]))
            order.done(pool.memset(h3[64:P, :, 0:1], 0.0))
            pool.tensor_copy(h3[64:P, :, 1:SEQ], y3[64:P, :, 0:SEQ - 1]).then_inc(m["shifted_ready"], 1)

        @block.vector
        def _(dve):
            order = Order(dve, m["dve_order"])
            dve.tensor_copy(h[0:64, :], yT[0:64, :]).then_inc(m["shifted_ready"], 1)
            dve.wait_ge(m["mean_product"], 1)
            dve.tensor_tensor(h[:, :], h[:, :], lo, ALU.subtract).then_inc(m["centred"], 1)
            dve.wait_ge(m["var_product"], 1)
            dve.tensor_scalar(sq[:, :], hi, EPS, None, ALU.add).then_inc(m["var_ready"], 1)
            dve.wait_ge(m["std_ready"], 1)
            order.done(dve.reciprocal(sq[:, :], sq[:, :]))
            dve.tensor_tensor(h[:, :], h[:, :], sq[:, :], ALU.mult).then_inc(m["scaled"], 1)
            for j, (c, n) in enumerate(chunks):
                dve.wait_ge(m["gate_ready"], j + 1)
                dve.wait_ge(m["a_product"], j + 1)
                dve.scalar_tensor_tensor(out=hidden[0:n, j, :], in0=hi[0:n, :], scalar=b1[0:n, 0, j:j + 1],
                                         in1=gate[0:n, j % 2, :], op0=ALU.add, op1=ALU.mult)\
                    .then_inc(m["hidden_ready"], 1)
            dve.wait_ge(m["out_product"], 1)
            dve.scalar_tensor_tensor(out=yT[:, :], in0=lo, scalar=b2, in1=yT[:, :], op0=ALU.add, op1=ALU.add)

        @block.scalar
        def _(act):
            act.wait_ge(m["centred"], 1)
            act.activation(sq[:, :], h[:, :], ACT.Square).then_inc(m["squared"], 1)
            act.wait_ge(m["var_ready"], 1)
            act.activation(sq[:, :], sq[:, :], ACT.Sqrt).then_inc(m["std_ready"], 1)
            act.wait_ge(m["scaled"], 1)
            act.wait_ge(m["loaded"], 16 * loads)
            act.activation(h[:, :], h[:, :], ACT.Identity, bias=offset, scale=gain).then_inc(m["h_ready"], 1)
            for j, (c, n) in enumerate(chunks):
                act.wait_ge(m["gate_product"], j + 1)
                wait(act, m["hidden_ready"], j - 1)
                act.activation(gate[0:n, j % 2, :], lo[0:n, :], ACT.Gelu, bias=b1[0:n, 1, j:j + 1])\
                    .then_inc(m["gate_ready"], 1)

        @block.tensor
        def _(pe):
            def product(base, lhsT, rhs, rows=P, start=True, stop=True, n=None):
                for k in range(TOKENS // BANK):
                    last = pe.matmul(ps[0:rows, base + k * BANK:base + (k + 1) * BANK], lhsT,
                                     rhs[:, k * BANK:(k + 1) * BANK], start=start, stop=stop)
                return last

            pe.wait_ge(m["constants"], 1)
            pe.wait_ge(m["shifted_ready"], 2)
            product(0, mean_of[:, :], h).then_inc(m["mean_product"], 1)
            pe.wait_ge(m["squared"], 1)
            product(TOKENS, mean_of[:, :], sq).then_inc(m["var_product"], 1)
            pe.wait_ge(m["loaded"], 16 * loads)
            pe.wait_ge(m["h_ready"], 1)
            for j, (c, n) in enumerate(chunks):
                wait(pe, m["gate_ready"], j)
                product(0, w1[:, hid + c:hid + c + n], h, n).then_inc(m["gate_product"], 1)
                wait(pe, m["hidden_ready"], j)
                product(TOKENS, w1[:, c:c + n], h, n).then_inc(m["a_product"], 1)
            pe.wait_ge(m["gate_ready"], len(chunks))
            for k in range(TOKENS // BANK):
                for j, (c, n) in enumerate(chunks):
                    if k == 0:
                        pe.wait_ge(m["hidden_ready"], j + 1)
                    last = pe.matmul(ps[:, k * BANK:(k + 1) * BANK], w2[0:n, j, :],
                                     hidden[0:n, j, k * BANK:(k + 1) * BANK], start=(j == 0),
                                     stop=(j == len(chunks) - 1))
            last.then_inc(m["out_product"], 1)


def causal_stage(nc, g, d):
    with ExitStack() as outer:
        so = Stage(nc, outer, g.sems, "causal")
        hT = so.sb("hT", [P, TOKENS])
        norm_to_channels(nc, g, "causal_norm", hT)
        causal_attention(nc, g, d, hT)


def causal_attention(nc, g, d, hT):
    with ExitStack() as ctx:
        s = Stage(nc, ctx, g.sems, "causal_attn")
        raw = s.sb("raw", [P, 3, P])
        wT = s.sb("wT", [P, 3, P])
        bcol = s.sb("bcol", [P, 3])
        qT = s.sb("qT", [P, TOKENS])
        kT = s.sb("kT", [P, TOKENS])
        value = s.sb("value", [P, TILES, P])
        peaks = s.sb("peaks", [P, 2, SLOTS])
        sums = s.sb("sums", [P, 2, SLOTS])
        inverse = s.sb("inverse", [P, 2, SLOTS])
        probs = s.sb("probs", [P, SLOTS, SPAN])
        probsT = s.sb("probsT", [P, SLOTS, SPAN])
        oT = s.sb("oT", [P, TOKENS])
        names = ("loaded w_transposed w_ready q_product k_product v_product q_ready k_ready v_ready scores_ready "
                 "peaks_ready exp_done normalized mixed o_ready o_transposed inverse_ready").split()
        m = {n: s.sem(n) for n in names}
        transposed = [s.sem(f"transposed{i}") for i in range(2)]
        probsT_copied = [s.sem(f"probsT_copied{i}") for i in range(2)]
        ps = g.ps
        lo, hi = ps[:, 0:TOKENS], ps[:, TOKENS:2 * TOKENS]
        block = ctx.enter_context(nc.Block())

        @block.sync
        def _(sp):
            for i, n in enumerate("qkv"):
                sp.dma_start(raw[:, i, :], d["L1_attn_W" + n]).then_inc(m["loaded"], 16)
                sp.dma_start(bcol[:, i:i + 1], column(d["L1_attn_b" + n])).then_inc(m["loaded"], 16)

        @block.tensor
        def _(pe):
            pe.wait_ge(m["loaded"], 96)
            for i in range(3):
                last = pe.transpose(ps[:, i * P:(i + 1) * P], raw[:, i, :], g.ident[:, :])
            last.then_inc(m["w_transposed"], 1)
            pe.wait_ge(m["w_ready"], 1)
            for base, i, done in ((0, 0, "q_product"), (TOKENS, 1, "k_product")):
                for k in range(TOKENS // BANK):
                    last = pe.matmul(ps[:, base + k * BANK:base + (k + 1) * BANK], wT[:, i, :],
                                     hT[:, k * BANK:(k + 1) * BANK], start=True, stop=True)
                last.then_inc(m[done], 1)
            pe.wait_ge(m["q_ready"], 1)
            for t in range(TILES):
                last = pe.matmul(ps[:, t * P:(t + 1) * P], hT[:, t * P:(t + 1) * P], wT[:, 2, :], start=True, stop=True)
            last.then_inc(m["v_product"], 1)
            pe.wait_ge(m["k_ready"], 1)
            pe.wait_ge(m["v_ready"], 1)
            for b in range(BATCHES):
                c = b * SEQ
                ins = slot_scores(pe, g, g.causal, b, lambda t: qT[:, c + t * P:c + (t + 1) * P],
                                  lambda n: kT[:, c:c + n * P])
                if b % 4 == 3:
                    ins.then_inc(m["scores_ready"], 1)
            pe.wait_ge(m["exp_done"], 2)
            for b in range(BATCHES):
                if b % 4 == 0:
                    pe.wait_ge(m["normalized"], b // 4 + 1)
                if b >= 2:
                    pe.wait_ge(probsT_copied[b % 2], b // 2)
                slot_transposes(pe, g, b, probs).then_inc(transposed[b % 2], 1)
            for b in range(BATCHES):
                pe.wait_ge(probsT_copied[b % 2], b // 2 + 1)
                last = slot_mix(pe, ps[:, b * SEQ:(b + 1) * SEQ], lambda kt: value[:, 2 * b + kt, :], b, probsT)
            last.then_inc(m["mixed"], 1)
            pe.wait_ge(m["o_ready"], 1)
            for t in range(TILES):
                last = pe.transpose(ps[:, TOKENS + t * P:TOKENS + (t + 1) * P], oT[:, t * P:(t + 1) * P], g.ident[:, :])
            last.then_inc(m["o_transposed"], 1)

        @block.scalar
        def _(act):
            act.wait_ge(m["w_transposed"], 1)
            act.activation(wT[:, :, :].rearrange("p i c -> p (i c)"), ps[:, 0:3 * P], ACT.Copy).then_inc(m["w_ready"], 1)
            act.wait_ge(m["loaded"], 96)
            act.wait_ge(m["k_product"], 1)
            act.activation(kT[:, :], hi, ACT.Identity, bias=bcol[:, 1:2]).then_inc(m["k_ready"], 1)
            act.wait_ge(m["v_product"], 1)
            act.activation(value[:, :, :].rearrange("p t c -> p (t c)"), lo, ACT.Copy).then_inc(m["v_ready"], 1)
            for b in range(BATCHES):
                if b % 4 == 0:
                    act.wait_ge(m["peaks_ready"], b // 4 + 1)
                ins = slot_exps(act, g, b, probs, peaks, sums, lambda t: 1.0)
                if b % 4 == 3:
                    ins.then_inc(m["exp_done"], 1)
            for b in range(0, BATCHES, 2):
                act.wait_ge(transposed[0], b // 2 + 1)
                act.activation(probsT[:, b, :], ps[:, 6 * BANK:6 * BANK + SPAN], ACT.Copy).then_inc(probsT_copied[0], 1)
            act.wait_ge(m["mixed"], 1)
            act.activation(oT[:, :], lo, ACT.Identity, bias=bcol[:, 2:3]).then_inc(m["o_ready"], 1)

        @block.vector
        def _(dve):
            dve.wait_ge(m["loaded"], 96)
            dve.wait_ge(m["q_product"], 1)
            dve.tensor_scalar(qT[:, :], lo, bcol[:, 0:1], float(P) ** -0.5, ALU.add, ALU.mult).then_inc(m["q_ready"], 1)
            for half in range(2):
                dve.wait_ge(m["scores_ready"], half + 1)
                slot_peaks(dve, g, half, peaks).then_inc(m["peaks_ready"], 1)
            for half in range(2):
                dve.wait_ge(m["exp_done"], half + 1)
                h = slice(4 * half, 4 * half + 4)
                dve.reciprocal(inverse[:, :, h], sums[:, :, h]).then_inc(m["inverse_ready"], 1)
                dve.wait_ge(m["inverse_ready"], half + 1)
                slot_normalize(dve, half, probs, inverse).then_inc(m["normalized"], 1)
            for b in range(1, BATCHES, 2):
                dve.wait_ge(transposed[1], b // 2 + 1)
                dve.tensor_copy(probsT[:, b, :], ps[:, 7 * BANK:7 * BANK + SPAN]).then_inc(probsT_copied[1], 1)
            dve.wait_ge(m["o_transposed"], 1)
            dve.tensor_tensor(g.x[:, :, :], g.x[:, :, :], hi.rearrange("p (t c) -> p t c", c=P), ALU.add)


LIMIT = 100.0


def binary_stage(nc, g, d):
    with ExitStack() as outer:
        so = Stage(nc, outer, g.sems, "binary")
        hT = so.sb("hT", [P, TOKENS])
        norm_to_channels(nc, g, "binary_norm", hT)
        binary_product(nc, g, d, hT)


def binary_product(nc, g, d, hT):
    with ExitStack() as ctx:
        s = Stage(nc, ctx, g.sems, "binary_product")
        w = s.sb("w", [P, P])
        wT = s.sb("wT", [P, P])
        scale = s.sb("scale", [P, P])
        bias = s.sb("bias", [P, P])
        y = s.sb("y", [P, TILES, P])
        loaded, signs, w_transposed, w_ready = s.sem("loaded"), s.sem("signs"), s.sem("w_transposed"), s.sem("w_ready")
        product_done, dve_order = s.sem("product_done"), s.sem("dve_order")
        block = ctx.enter_context(nc.Block())
        wide = [P, TILES, P]

        @block.sync
        def _(sp):
            sp.dma_start(w[:, :], d["L1_ffn_weights"]).then_inc(loaded, 16)
            sp.dma_start(scale[:, :], d["L1_ffn_scale"].partition_broadcast(P)).then_inc(loaded, 16)
            sp.dma_start(bias[:, :], d["L1_ffn_bias"].partition_broadcast(P)).then_inc(loaded, 16)

        @block.vector
        def _(dve):
            order = Order(dve, dve_order)
            dve.wait_ge(loaded, 48)
            order.done(dve.tensor_scalar(w[:, :], w[:, :], 0.0, 2.0, ALU.is_ge, ALU.mult))
            dve.tensor_scalar(w[:, :], w[:, :], 1.0, None, ALU.subtract).then_inc(signs, 1)
            dve.wait_ge(product_done, 1)
            order.done(dve.tensor_tensor(y[:, :, :], g.ps[:, 0:TOKENS].rearrange("p (t c) -> p t c", c=P),
                                         scale[:, :].unsqueeze(1).to_broadcast(wide), ALU.mult))
            order.done(dve.tensor_tensor(y[:, :, :], y[:, :, :], bias[:, :].unsqueeze(1).to_broadcast(wide), ALU.add))
            order.done(dve.tensor_scalar(y[:, :, :], y[:, :, :], -LIMIT, LIMIT, ALU.max, ALU.min))
            dve.tensor_tensor(g.x[:, :, :], g.x[:, :, :], y[:, :, :], ALU.add)

        @block.scalar
        def _(act):
            act.wait_ge(w_transposed, 1)
            act.activation(wT[:, :], g.ps[:, 0:P], ACT.Copy).then_inc(w_ready, 1)

        @block.tensor
        def _(pe):
            pe.wait_ge(signs, 1)
            pe.transpose(g.ps[:, 0:P], w[:, :], g.ident[:, :]).then_inc(w_transposed, 1)
            pe.wait_ge(w_ready, 1)
            for t in range(TILES):
                last = pe.matmul(g.ps[:, t * P:(t + 1) * P], hT[:, t * P:(t + 1) * P], wT[:, :], start=True, stop=True)
            last.then_inc(product_done, 1)


class Globals:
    pass


def build(nc, d, out, stop=99):
    g = Globals()
    with ExitStack() as ctx:
        g.x = ctx.enter_context(nc.sbuf_tensor("x_residual", [P, 16, P], F32))
        g.ident = ctx.enter_context(nc.sbuf_tensor("ident", [P, P], F32))
        g.identb = ctx.enter_context(nc.sbuf_tensor("identb", [P, P], BF16))
        g.causal = ctx.enter_context(nc.sbuf_tensor("causal_mask", [P, 3 * P], BF16))
        g.band = ctx.enter_context(nc.sbuf_tensor("band_mask", [P, 3 * P], BF16))
        g.ps = ctx.enter_context(nc.psum_tensor("banks", [P, 8 * BANK], F32))
        g.ctxT = ctx.enter_context(nc.sbuf_tensor("contextT", [P, BATCHES, KEYS], F32))
        stages = [load_stage, context_stage, scan_stage,
                  lambda *a: narrow_cross_stage(*a, "L0_xattn", 8 ** -0.5),
                  local_stage, causal_stage,
                  lambda *a: cross_stage(*a, "L1_xattn", 64 ** -0.5),
                  binary_stage]
        for i, f in enumerate(stages):
            if i <= stop:
                with ExitStack() as sem_ctx:
                    g.sems = Semaphores(nc, sem_ctx)
                    f(nc, g, d)
                    g.sems.clear()
        stored = ctx.enter_context(nc.semaphore("stored"))
        block = ctx.enter_context(nc.Block())

        @block.sync
        def _(sp):
            sp.dma_start(out.rearrange("b (t p) c -> p (b t) c", p=P), g.x[:, :, :]).then_inc(stored, 16)
            sp.wait_ge(stored, 16)


def rotary_tables():
    import numpy as np
    f = np.float32
    half = np.arange(0, LDIM, 2, dtype=f)
    inv_freq = (f(1.0) / np.power(f(10000.0), half / f(LDIM))).astype(f)
    t = np.arange(SEQ, dtype=f)
    freqs = np.tile(t[:, None] * inv_freq[None, :], (1, 2)).astype(f)
    base = ((half + f(0.4 * LDIM)) / f(1.4 * LDIM)).astype(f)
    power = ((t - SEQ // 2) / f(WINDOW // 2)).astype(f)
    scale = np.tile(np.power(base[None, :], power[:, None]), (1, 2)).astype(f)
    sign = np.where(np.arange(LDIM) < LDIM // 2, f(-1.0), f(1.0))
    cos, sin = np.cos(freqs), np.sin(freqs) * sign
    return np.stack([cos * scale, sin * scale, cos / scale, sin / scale]).astype(f)


def kernel(**inputs):
    import numpy as np
    from concourse import bacc
    from concourse.bass_utils import run_bass_kernel_spmd

    nc = bacc.Bacc("TRN2", target_bir_lowering=False, num_devices=1)
    arrays, d = {}, {}
    for name, a in list(inputs.items()) + [("rotary", rotary_tables())]:
        a = np.ascontiguousarray(a)
        arrays[f"in_{name}_dram"] = a
        d[name] = nc.dram_tensor(f"in_{name}_dram", a.shape, mybir.dt.from_np(a.dtype), kind="ExternalInput").ap()
    out = nc.dram_tensor("out_0_dram", inputs["x"].shape, F32, kind="ExternalOutput").ap()
    build(nc, d, out)
    r = run_bass_kernel_spmd(nc, [arrays], core_ids=[0])
    return r.results[0]["out_0_dram"]
```

```python
from contextlib import ExitStack

import concourse.bass as bass
from concourse import mybir

F32 = mybir.dt.float32
BF16 = mybir.dt.bfloat16
I32 = mybir.dt.int32
ALU = mybir.AluOpType
ACT = mybir.ActivationFunctionType
AX = mybir.AxisListType

P = 128
BANK = 512
EPS = 1e-5


def wait(eng, sem, value):
    if not isinstance(value, int) or value > 0:
        eng.wait_ge(sem, value)


class Order:

    def __init__(self, eng, sem):
        self.eng, self.sem, self.n = eng, sem, 0

    def done(self, ins):
        self.n += 1
        ins.then_inc(self.sem, 1)
        self.eng.wait_ge(self.sem, self.n)


class Stage:

    def __init__(self, nc, ctx, sems, name):
        self.nc, self.ctx, self.sems, self.name = nc, ctx, sems, name

    def sb(self, name, shape, dt=F32):
        return self.ctx.enter_context(self.nc.sbuf_tensor(f"{self.name}_{name}", shape, dt))

    def sem(self, name):
        return self.sems.new(f"{self.name}_{name}")


class Semaphores:

    def __init__(self, nc, ctx):
        self.nc, self.ctx, self.held = nc, ctx, []

    def new(self, name):
        self.held.append(self.ctx.enter_context(self.nc.semaphore(name)))
        return self.held[-1]

    def clear(self):
        with self.nc.Block() as block:
            @block.sync
            def _(sp):
                for sem in self.held:
                    sp.sem_clear(sem)


def column(ap):
    return ap.rearrange("(p o) -> p o", o=1)


class NormSteps:

    def __init__(self, s):
        self.centred, self.squared = s.sem("norm_centred"), s.sem("norm_squared")
        self.var_ready, self.std_ready = s.sem("norm_var_ready"), s.sem("norm_std_ready")


def norm_vector(dve, order, src, dst, sq, st, steps, count):
    n = src.shape[1]
    halves = [slice(0, n // 2), slice(n // 2, n)]
    order.done(dve.tensor_reduce(st[:, 0, :], src, AX.X, ALU.add))
    order.done(dve.tensor_scalar(st[:, 0, :], st[:, 0, :], 1.0 / P, None, ALU.mult))
    for t in halves:
        dve.tensor_tensor(dst[:, t], src[:, t], st[:, 0, t].unsqueeze(2).to_broadcast([P, n // 2, P]), ALU.subtract)\
            .then_inc(steps.centred, 1)
    for i, t in enumerate(halves):
        dve.wait_ge(steps.squared, 2 * (count - 1) + i + 1)
        order.done(dve.tensor_reduce(st[:, 1, t], sq[:, t], AX.X, ALU.add))
    dve.tensor_scalar(st[:, 1, :], st[:, 1, :], 1.0 / P, EPS, ALU.mult, ALU.add).then_inc(steps.var_ready, 1)
    dve.wait_ge(steps.std_ready, count)
    order.done(dve.reciprocal(st[:, 2, :], st[:, 1, :]))
    order.done(dve.tensor_tensor(dst, dst, st[:, 2, :].unsqueeze(2).to_broadcast([P, n, P]), ALU.mult))


def norm_scalar(act, dst, sq, st, steps, count):
    n = dst.shape[1]
    for i, t in enumerate((slice(0, n // 2), slice(n // 2, n))):
        act.wait_ge(steps.centred, 2 * (count - 1) + i + 1)
        act.activation(sq[:, t], dst[:, t], ACT.Square).then_inc(steps.squared, 1)
    act.wait_ge(steps.var_ready, count)
    act.activation(st[:, 1, :], st[:, 1, :], ACT.Sqrt).then_inc(steps.std_ready, 1)


def load_stage(nc, g, d):
    with ExitStack() as ctx:
        s = Stage(nc, ctx, g.sems, "load")
        x_loaded = s.sem("x_loaded")
        zeroed, made = s.sem("zeroed"), s.sem("made")
        block = ctx.enter_context(nc.Block())

        @block.sync
        def _(sp):
            sp.dma_start(g.x[:, :, :], d["x"].rearrange("b (t p) c -> p (b t) c", p=P)).then_inc(x_loaded, 16)
            sp.wait_ge(x_loaded, 16)

        @block.gpsimd
        def _(pool):
            pool.memset(g.ident[:, :], 0.0).then_inc(zeroed, 1)
            pool.memset(g.identb[:, :], 0.0).then_inc(zeroed, 1)
            pool.memset(g.causal[:, :], 0.0).then_inc(zeroed, 1)
            pool.wait_ge(zeroed, 3)
            for m in (g.ident, g.identb):
                pool.affine_select(out=m[:, :], in_=m[:, :], compare_op=ALU.not_equal, fill=1.0, base=0,
                                   pattern=[[-1, P]], channel_multiplier=1).then_inc(made, 1)
            for col, n, first in ((0, P, 0), (P, 2 * P, P)):
                m = g.causal[:, col:col + n]
                pool.affine_select(out=m, in_=m, compare_op=ALU.is_ge, fill=MASKED, base=first,
                                   pattern=[[-1, n]], channel_multiplier=1).then_inc(made, 1)
            pool.wait_ge(made, 4)
            for col, n, first in ((0, P, 0), (P, 2 * P, P)):
                pool.affine_select(out=g.band[:, col:col + n], in_=g.causal[:, col:col + n], compare_op=ALU.is_ge,
                                   fill=MASKED, base=WINDOW - first, pattern=[[1, n]],
                                   channel_multiplier=-1).then_inc(made, 1)


MASKED = -1.0e25
WINDOW = 64


def scan_stage(nc, g, d):
    tokens = g.x.shape[1] * P
    T = tokens // P
    B, L = 8, tokens // 8
    with ExitStack() as ctx:
        s = Stage(nc, ctx, g.sems, "scan")
        h0 = s.sb("h0", [P, T, P])
        hn = s.sb("hn", [P, T, P])
        sq = s.sb("sq", [P, T, P])
        st = s.sb("st", [P, 3, T])
        hT = s.sb("hT", [P, tokens])
        xc = s.sb("xc", [P, tokens])
        xa = s.sb("xa", [P, tokens])
        zs = s.sb("zs", [P, tokens])
        low = s.sb("low", [112, tokens])
        v = s.sb("v", [P, tokens])
        e = s.sb("e", [P, tokens])
        u = s.sb("u", [P, tokens])
        small = s.sb("small", [P, tokens], I32)
        series = s.sb("series", [P, tokens])
        dA = s.sb("dA", [P, tokens])
        w_in = s.sb("w_in", [P, 2 * P])
        w_low = s.sb("w_low", [P, 112])
        w_up = s.sb("w_up", [112, P])
        w_out = s.sb("w_out", [P, P])
        conv = s.sb("conv", [P, 3])
        cols = s.sb("cols", [P, 6])
        gamma, beta, conv_b, b_dt, A, skip = (cols[:, i:i + 1] for i in range(6))
        loaded, gap_zeroed = s.sem("loaded"), s.sem("gap_zeroed")
        steps = NormSteps(s)
        hn_ready, hn_transposed, hT_ready = s.sem("hn_ready"), s.sem("hn_transposed"), s.sem("hT_ready")
        xb_ready, z_ready, zs_ready = s.sem("xb_ready"), s.sem("z_ready"), s.sem("zs_ready")
        xc_ready, xa_ready = s.sem("xc_ready"), s.sem("xa_ready")
        low_product, low_ready = s.sem("low_product"), s.sem("low_ready")
        v_product, bm_product, cm_product = s.sem("v_product"), s.sem("bm_product"), s.sem("cm_product")
        v_ready, e_ready, u_ready, log_ready = s.sem("v_ready"), s.sem("e_ready"), s.sem("u_ready"), s.sem("log_ready")
        delta_ready, dA_ready = s.sem("delta_ready"), s.sem("dA_ready")
        gated_ready, out_product = s.sem("gated_ready"), s.sem("out_product")
        dve_order, act_order = s.sem("dve_order"), s.sem("act_order")
        LOADS = 15
        ps = g.ps
        lo, hi = ps[:, 0:tokens], ps[:, tokens:2 * tokens]
        block = ctx.enter_context(nc.Block())

        @block.sync
        def _(sp):
            pairs = [(w_in[:, :], d["L0_attn_W_in"]), (w_out[:, :], d["L0_attn_W_out"])]
            pairs += [(c, column(d["L0_attn_" + n])) for c, n in (
                (gamma, "gamma"), (beta, "beta"), (conv_b, "conv_b"), (b_dt, "b_dt"), (A, "A"), (skip, "D_skip"))]
            for dst, src in pairs:
                sp.dma_start(dst, src).then_inc(loaded, 16)
            for k in range(3):
                sp.dma_start(conv[:, k:k + 1], d["L0_attn_conv_w"][k].rearrange("o c -> c o")).then_inc(loaded, 16)
            sp.dma_start(w_up[0:64, :], d["L0_attn_W_dt"]).then_inc(loaded, 16)
            sp.dma_start(w_up[64:80, :], d["L0_attn_W_Bp"]).then_inc(loaded, 16)
            sp.dma_start(w_up[96:112, :], d["L0_attn_W_Cp"]).then_inc(loaded, 16)
            sp.wait_ge(gap_zeroed, 1)
            sp.dma_start(w_low[:, 0:64], d["L0_attn_W_xp"]).then_inc(loaded, 16)
            sp.dma_start(w_low[:, 64:80], d["L0_attn_W_Bg"]).then_inc(loaded, 16)
            sp.dma_start(w_low[:, 96:112], d["L0_attn_W_Cg"]).then_inc(loaded, 16)

        @block.gpsimd
        def _(pool):
            pool.memset(w_low[:, :], 0.0).then_inc(gap_zeroed, 1)

        @block.vector
        def _(dve):
            order = Order(dve, dve_order)
            norm_vector(dve, order, g.x[:, :, :], h0[:, :, :], sq[:, :, :], st, steps, 1)
            norm_vector(dve, order, h0[:, :, :], hn[:, :, :], sq[:, :, :], st, steps, 2)
            order.done(dve.tensor_tensor(g.x[:, :, :], g.x[:, :, :], h0[:, :, :], ALU.add))
            dve.sem_inc(hn_ready, 1)
            dve.wait_ge(xb_ready, 1)
            dve.wait_ge(loaded, 16 * (LOADS + 2))
            order.done(dve.tensor_scalar(xc[:, :], hi, conv[:, 1:2], conv_b, ALU.mult, ALU.add))
            c3, x3 = xc[:, :].rearrange("p (b l) -> p b l", b=B), hi.rearrange("p (b l) -> p b l", b=B)
            order.done(dve.scalar_tensor_tensor(out=c3[:, :, 1:L], in0=x3[:, :, 0:L - 1], scalar=conv[:, 0:1],
                                                in1=c3[:, :, 1:L], op0=ALU.mult, op1=ALU.add))
            dve.scalar_tensor_tensor(out=c3[:, :, 0:L - 1], in0=x3[:, :, 1:L], scalar=conv[:, 2:3],
                                     in1=c3[:, :, 0:L - 1], op0=ALU.mult, op1=ALU.add).then_inc(xc_ready, 1)
            dve.wait_ge(v_product, 1)
            dve.tensor_scalar(v[:, :], lo, b_dt, None, ALU.add).then_inc(v_ready, 1)
            dve.wait_ge(e_ready, 1)
            order.done(dve.tensor_scalar(series[:, :], e[:, :], 1.0 / 3, -0.5, ALU.mult, ALU.add))
            order.done(dve.tensor_scalar(small[:, :], e[:, :], 2.0 ** -7, None, ALU.is_lt))
            order.done(dve.tensor_tensor(series[:, :], series[:, :], e[:, :], ALU.mult))
            order.done(dve.scalar_tensor_tensor(out=series[:, :], in0=series[:, :], scalar=1.0, in1=e[:, :],
                                                op0=ALU.add, op1=ALU.mult))
            dve.wait_ge(log_ready, 1)
            order.done(dve.copy_predicated(u[:, :], small[:, :], series[:, :]))
            dve.scalar_tensor_tensor(out=v[:, :], in0=v[:, :], scalar=0.0, in1=u[:, :], op0=ALU.max,
                                     op1=ALU.add).then_inc(delta_ready, 1)
            dve.wait_ge(delta_ready, 1)
            dve.wait_ge(bm_product, 1)
            order.done(dve.tensor_tensor(e[:, :], v[:, :], hi, ALU.mult))
            order.done(dve.tensor_tensor(e[:, :], e[:, :], xa[:, :], ALU.mult))
            dve.wait_ge(dA_ready, 1)
            for b in range(B):
                c = slice(b * L, (b + 1) * L)
                order.done(dve.tensor_tensor_scan(u[:, c], dA[:, c], e[:, c], 0.0, ALU.mult, ALU.add))
            dve.wait_ge(cm_product, 1)
            order.done(dve.tensor_tensor(u[:, :], u[:, :], lo, ALU.mult))
            order.done(dve.scalar_tensor_tensor(out=u[:, :], in0=xa[:, :], scalar=skip, in1=u[:, :],
                                                op0=ALU.mult, op1=ALU.add))
            dve.wait_ge(zs_ready, 1)
            dve.tensor_tensor(u[:, :], u[:, :], zs[:, :], ALU.mult).then_inc(gated_ready, 1)
            dve.wait_ge(out_product, 1)
            dve.tensor_tensor(g.x[:, :, :], g.x[:, :, :], hi.rearrange("p (t c) -> p t c", c=P), ALU.add)

        @block.scalar
        def _(act):
            order = Order(act, act_order)
            norm_scalar(act, h0[:, :, :], sq[:, :, :], st, steps, 1)
            norm_scalar(act, hn[:, :, :], sq[:, :, :], st, steps, 2)
            act.wait_ge(loaded, 16 * (LOADS + 2))
            act.wait_ge(hn_transposed, 1)
            act.activation(hT[:, :], lo, ACT.Identity, bias=beta, scale=gamma).then_inc(hT_ready, 1)
            act.wait_ge(z_ready, 1)
            act.activation(zs[:, :], lo, ACT.Silu).then_inc(zs_ready, 1)
            act.wait_ge(xc_ready, 1)
            act.activation(xa[:, :], xc[:, :], ACT.Silu).then_inc(xa_ready, 1)
            act.wait_ge(low_product, 1)
            act.activation(low[:, :], hi[0:112, :], ACT.Copy).then_inc(low_ready, 1)
            act.wait_ge(v_ready, 1)
            order.done(act.activation(e[:, :], v[:, :], ACT.Abs))
            act.activation(e[:, :], e[:, :], ACT.Exp, scale=-1.0).then_inc(e_ready, 1)
            act.wait_ge(e_ready, 1)
            act.activation(u[:, :], e[:, :], ACT.Ln, bias=1.0).then_inc(log_ready, 1)
            act.wait_ge(delta_ready, 1)
            act.activation(dA[:, :], v[:, :], ACT.Exp, scale=A).then_inc(dA_ready, 1)

        @block.tensor
        def _(pe):
            def product(base, lhsT, rhs, rows=P):
                for n in range(tokens // BANK):
                    c = slice(n * BANK, (n + 1) * BANK)
                    last = pe.matmul(ps[0:rows, base + n * BANK:base + (n + 1) * BANK], lhsT, rhs[:, c],
                                     start=True, stop=True)
                return last

            pe.wait_ge(hn_ready, 1)
            for t in range(T):
                last = pe.transpose(ps[:, t * P:(t + 1) * P], hn[:, t, :], g.ident[:, :])
            last.then_inc(hn_transposed, 1)
            pe.wait_ge(hT_ready, 1)
            product(tokens, w_in[:, 0:P], hT).then_inc(xb_ready, 1)
            product(0, w_in[:, P:2 * P], hT).then_inc(z_ready, 1)
            pe.wait_ge(xa_ready, 1)
            product(tokens, w_low[:, :], xa, 112).then_inc(low_product, 1)
            pe.wait_ge(low_ready, 1)
            pe.wait_ge(zs_ready, 1)
            product(0, w_up[0:64, :], low[0:64, :]).then_inc(v_product, 1)
            product(tokens, w_up[64:80, :], low[64:80, :]).then_inc(bm_product, 1)
            pe.wait_ge(v_ready, 1)
            product(0, w_up[96:112, :], low[96:112, :]).then_inc(cm_product, 1)
            pe.wait_ge(gated_ready, 1)
            for t in range(T):
                last = pe.matmul(ps[:, tokens + t * P:tokens + (t + 1) * P], u[:, t * P:(t + 1) * P], w_out[:, :],
                                 start=True, stop=True)
            last.then_inc(out_product, 1)


HEADS = 16
BATCHES = 8
TILES = 16
KEYS = 1601
KT = (KEYS + P - 1) // P
TAIL = KEYS - (KT - 1) * P
SPLIT = ((0, 401), (401, 400), (801, 400), (1201, 400))
GROUPS = ((0, 4), (4, 4), (8, 4), (12, 1))


def load_context(sp, d, b, dst, loaded):
    c = d["ctx_1024"][b]
    whole = (KT - 1) * P
    sp.dma_start(dst[:, 0:KT - 1, :], c[0:whole, :].rearrange("(t p) c -> p t c", p=P)).then_inc(loaded, 16)
    sp.dma_start(dst[0:TAIL, KT - 1, :], c[whole:KEYS, :]).then_inc(loaded, 16)


def context_stage(nc, g, d):
    with ExitStack() as ctx:
        s = Stage(nc, ctx, g.sems, "context")
        raw = [s.sb(f"raw{i}", [P, KT, P]) for i in range(2)]
        raw_loaded = [s.sem(f"raw_loaded{i}") for i in range(2)]
        transposed = [s.sem(f"transposed{i}") for i in range(2)]
        copied = [s.sem(f"copied{i}") for i in range(2)]
        block = ctx.enter_context(nc.Block())

        def bank(n):
            return g.ps[:, (n % 8) * BANK:(n % 8 + 1) * BANK]

        @block.sync
        def _(sp):
            for b in range(BATCHES):
                wait(sp, transposed[1], 2 * b - 2)
                load_context(sp, d, b, raw[b % 2], raw_loaded[b % 2])

        @block.tensor
        def _(pe):
            for b in range(BATCHES):
                pe.wait_ge(raw_loaded[b % 2], 32 * (b // 2 + 1))
                for j, (t0, n) in enumerate(GROUPS):
                    wait(pe, copied[j % 2], 2 * (b - 2) + j // 2 + 1)
                    for i in range(n):
                        rows = P if t0 + i < KT - 1 else TAIL
                        last = pe.transpose(bank(4 * b + j)[:, i * P:i * P + rows], raw[b % 2][0:rows, t0 + i, :],
                                            g.ident[0:rows, 0:rows])
                    last.then_inc(transposed[j % 2], 1)

        def copies(eng, side, copy):
            for b in range(BATCHES):
                for j in (side, side + 2):
                    t0, n = GROUPS[j]
                    cols = min(n * P, KEYS - t0 * P)
                    eng.wait_ge(transposed[side], 2 * b + j // 2 + 1)
                    copy(g.ctxT[:, b, t0 * P:t0 * P + cols], bank(4 * b + j)[:, 0:cols]).then_inc(copied[side], 1)

        @block.scalar
        def _(act):
            copies(act, 0, lambda o, i: act.activation(o, i, ACT.Copy))

        @block.vector
        def _(dve):
            copies(dve, 1, dve.tensor_copy)


def transpose_tokens(g, pe, src, base, done):
    for t in range(TILES):
        last = pe.transpose(g.ps[:, base + t * P:base + (t + 1) * P], src[:, t, :], g.ident[:, :])
    last.then_inc(done, 1)


def cross_stage(nc, g, d, name, scale):
    wq, wk, wv = (d[f"{name}_W{n}"].rearrange("c h e -> c (h e)") for n in "qkv")
    bq, bk, bv = (d[f"{name}_b{n}"].rearrange("h e -> (h e)") for n in "qkv")
    wo = d[name + "_Wo"].rearrange("h e c -> (h e) c")
    with ExitStack() as ctx:
        so = Stage(nc, ctx, g.sems, name)
        A = so.sb("A", [P, HEADS, P + 1])
        B = so.sb("B", [P, HEADS, P])
        cb = so.sb("cb", [P, TILES, HEADS])
        hT = so.sb("hT", [P, TILES * P])
        fold_weights(nc, g, name, A, B, cb, hT, scale, wq, wk, wv, wo, bq, bk, bv, d[name + "_bo"])
        cross_heads(nc, g, d, name, A, B, cb, hT)


def fold_weights(nc, g, name, A, B, cb, hT, scale, wq, wk, wv, wo, bq, bk, bv, bo):
    nb = wq.shape[1] // P
    per = HEADS // nb
    dh = P // per
    with ExitStack() as ctx:
        s = Stage(nc, ctx, g.sems, name + "_fold")
        hn = s.sb("hn", [P, TILES, P])
        sq = s.sb("sq", [P, TILES, P])
        st = s.sb("st", [P, 3, TILES])
        raw = s.sb("raw", [P, 3, nb * P])
        wT = s.sb("wT", [P, 3, nb, P])
        wo_sb = s.sb("wo", [P, nb, P])
        masked = s.sb("masked", [P, 2, HEADS, P])
        head_rows = s.sb("head_rows", [P, per])
        bcol = s.sb("bcol", [P, 3, nb])
        bmask = s.sb("bmask", [P, 2, nb, per])
        bwide = s.sb("bwide", [P, 2, nb, P])
        bo_rows = s.sb("bo_rows", [P, P])
        c_all = s.sb("c_all", [P, HEADS])
        c0 = s.sb("c0", [P, HEADS])
        orow = s.sb("orow", [P, P])
        w_loaded, b_loaded, rows_made = s.sem("w_loaded"), s.sem("b_loaded"), s.sem("rows_made")
        steps = NormSteps(s)
        hn_ready, hn_transposed, hT_ready = s.sem("hn_ready"), s.sem("hn_transposed"), s.sem("hT_ready")
        w_transposed, w_ready = s.sem("w_transposed"), s.sem("w_ready")
        bias_masks_ready = s.sem("bias_masks_ready")
        masks_ready, a_product, a_copied = s.sem("masks_ready"), s.sem("a_product"), s.sem("a_copied")
        b_product, b_copied = s.sem("b_product"), s.sem("b_copied")
        bias_product, c_ready, cb_product = s.sem("bias_product"), s.sem("c_ready"), s.sem("cb_product")
        dve_order, pool_order = s.sem("dve_order"), s.sem("pool_order")
        ps = g.ps
        WEIGHTS, BIASES = 3 + 1, 3 + 1
        SUMS = 2 * BANK
        CB = 3 * BANK
        block = ctx.enter_context(nc.Block())

        @block.sync
        def _(sp):
            for i, w in enumerate((wq, wk, wv)):
                sp.dma_start(raw[:, i, :], w).then_inc(w_loaded, 16)
            sp.dma_start(wo_sb[:, :, :], wo.rearrange("(j p) c -> p j c", p=P)).then_inc(w_loaded, 16)
            for i, b in enumerate((bq, bk, bv)):
                sp.dma_start(bcol[:, i, :], b.rearrange("(j p) -> p j", p=P), allow_slow_non_contiguous=True)\
                    .then_inc(b_loaded, 16)
            sp.dma_start(bo_rows[:, :], bo.partition_broadcast(P)).then_inc(b_loaded, 16)

        @block.gpsimd
        def _(pool):
            order = Order(pool, pool_order)
            order.done(pool.memset(head_rows[:, :], 1.0))
            order.done(pool.affine_select(out=head_rows[:, :], in_=head_rows[:, :], compare_op=ALU.is_ge, fill=0.0,
                                          base=0, pattern=[[-dh, per]], channel_multiplier=1))
            pool.affine_select(out=head_rows[:, :], in_=head_rows[:, :], compare_op=ALU.is_ge, fill=0.0,
                               base=dh - 1, pattern=[[dh, per]], channel_multiplier=-1).then_inc(rows_made, 1)

        @block.vector
        def _(dve):
            order = Order(dve, dve_order)
            norm_vector(dve, order, g.x[:, :, :], hn[:, :, :], sq[:, :, :], st, steps, 1)
            dve.sem_inc(hn_ready, 1)
            dve.wait_ge(rows_made, 1)
            dve.wait_ge(w_ready, 1)
            for i in range(2):
                for r in range(per):
                    order.done(dve.tensor_scalar(masked[:, i, r:HEADS:per, :], wT[:, 2 * i, :, :],
                                                 head_rows[:, r:r + 1], None, ALU.mult))
                dve.sem_inc(masks_ready, 1)
            dve.wait_ge(b_loaded, 16 * BIASES)
            for i in range(2):
                order.done(dve.tensor_tensor(bmask[:, i, :, :],
                                             head_rows[:, :].unsqueeze(1).to_broadcast([P, nb, per]),
                                             bcol[:, i, :].unsqueeze(2).to_broadcast([P, nb, per]), ALU.mult))
                order.done(dve.tensor_copy(bwide[:, i, :, :],
                                           bcol[:, 2 * i, :].unsqueeze(2).to_broadcast([P, nb, P])))
            dve.sem_inc(bias_masks_ready, 1)
            dve.wait_ge(b_product, 1)
            dve.tensor_copy(B[:, :, :], ps[:, 4 * BANK:8 * BANK].rearrange("p (h c) -> p h c", c=P))\
                .then_inc(b_copied, 1)
            dve.wait_ge(bias_product, 1)
            order.done(dve.tensor_scalar(A[:, :, P], ps[:, SUMS:SUMS + HEADS], scale, None, ALU.mult))
            order.done(dve.tensor_scalar(c_all[:, :], ps[:, SUMS + 16:SUMS + 32], scale, None, ALU.mult))
            order.done(dve.tensor_scalar(c0[:, :], ps[:, SUMS + 32:SUMS + 48], scale, None, ALU.mult))
            order.done(dve.tensor_tensor(orow[:, :], ps[:, SUMS + P:SUMS + 2 * P], bo_rows[:, :], ALU.add))
            dve.sem_inc(c_ready, 1)
            order.done(dve.tensor_tensor(g.x[:, :, :], g.x[:, :, :],
                                         orow[:, :].unsqueeze(1).to_broadcast([P, TILES, P]), ALU.add))
            dve.wait_ge(cb_product, 1)
            dve.tensor_tensor(cb[:, :, :], ps[:, CB:CB + TILES * HEADS].rearrange("p (t h) -> p t h", h=HEADS),
                              c0[:, :].unsqueeze(1).to_broadcast([P, TILES, HEADS]), ALU.add)

        @block.scalar
        def _(act):
            norm_scalar(act, hn[:, :, :], sq[:, :, :], st, steps, 1)
            act.wait_ge(w_transposed, 1)
            act.activation(wT[:, :, :, :].rearrange("p k j c -> p (k j c)"), ps[:, 0:3 * nb * P], ACT.Copy)\
                .then_inc(w_ready, 1)
            act.wait_ge(a_product, 1)
            act.activation(A[:, :, 0:P], ps[:, 0:4 * BANK].rearrange("p (h c) -> p h c", c=P), ACT.Copy, scale=scale)\
                .then_inc(a_copied, 1)
            act.wait_ge(hn_transposed, 1)
            act.activation(hT[:, :], ps[:, 4 * BANK:8 * BANK], ACT.Copy).then_inc(hT_ready, 1)

        @block.tensor
        def _(pe):
            pe.wait_ge(w_loaded, 16 * WEIGHTS)
            for i in range(3):
                for j in range(nb):
                    c = (i * nb + j) * P
                    last = pe.transpose(ps[:, c:c + P], raw[:, i, j * P:(j + 1) * P], g.ident[:, :])
            last.then_inc(w_transposed, 1)
            pe.wait_ge(masks_ready, 1)
            for h in range(HEADS):
                last = pe.matmul(ps[:, h * P:(h + 1) * P], masked[:, 0, h, :], wT[:, 1, h // per, :],
                                 start=True, stop=True)
            last.then_inc(a_product, 1)
            pe.wait_ge(masks_ready, 2)
            for h in range(HEADS):
                c = 4 * BANK + h * P
                last = pe.matmul(ps[:, c:c + P], masked[:, 1, h, :], wo_sb[:, h // per, :], start=True, stop=True)
            last.then_inc(b_product, 1)
            pe.wait_ge(a_copied, 1)
            pe.wait_ge(bias_masks_ready, 1)
            for j in range(nb):
                c = SUMS + j * per
                pe.matmul(ps[:, c:c + per], wT[:, 1, j, :], bmask[:, 0, j, :], start=True, stop=True)
                pe.matmul(ps[:, c + 16:c + 16 + per], wT[:, 0, j, :], bmask[:, 1, j, :], start=True, stop=True)
                pe.matmul(ps[:, c + 32:c + 32 + per], bwide[:, 0, j, :], bmask[:, 1, j, :], start=True, stop=True)
            for j in range(nb):
                last = pe.matmul(ps[:, SUMS + P:SUMS + 2 * P], bwide[:, 1, j, :], wo_sb[:, j, :], start=(j == 0),
                                 stop=(j == nb - 1))
            last.then_inc(bias_product, 1)
            pe.wait_ge(hn_ready, 1)
            pe.wait_ge(b_copied, 1)
            transpose_tokens(g, pe, hn, 4 * BANK, hn_transposed)
            pe.wait_ge(hT_ready, 1)
            pe.wait_ge(c_ready, 1)
            for t in range(TILES):
                last = pe.matmul(ps[:, CB + t * HEADS:CB + (t + 1) * HEADS], hT[:, t * P:(t + 1) * P], c_all[:, :],
                                 start=True, stop=True)
            last.then_inc(cb_product, 1)


def cross_heads(nc, g, d, name, A, B, cb, hT):
    with ExitStack() as ctx:
        s = Stage(nc, ctx, g.sems, name + "_heads")
        kv = [s.sb(f"context{i}", [P, KT, P]) for i in range(2)]
        a_head = s.sb("a_head", [P, P + 1])
        qT = [s.sb(f"qT{i}", [P, 2 * P]) for i in range(2)]
        probs = [s.sb(f"probs{i}", [P, KEYS]) for i in range(2)]
        pT = [s.sb(f"pT{i}", [P, KT, 2 * P]) for i in range(2)]
        mixed = s.sb("mixed", [P, 2 * P])
        peak = s.sb("peak", [P, 2, 3])
        shift = s.sb("shift", [P, 2])
        total = s.sb("total", [P, 2, 2, 2])
        inverse = s.sb("inverse", [P, 2, 2])
        kv_loaded = [s.sem(f"kv_loaded{i}") for i in range(2)]
        a_copied, q_product, q_ready = s.sem("a_copied"), s.sem("q_product"), s.sem("q_ready")
        scores_ready, parts_ready, peak_ready = s.sem("scores_ready"), s.sem("parts_ready"), s.sem("peak_ready")
        shift_ready, exp_done = s.sem("shift_ready"), s.sem("exp_done")
        transposed = [s.sem(f"transposed{i}") for i in range(2)]
        pT_copied = [s.sem(f"pT_copied{i}") for i in range(2)]
        mix_product, mix_ready = s.sem("mix_product"), s.sem("mix_ready")
        out_product, out_added = s.sem("out_product"), s.sem("out_added")
        sums_ready, inverse_ready = s.sem("sums_ready"), s.sem("inverse_ready")
        ps = g.ps
        score = ps[:, 0:4 * BANK].rearrange("p (k n) -> p k n", n=BANK)
        tbank = [ps[:, (4 + i) * BANK:(5 + i) * BANK] for i in range(2)]
        mix = ps[:, 6 * BANK:6 * BANK + 2 * P]
        q_ps = ps[:, 7 * BANK:7 * BANK + 2 * P]
        out_ps = ps[:, 7 * BANK + 2 * P:8 * BANK]
        xf = g.x[:, :, :].rearrange("p t c -> p (t c)")
        cbf = cb[:, :, :].rearrange("p t h -> p (t h)")
        LAST = BATCHES * HEADS - 1
        QUARTER = KEYS // 4
        EARLY = KT // 2
        block = ctx.enter_context(nc.Block())

        def walk(eng, step):
            def batch(b, slot, first):
                step(b, 0, 0, slot, 0 if first else 2)
                step(b, 1, 1, slot, 1 if first else 2)
                with eng.Fori(1, HEADS // 2) as pair:
                    for k in range(2):
                        step(b, pair * 2 + k, k, slot, 2)

            batch(0, 0, True)
            batch(1, 1, False)
            with eng.Fori(1, BATCHES // 2) as two:
                for slot in range(2):
                    batch(two * 2 + slot, slot, False)

        def earlier(b, h, back):
            if isinstance(h, int) and h < back:
                return b - 1, h - back + HEADS
            return b, h - back

        def slot_of(h, slot, back):
            return 1 - slot if isinstance(h, int) and h < back else slot

        @block.sync
        def _(sp):
            for b in range(BATCHES):
                wait(sp, mix_product, HEADS * (b - 1))
                load_context(sp, d, b, kv[b % 2], kv_loaded[b % 2])

        @block.gpsimd
        def _(pool):
            def take(b, h):
                pool.wait_ge(q_ready, b * HEADS + h)
                pool.tensor_copy(a_head[:, :], A[:, :, :].rearrange("p h c -> p (h c)")[
                    :, bass.ds(h * (P + 1), P + 1)]).then_inc(a_copied, 1)

            pool.tensor_copy(a_head[:, :], A[:, 0, :]).then_inc(a_copied, 1)
            with pool.Fori(1, HEADS) as h:
                take(0, h)
            with pool.Fori(1, BATCHES) as b:
                with pool.Fori(0, HEADS) as h:
                    take(b, h)

        @block.tensor
        def _(pe):
            def project(n, b):
                pe.wait_ge(a_copied, n + 1)
                wait(pe, out_added, n - 2)
                pe.matmul(q_ps, a_head[:, 0:P], hT[:, bass.ds(b * (2 * P), 2 * P)], start=True, stop=True)\
                    .then_inc(q_product, 1)

            def scores(n, b, k, q):
                u = n * 2 + q
                pe.wait_ge(q_ready, n + 1)
                for i, (bank, width) in enumerate(((3, QUARTER + 1), (2, QUARTER + 1), (0, QUARTER), (1, QUARTER))):
                    if i == 0:
                        wait(pe, exp_done, u * 2 - 1)
                    if i == 1:
                        wait(pe, exp_done, u * 2)
                    ins = pe.matmul(score[:, bank, 0:width], qT[k][:, q * P:(q + 1) * P],
                                    g.ctxT[:, b, bank * QUARTER:bank * QUARTER + width], start=True, stop=True)
                    if i % 2 == 1:
                        ins.then_inc(scores_ready, 1)

            def transposes(n, q, groups):
                u = n * 2 + q
                pe.wait_ge(exp_done, u * 2 + 2)
                for j in groups:
                    t0, w = GROUPS[j]
                    wait(pe, pT_copied[j % 2], u * 2 + j // 2)
                    for t in range(t0, t0 + w):
                        rows = P if t < KT - 1 else TAIL
                        ins = pe.transpose(tbank[j % 2][0:rows, (t - t0) * P:(t - t0 + 1) * P],
                                           probs[q][:, t * P:t * P + rows], g.ident[:, :])
                    ins.then_inc(transposed[j % 2], 1)

            def mix_tiles(n, k, slot, tiles):
                u = n * 2 + 1
                if tiles[0] == 0:
                    wait(pe, mix_ready, n)
                for t in tiles:
                    if t % 4 == 0 or t == tiles[0]:
                        j = t // 4
                        pe.wait_ge(pT_copied[j % 2], u * 2 + j // 2 + 1)
                    rows = P if t < KT - 1 else TAIL
                    ins = pe.matmul(mix, kv[slot][0:rows, t, :], pT[k][0:rows, t, :], start=(t == 0),
                                    stop=(t == KT - 1))
                if tiles[-1] == KT - 1:
                    ins.then_inc(mix_product, 1)

            def output(n, h):
                pe.wait_ge(mix_ready, n + 1)
                wait(pe, out_added, n)
                for q in range(2):
                    ins = pe.matmul(out_ps[:, q * P:(q + 1) * P], mixed[:, q * P:(q + 1) * P],
                                    B[:, :, :].rearrange("p h c -> p (h c)")[:, bass.ds(h * P, P)],
                                    start=True, stop=True)
                ins.then_inc(out_product, 1)

            def step(b, h, k, slot, before):
                n = b * HEADS + h
                if isinstance(h, int) and h == 1:
                    pe.wait_ge(kv_loaded[slot], (b - slot) * 16 + 32)
                project(n, b)
                if before >= 2:
                    mix_tiles(n - 2, k, slot_of(h, slot, 2), range(EARLY, EARLY + 2))
                scores(n, b, k, 0)
                if before >= 1:
                    transposes(n - 1, 1, (0, 1))
                if before >= 2:
                    mix_tiles(n - 2, k, slot_of(h, slot, 2), range(EARLY + 2, EARLY + 4))
                if before >= 1:
                    transposes(n - 1, 1, (2,))
                if before >= 2:
                    mix_tiles(n - 2, k, slot_of(h, slot, 2), range(EARLY + 4, KT))
                if before >= 1:
                    transposes(n - 1, 1, (3,))
                scores(n, b, k, 1)
                transposes(n, 0, (0, 1))
                if before >= 1:
                    mix_tiles(n - 1, 1 - k, slot_of(h, slot, 1), range(0, 2))
                transposes(n, 0, (2,))
                if before >= 2:
                    output(n - 2, earlier(b, h, 2)[1])
                if before >= 1:
                    mix_tiles(n - 1, 1 - k, slot_of(h, slot, 1), range(2, EARLY))
                transposes(n, 0, (3,))

            walk(pe, step)
            mix_tiles(LAST - 1, 0, 1, range(EARLY, KT))
            transposes(LAST, 1, range(4))
            output(LAST - 1, HEADS - 2)
            mix_tiles(LAST, 1, 1, range(0, KT))
            output(LAST, HEADS - 1)

        def copy_groups(eng, side, copy, n, k, q, which=(0, 1)):
            u = n * 2 + q
            if q == 0:
                wait(eng, mix_product, n - 1)
            for j in (side + 2 * i for i in which):
                t0, w = GROUPS[j]
                rows = P if j < 3 else TAIL
                eng.wait_ge(transposed[side], u * 2 + j // 2 + 1)
                copy(pT[k][0:rows, t0:t0 + w, q * P:(q + 1) * P],
                     tbank[side][0:rows, 0:w * P].rearrange("p (t c) -> p t c", c=P)).then_inc(pT_copied[side], 1)

        @block.scalar
        def _(act):
            def copy(o, i):
                return act.activation(o, i, ACT.Copy)

            def exps(n, k, q):
                u = n * 2 + q
                act.wait_ge(shift_ready, u + 1)
                wait(act, transposed[1], u * 2 - 2)
                wait(act, inverse_ready, n - 1)
                act.activation(probs[q][:, 3 * QUARTER:KEYS], score[:, 3, 0:QUARTER + 1], ACT.Exp,
                               bias=shift[:, q:q + 1], accum_out=total[:, k, q, 0:1]).then_inc(exp_done, 1)
                act.activation(probs[q][:, 0:3 * QUARTER].rearrange("p (a n) -> p a n", n=QUARTER),
                               score[:, 0:3, 0:QUARTER], ACT.Exp, bias=shift[:, q:q + 1],
                               accum_out=total[:, k, q, 1:2]).then_inc(exp_done, 1)

            def take_mix(n):
                act.wait_ge(mix_product, n + 1)
                wait(act, out_product, n)
                act.activation(mixed[:, :], mix, ACT.Copy).then_inc(mix_ready, 1)

            def step(b, h, k, slot, before):
                n = b * HEADS + h
                act.wait_ge(q_product, n + 1)
                act.activation(qT[k][:, :], q_ps, ACT.Identity, bias=a_head[:, P:P + 1]).then_inc(q_ready, 1)
                if before >= 1:
                    copy_groups(act, 0, copy, n - 1, 1 - k, 1, (0,))
                exps(n, k, 0)
                if before >= 1:
                    copy_groups(act, 0, copy, n - 1, 1 - k, 1, (1,))
                if before >= 2:
                    take_mix(n - 2)
                copy_groups(act, 0, copy, n, k, 0, (0,))
                exps(n, k, 1)
                copy_groups(act, 0, copy, n, k, 0, (1,))

            walk(act, step)
            take_mix(LAST - 1)
            copy_groups(act, 0, copy, LAST, 1, 1)
            take_mix(LAST)

        @block.vector
        def _(dve):
            def shifts(b, h, n, q):
                u = n * 2 + q
                dve.wait_ge(scores_ready, u * 2 + 1)
                dve.tensor_reduce(peak[:, q, 0:1], score[:, 2:4, 0:QUARTER + 1], AX.XY, ALU.max)
                dve.wait_ge(scores_ready, u * 2 + 2)
                dve.tensor_reduce(peak[:, q, 1:2], score[:, 0:2, 0:QUARTER], AX.XY, ALU.max).then_inc(parts_ready, 1)
                cb_u = cbf[:, bass.ds((b * 2 + q) * HEADS + h, 1)]
                dve.wait_ge(parts_ready, u + 1)
                dve.scalar_tensor_tensor(out=peak[:, q, 2:3], in0=peak[:, q, 0:1], scalar=peak[:, q, 1:2], in1=cb_u,
                                         op0=ALU.max, op1=ALU.add).then_inc(peak_ready, 1)
                dve.wait_ge(peak_ready, u + 1)
                dve.tensor_tensor(shift[:, q:q + 1], cb_u, peak[:, q, 2:3], ALU.subtract).then_inc(shift_ready, 1)

            def inverses(n, k):
                dve.wait_ge(exp_done, n * 4 + 4)
                dve.tensor_tensor(inverse[:, k, :], total[:, k, :, 0], total[:, k, :, 1], ALU.add).then_inc(sums_ready, 1)
                dve.wait_ge(sums_ready, n + 1)
                dve.reciprocal(inverse[:, k, :], inverse[:, k, :]).then_inc(inverse_ready, 1)

            def add_output(n, k, b):
                dve.wait_ge(out_product, n + 1)
                dve.wait_ge(inverse_ready, n + 1)
                for q in range(2):
                    rows = xf[:, bass.ds((b * 2 + q) * P, P)]
                    ins = dve.scalar_tensor_tensor(out=rows, in0=out_ps[:, q * P:(q + 1) * P],
                                                   scalar=inverse[:, k, q:q + 1], in1=rows, op0=ALU.mult, op1=ALU.add)
                ins.then_inc(out_added, 1)

            def step(b, h, k, slot, before):
                n = b * HEADS + h
                shifts(b, h, n, 0)
                if before >= 1:
                    inverses(n - 1, 1 - k)
                    copy_groups(dve, 1, dve.tensor_copy, n - 1, 1 - k, 1)
                shifts(b, h, n, 1)
                copy_groups(dve, 1, dve.tensor_copy, n, k, 0, (0,))
                if before >= 2:
                    add_output(n - 2, k, earlier(b, h, 2)[0])
                copy_groups(dve, 1, dve.tensor_copy, n, k, 0, (1,))

            walk(dve, step)
            dve.wait_ge(out_added, LAST - 1)
            inverses(LAST, 1)
            copy_groups(dve, 1, dve.tensor_copy, LAST, 1, 1)
            add_output(LAST - 1, 0, BATCHES - 1)
            add_output(LAST, 1, BATCHES - 1)


PRODUCTS = 6
SHIFT_ROWS = 3
PAIR = 2 * 2 * P
QUADS = HEADS // 4
WINDOW_KEYS = KEYS // 4 + 1
CHUNKS = 16
LAG = 2
SCORE_RING = 2
PROBS_RING = 4


def narrow_cross_stage(nc, g, d, name, scale):
    dh = P // HEADS
    qd = nc.dram_tensor(name + "_queries", (3, BATCHES, P, 2 * P), BF16, kind="Internal").ap()
    kd = nc.dram_tensor(name + "_keys", (3, BATCHES, P, KEYS), BF16, kind="Internal").ap()
    vd = nc.dram_tensor(name + "_values", (BATCHES, P, KT * HEADS * (dh + 1)), F32, kind="Internal").ap()
    narrow_queries(nc, g, d, name, qd, scale)
    with ExitStack() as ctx:
        so = Stage(nc, ctx, g.sems, name)
        quads = QuadBuffers(so, qd, kd, vd, dh)
        narrow_keys(nc, g, d, name, kd, vd, dh, quads)
        heads_out = so.sb("heads_out", [P, TILES, P])
        narrow_heads(nc, g, name, quads, heads_out, dh)
        reshuffled_output(nc, g, name, heads_out, d[name + "_w_0"], d[name + "_b_v"], dh)


class QuadBuffers:
    LOADS = 2 + 2 * 3 * 2 + 1

    def __init__(self, s, qd, kd, vd, dh):
        self.dh = dh
        self.kstack = [s.sb(f"kstack{j}", [P, 2, KEYS], BF16) for j in range(QUADS)]
        self.qstack = [s.sb(f"qstack{j}", [P, 2, 2, 2 * P], BF16) for j in range(QUADS)]
        self.values = [s.sb(f"values{j}", [P, KT, 4, dh + 1]) for j in range(QUADS)]
        self.zeros = s.sb("zeros", [P, 2, 2, 2 * P], BF16)
        self.cleared = s.sem("cleared")
        self.loaded = [s.sem(f"loaded{j}") for j in range(QUADS)]
        self.kd, self.qd = (x.rearrange("a b (j i e r) n -> a j i b e (r n)", j=QUADS, i=2, r=2) for x in (kd, qd))
        self.vd = vd.rearrange("b p (t h e) -> (b p) t (h e)", t=KT, h=HEADS)

    def clear(self, eng, j):
        eng.memset(self.qstack[j][:, :, :, :], 0.0).then_inc(self.cleared, 1)
        eng.memset(self.kstack[j][:, :, :], 1.0).then_inc(self.cleared, 1)

    def load(self, sp, b, j):
        done = self.loaded[j]
        for i in range(2):
            rows = slice(64 * i, 64 * i + SHIFT_ROWS)
            sp.dma_start(self.qstack[j][rows, :, :, :], self.zeros[rows, :, :, :]).then_inc(done, 16)
        for i in range(2):
            row = 64 * i + SHIFT_ROWS
            for part, copies in ((0, 3), (1, 2), (2, 1)):
                rows = slice(row, row + copies * self.dh)
                sp.dma_start(self.kstack[j][rows, :, :], self.kd[part:part + 1, j, i, bass.ds(b, 1)]
                             .to_broadcast([copies, 1, self.dh, 2 * KEYS])).then_inc(done, 16)
                sp.dma_start(self.qstack[j][rows, i, :, :], self.qd[0:copies, j, i, bass.ds(b, 1)]).then_inc(done, 16)
                row += copies * self.dh
        per = 4 * (self.dh + 1)
        sp.dma_start(self.values[j][:, :, :, :].rearrange("p t h e -> p t (h e)"),
                     self.vd[bass.ds(b * P, P), :, j * per:(j + 1) * per]).then_inc(done, 16)


def order_weights(act, dst, src, done):
    new = dst[:, :].rearrange("p (j i e r) -> p j i e r", j=QUADS, i=2, r=2)
    old = src[:, :].rearrange("p (j r i e) -> p j i e r", j=QUADS, i=2, r=2)
    for j in range(QUADS):
        act.activation(new[:, j], old[:, j], ACT.Copy).then_inc(done, 1)


def load_ordered_bias(sp, dst, src, loaded):
    per = P // QUADS
    for j in range(QUADS):
        sp.dma_start(dst[j * per:(j + 1) * per, :],
                     src[j * per:(j + 1) * per].rearrange("(r i e) -> i e r", r=2, i=2),
                     allow_slow_non_contiguous=True).then_inc(loaded, 16)


def narrow_queries(nc, g, d, name, qd, scale):
    with ExitStack() as ctx:
        s = Stage(nc, ctx, g.sems, name + "_q")
        hn = s.sb("hn", [P, TILES, P])
        sq = s.sb("sq", [P, TILES, P])
        st = s.sb("st", [P, 3, TILES])
        hT = s.sb("hT", [P, TILES * P])
        q = s.sb("q", [P, TILES * P])
        rest = s.sb("rest", [P, TILES * P])
        parts = s.sb("parts", [P, 3, TILES * P], BF16)
        wq_raw = s.sb("wq_raw", [P, P])
        wq = s.sb("wq", [P, P])
        bq = s.sb("bq", [P, 1])
        b0_rows = s.sb("b0_rows", [P, P])
        loaded, steps = s.sem("loaded"), NormSteps(s)
        hn_ready, hn_transposed, hT_ready = s.sem("hn_ready"), s.sem("hn_transposed"), s.sem("hT_ready")
        q_product, parts_ready, stored = s.sem("q_product"), s.sem("parts_ready"), s.sem("stored")
        dve_order = s.sem("dve_order")
        w_ordered = s.sem("w_ordered")
        LOADS = 2 + QUADS
        block = ctx.enter_context(nc.Block())

        @block.sync
        def _(sp):
            sp.dma_start(wq_raw[:, :], d[name + "_w_q"]).then_inc(loaded, 16)
            load_ordered_bias(sp, bq, d[name + "_b_q"], loaded)
            sp.dma_start(b0_rows[:, :], d[name + "_b_0"].partition_broadcast(P)).then_inc(loaded, 16)
            for i in range(3):
                sp.wait_ge(parts_ready, i + 1)
                sp.dma_start(qd[i].rearrange("b p n -> p b n"), parts[:, i, :].rearrange("p (b n) -> p b n", b=BATCHES))\
                    .then_inc(stored, 16)
            sp.wait_ge(stored, 3 * 16)

        @block.vector
        def _(dve):
            order = Order(dve, dve_order)
            norm_vector(dve, order, g.x[:, :, :], hn[:, :, :], sq[:, :, :], st, steps, 1)
            dve.sem_inc(hn_ready, 1)
            dve.wait_ge(loaded, LOADS * 16)
            order.done(dve.tensor_tensor(g.x[:, :, :], g.x[:, :, :],
                                         b0_rows[:, :].unsqueeze(1).to_broadcast([P, TILES, P]), ALU.add))
            dve.wait_ge(q_product, 1)
            order.done(dve.tensor_scalar(q[:, :], g.ps[:, 0:4 * BANK], bq[:, 0:1], scale, ALU.add, ALU.mult))
            order.done(dve.tensor_copy(parts[:, 0, :], q[:, :]))
            dve.sem_inc(parts_ready, 1)
            order.done(dve.tensor_tensor(rest[:, :], q[:, :], parts[:, 0, :], ALU.subtract))
            order.done(dve.tensor_copy(parts[:, 1, :], rest[:, :]))
            dve.sem_inc(parts_ready, 1)
            dve.tensor_tensor(parts[:, 2, :], rest[:, :], parts[:, 1, :], ALU.subtract).then_inc(parts_ready, 1)

        @block.scalar
        def _(act):
            norm_scalar(act, hn[:, :, :], sq[:, :, :], st, steps, 1)
            act.wait_ge(loaded, LOADS * 16)
            order_weights(act, wq, wq_raw, w_ordered)
            act.wait_ge(hn_transposed, 1)
            act.activation(hT[:, :], g.ps[:, 4 * BANK:8 * BANK], ACT.Copy).then_inc(hT_ready, 1)

        @block.tensor
        def _(pe):
            pe.wait_ge(hn_ready, 1)
            transpose_tokens(g, pe, hn, 4 * BANK, hn_transposed)
            pe.wait_ge(hT_ready, 1)
            pe.wait_ge(loaded, LOADS * 16)
            pe.wait_ge(w_ordered, QUADS)
            for i in range(4):
                last = pe.matmul(g.ps[:, i * BANK:(i + 1) * BANK], wq[:, :], hT[:, i * BANK:(i + 1) * BANK],
                                 start=True, stop=True)
            last.then_inc(q_product, 1)


def narrow_keys(nc, g, d, name, kd, vd, dh, quads):
    with ExitStack() as ctx:
        s = Stage(nc, ctx, g.sems, name + "_kv")
        wk_raw = s.sb("wk_raw", [P, P])
        wk = s.sb("wk", [P, P])
        wv = s.sb("wv", [P, P])
        bk = s.sb("bk", [P, 1])
        keys = [s.sb(f"keys{i}", [P, KEYS]) for i in range(2)]
        rest = [s.sb(f"rest{i}", [P, KEYS]) for i in range(2)]
        parts = [s.sb(f"parts{i}", [P, 3, KEYS], BF16) for i in range(2)]
        values = [s.sb(f"values{i}", [P, KT, HEADS, dh + 1]) for i in range(2)]
        loaded, ones_made = s.sem("loaded"), s.sem("ones_made")
        k_product, k_ready, high_ready = s.sem("k_product"), s.sem("k_ready"), s.sem("high_ready")
        rest_ready, middle_ready, parts_ready = s.sem("rest_ready"), s.sem("middle_ready"), s.sem("parts_ready")
        v_product, v_ready = s.sem("v_product"), s.sem("v_ready")
        k_stored = [s.sem(f"k_stored{i}") for i in range(2)]
        v_stored = [s.sem(f"v_stored{i}") for i in range(2)]
        ps = g.ps
        V = 4 * BANK
        whole = KT - 1
        w_ordered = s.sem("w_ordered")
        LOADS = 2 + QUADS
        block = ctx.enter_context(nc.Block())

        @block.sync
        def _(sp):
            sp.dma_start(wk_raw[:, :], d[name + "_w_k"]).then_inc(loaded, 16)
            sp.dma_start(wv[:, :], d[name + "_w_v"]).then_inc(loaded, 16)
            load_ordered_bias(sp, bk, d[name + "_b_k"], loaded)
            for b in range(BATCHES):
                k = b % 2
                sp.wait_ge(v_ready, b + 1)
                sp.dma_start(vd[b], values[k][:, :, :, :].rearrange("p t h e -> p (t h e)")).then_inc(v_stored[k], 16)
                for i, ready in enumerate((high_ready, middle_ready, parts_ready)):
                    sp.wait_ge(ready, b + 1)
                    sp.dma_start(kd[i, b], parts[k][:, i, :]).then_inc(k_stored[k], 16)
                if b == BATCHES - 3:
                    sp.wait_ge(quads.cleared, 2 * QUADS + 1)
                    sp.wait_ge(v_stored[0], 16)
                    sp.wait_ge(k_stored[0], 3 * 16)
                    quads.load(sp, 0, 0)
            for k in range(2):
                sp.wait_ge(v_stored[k], 16 * BATCHES // 2)
                sp.wait_ge(k_stored[k], 3 * 16 * BATCHES // 2)

        @block.gpsimd
        def _(pool):
            for k in range(2):
                pool.memset(values[k][:, :, :, :], 1.0).then_inc(ones_made, 1)
            pool.memset(quads.zeros[:, :, :, :], 0.0).then_inc(quads.cleared, 1)
            for b in range(BATCHES):
                k = b % 2
                pool.wait_ge(high_ready, b + 1)
                wait(pool, parts_ready, b - 1)
                pool.tensor_tensor(rest[k][:, :], keys[k][:, :], parts[k][:, 0, :], ALU.subtract)\
                    .then_inc(rest_ready, 1)

        @block.vector
        def _(dve):
            def high(b):
                k = b % 2
                dve.wait_ge(k_ready, b + 1)
                wait(dve, k_stored[k], 3 * 16 * (b // 2))
                dve.tensor_copy(parts[k][:, 0, :], keys[k][:, :]).then_inc(high_ready, 1)

            high(0)
            for b in range(BATCHES):
                k = b % 2
                if b + 1 < BATCHES:
                    high(b + 1)
                dve.wait_ge(rest_ready, b + 1)
                dve.tensor_copy(parts[k][:, 1, :], rest[k][:, :]).then_inc(middle_ready, 1)
                dve.wait_ge(middle_ready, b + 1)
                dve.tensor_tensor(parts[k][:, 2, :], rest[k][:, :], parts[k][:, 1, :], ALU.subtract)\
                    .then_inc(parts_ready, 1)
                if b < QUADS:
                    quads.clear(dve, b)

        @block.scalar
        def _(act):
            act.wait_ge(loaded, LOADS * 16)
            order_weights(act, wk, wk_raw, w_ordered)
            act.wait_ge(ones_made, 2)
            for b in range(BATCHES):
                k = b % 2
                act.wait_ge(k_product, b + 1)
                wait(act, rest_ready, b - 1)
                act.activation(keys[k][:, 0:401], ps[:, 0:401], ACT.Identity, bias=bk[:, 0:1])
                act.activation(keys[k][:, 401:KEYS].rearrange("p (a n) -> p a n", n=400),
                               ps[:, BANK:4 * BANK].rearrange("p (a n) -> p a n", n=BANK)[:, :, 0:400], ACT.Identity,
                               bias=bk[:, 0:1]).then_inc(k_ready, 1)
                act.wait_ge(v_product, b + 1)
                wait(act, v_stored[k], 16 * (b // 2))
                act.activation(values[k][:, 0:whole, :, 0:dh],
                               ps[:, V:V + whole * P].rearrange("p (t h e) -> p t h e", h=HEADS, e=dh), ACT.Copy)
                act.activation(values[k][0:TAIL, whole, :, 0:dh],
                               ps[0:TAIL, V + whole * P:V + KT * P].rearrange("p (h e) -> p h e", e=dh), ACT.Copy)\
                    .then_inc(v_ready, 1)

        @block.tensor
        def _(pe):
            pe.wait_ge(loaded, LOADS * 16)
            pe.wait_ge(w_ordered, QUADS)
            for b in range(BATCHES):
                wait(pe, k_ready, b)
                for i, (c, w) in enumerate(SPLIT):
                    last = pe.matmul(ps[:, i * BANK:i * BANK + w], wk[:, :], g.ctxT[:, b, c:c + w], start=True, stop=True)
                last.then_inc(k_product, 1)
                wait(pe, v_ready, b)
                for t in range(KT):
                    rows = P if t < whole else TAIL
                    last = pe.matmul(ps[0:rows, V + t * P:V + (t + 1) * P], g.ctxT[:, b, t * P:t * P + rows], wv[:, :],
                                     start=True, stop=True)
                last.then_inc(v_product, 1)


def narrow_heads(nc, g, name, quads, heads_out, dh):
    with ExitStack() as ctx:
        s = Stage(nc, ctx, g.sems, name + "_heads")
        kstack, qstack, values, loaded = quads.kstack, quads.qstack, quads.values, quads.loaded
        probsT = [s.sb(f"probsT{i}", [P, 2, PAIR]) for i in range(PROBS_RING)]
        peaks = [s.sb(f"peaks{i}", [P, 4, 2]) for i in range(2)]
        peak = s.sb("peak", [P, 4])
        rest = s.sb("rest", [P, 4])
        lows = [s.sb(f"lows{i}", [P, 2, P], BF16) for i in range(2)]
        mixed = s.sb("mixed", [P, 2 * P])
        inverse = s.sb("inverse", [P, 2, 4])
        chunk_ready, chunk_taken = s.sem("chunk_ready"), s.sem("chunk_taken")
        lows_ready, rows_product = s.sem("lows_ready"), s.sem("rows_product")
        upper_copied, lower_copied = s.sem("upper_copied"), s.sem("lower_copied")
        score_ready, exp_done, tile_mixed = s.sem("score_ready"), s.sem("exp_done"), s.sem("tile_mixed")
        mix_copied, mix_turned, mix_divided = s.sem("mix_copied"), s.sem("mix_turned"), s.sem("mix_divided")
        max_step, inverse_ready = s.sem("max_step"), s.sem("inverse_ready")
        bank_cleared, lows_cleared = s.sem("bank_cleared"), s.sem("lows_cleared")
        ps = g.ps
        half = [ps[:, 2 * i * BANK:(2 * i + 2) * BANK].rearrange("p (a n) -> p a n", n=BANK) for i in range(2)]
        score = [ps[:, (4 + i) * BANK:(5 + i) * BANK] for i in range(SCORE_RING)]
        mix = ps[:, 7 * BANK:7 * BANK + 2 * P]
        side = ps[:, 6 * BANK:6 * BANK + 2 * P]
        QN = BATCHES * QUADS
        STEPS = 2 * KT
        out_f = heads_out[:, :, :].rearrange("p t c -> p (t c)")
        block = ctx.enter_context(nc.Block())

        def walk(eng, stream):
            for j in range(QUADS):
                stream(0, j)
            with eng.Fori(1, BATCHES - 1) as b:
                for j in range(QUADS):
                    stream(b, j)
            for j in range(QUADS):
                stream(BATCHES - 1, j)

        def is_last(b, j, ahead):
            return isinstance(b, int) and b * QUADS + j + ahead >= QN

        @block.gpsimd
        def _(pool):
            for i in range(2):
                pool.memset(lows[i][:, :, :], 0.0).then_inc(lows_cleared, 1)

        @block.sync
        def _(sp):
            def stream(b, j):
                if not (isinstance(b, int) and b == 0):
                    sp.wait_ge(tile_mixed, (b * QUADS + j - QUADS + 1) * KT)
                elif j == 0:
                    return
                quads.load(sp, b, j)

            walk(sp, stream)

        @block.tensor
        def _(pe):
            def chunk(m, j, r, c):
                i, q, side_half = c // 4, c // 2 % 2, c % 2
                wait(pe, chunk_taken, m * 8 + c - 1)
                for a in range(2):
                    k0 = (2 * side_half + a) * (WINDOW_KEYS - 1)
                    ins = pe.matmul(half[c % 2][:, a, 0:WINDOW_KEYS], qstack[j][:, i, r, q * P:(q + 1) * P],
                                    kstack[j][:, r, k0:k0 + WINDOW_KEYS], start=True, stop=True)
                ins.then_inc(chunk_ready, 1)

            def first_loads(b, j):
                pe.wait_ge(loaded[j], (b + 1) * (16 * quads.LOADS))

            def mix_tile(n, j, t):
                if t == 0:
                    wait(pe, mix_copied, n)
                pe.wait_ge(exp_done, n * STEPS + 2 * t + 2)
                rows_ = P if t < KT - 1 else TAIL
                for h in range(4):
                    ins = pe.matmul(mix[32 * h:32 * h + dh + 1, :], values[j][0:rows_, t, h, :],
                                    probsT[(j * KT + t) % PROBS_RING][0:rows_, h // 2, (h % 2) * 2 * P:(h % 2 + 1) * 2 * P],
                                    start=(t == 0), stop=(t == KT - 1), tile_position=(0, 32 * h))
                ins.then_inc(tile_mixed, 1)

            def turn(n):
                pe.wait_ge(mix_copied, n + 1)
                wait(pe, mix_divided, n)
                for q in range(2):
                    ins = pe.transpose(side[:, q * P:(q + 1) * P], mixed[:, q * P:(q + 1) * P], g.ident[:, :])
                ins.then_inc(mix_turned, 1)

            def stream(b, j):
                n = b * QUADS + j
                taken = 0
                for t in range(KT):
                    for r in range(2):
                        i = 2 * t + r
                        if t == 0:
                            pe.wait_ge(upper_copied, n * 2 + r + 1)
                            pe.wait_ge(lower_copied, n * 2 + r + 1)
                        wait(pe, exp_done, n * STEPS + i - SCORE_RING + 1)
                        rows_ = P if t < KT - 1 else TAIL
                        pe.matmul(score[i % SCORE_RING][0:rows_, :], kstack[j][:, r, t * P:t * P + rows_], qstack[j][:, :, r, :],
                                  start=True, stop=True).then_inc(score_ready, 1)
                        if r == 0 or t in (2, 6, 10):
                            if taken < 8 and not is_last(b, j, 1):
                                chunk(2 * n + 3, (j + 1) % QUADS, 1, taken)
                            if taken >= 8 and not is_last(b, j, 2):
                                if taken == 8:
                                    first_loads(b + (j + 2) // QUADS, (j + 2) % QUADS)
                                chunk(2 * n + 4, (j + 2) % QUADS, 0, taken - 8)
                            taken += 1
                    if t >= LAG:
                        mix_tile(n, j, t - LAG)
                    elif not (isinstance(b, int) and n == 0):
                        mix_tile(n - 1, (j - 1) % QUADS, KT - LAG + t)
                    if t == 2 and not (isinstance(b, int) and n == 0):
                        turn(n - 1)
                    if t == 4 and not is_last(b, j, 1):
                        wait(pe, mix_divided, n)
                        rows_at(2 * n + 2, 0)
                    if t == 10 and not is_last(b, j, 1):
                        pe.wait_ge(upper_copied, 2 * n + 3)
                        pe.wait_ge(lower_copied, 2 * n + 3)
                        rows_at(2 * n + 3, 1)

            def rows_at(m, parity):
                pe.wait_ge(lows_ready, m + 1)
                for q in range(2):
                    ins = pe.matmul(side[:, q * P:(q + 1) * P], lows[parity][:, q, :], g.identb[:, :], start=True, stop=True)
                ins.then_inc(rows_product, 1)

            pe.wait_ge(bank_cleared, 1)
            first_loads(0, 0)
            for c in range(8):
                chunk(0, 0, 0, c)
            for c in range(8):
                chunk(1, 0, 1, c)
            rows_at(0, 0)
            first_loads(0, 1)
            for c in range(8):
                chunk(2, 1, 0, c)
            pe.wait_ge(upper_copied, 1)
            pe.wait_ge(lower_copied, 1)
            rows_at(1, 1)
            walk(pe, stream)
            for t in range(KT - LAG, KT):
                mix_tile(QN - 1, QUADS - 1, t)
            turn(QN - 1)

        @block.scalar
        def _(act):
            def copy_lower(m, j, r):
                act.wait_ge(rows_product, m + 1)
                act.activation(qstack[j][64:64 + SHIFT_ROWS, 1, r, :], side[64:64 + SHIFT_ROWS, :], ACT.Copy)\
                    .then_inc(lower_copied, 1)

            def copy_mix(n):
                act.wait_ge(tile_mixed, (n + 1) * KT)
                wait(act, mix_turned, n)
                act.activation(mixed[:, :], mix, ACT.Copy).then_inc(mix_copied, 1)

            def stream(b, j):
                n = b * QUADS + j
                for t in range(KT):
                    for r in range(2):
                        i = 2 * t + r
                        rows_ = P if t < KT - 1 else TAIL
                        act.wait_ge(score_ready, n * STEPS + i + 1)
                        if r == 0:
                            wait(act, tile_mixed, n * KT + t - PROBS_RING + 1)
                        act.activation(probsT[(j * KT + t) % PROBS_RING][0:rows_, r, :], score[i % SCORE_RING][0:rows_, :], ACT.Exp)\
                            .then_inc(exp_done, 1)
                    if t == 1 and not (isinstance(b, int) and n == 0):
                        copy_mix(n - 1)
                    if t == 5 and not is_last(b, j, 1):
                        copy_lower(2 * n + 2, (j + 1) % QUADS, 0)
                    if t == 11 and not is_last(b, j, 1):
                        copy_lower(2 * n + 3, (j + 1) % QUADS, 1)

            copy_lower(0, 0, 0)
            copy_lower(1, 0, 1)
            walk(act, stream)
            copy_mix(QN - 1)

        @block.vector
        def _(dve):
            dve.memset(mix, 0.0).then_inc(bank_cleared, 1)

            def chunk(m, parity, c):
                i, q = c // 4, c // 2 % 2
                dve.wait_ge(chunk_ready, m * 8 + c + 1)
                dve.tensor_reduce(peaks[parity][:, 2 * q + i, c % 2:c % 2 + 1], half[c % 2][:, :, 0:WINDOW_KEYS], AX.XY,
                                  ALU.max).then_inc(chunk_taken, 1)

            dve.wait_ge(lows_cleared, 2)

            def maxima(m, parity, steps=range(5)):
                low = lows[parity]
                pk = peak[:, :].rearrange("p (q i) -> p q i", i=2)
                rs = rest[:, :].rearrange("p (q i) -> p q i", i=2)

                def part(i):
                    return low[:, :, i:P:64]

                for step in steps:
                    if step == 0:
                        dve.wait_ge(chunk_taken, m * 8 + 8)
                        wait(dve, lows_ready, m)
                        dve.tensor_tensor(peak[:, :], peaks[parity][:, :, 0], peaks[parity][:, :, 1], ALU.max)\
                            .then_inc(max_step, 1)
                        continue
                    dve.wait_ge(max_step, m * 4 + step)
                    if step == 1:
                        wait(dve, rows_product, m - 1)
                        dve.tensor_scalar(part(0), pk, -1.0, None, ALU.mult).then_inc(max_step, 1)
                    elif step == 2:
                        dve.scalar_tensor_tensor(out=rs, in0=pk, scalar=-1.0, in1=part(0), op0=ALU.mult,
                                                 op1=ALU.subtract).then_inc(max_step, 1)
                    elif step == 3:
                        dve.tensor_copy(part(1), rs).then_inc(max_step, 1)
                    else:
                        dve.tensor_tensor(part(2), rs, part(1), ALU.subtract).then_inc(lows_ready, 1)

            def copy_upper(m, j, r):
                dve.wait_ge(rows_product, m + 1)
                dve.tensor_copy(qstack[j][0:SHIFT_ROWS, 0, r, :], side[0:SHIFT_ROWS, :]).then_inc(upper_copied, 1)

            def divide(n, b, j):
                dve.wait_ge(mix_turned, n + 1)
                turned = side.rearrange("p (q h e) -> p q h e", q=2, h=4)
                dve.reciprocal(inverse[:, :, :], turned[:, :, :, dh]).then_inc(inverse_ready, 1)
                dve.wait_ge(inverse_ready, n + 1)
                for q in range(2):
                    ins = dve.tensor_tensor(
                        out_f[:, bass.ds((b * 2 + q) * P + 4 * j * dh, 4 * dh)].rearrange("p (h e) -> p h e", e=dh),
                        turned[:, q, :, 0:dh], inverse[:, q, :].unsqueeze(2).to_broadcast([P, 4, dh]), ALU.mult)
                ins.then_inc(mix_divided, 1)

            def stream(b, j):
                n = b * QUADS + j
                for c in range(CHUNKS):
                    if c < 8 and not is_last(b, j, 1):
                        chunk(2 * n + 3, 1, c)
                    if c >= 8 and not is_last(b, j, 2):
                        chunk(2 * n + 4, 0, c - 8)
                    if c == 4 and not (isinstance(b, int) and n == 0):
                        divide(n - 1, b if j else b - 1, (j - 1) % QUADS)
                    if c == 8 and not is_last(b, j, 1):
                        copy_upper(2 * n + 2, (j + 1) % QUADS, 0)
                    if 7 <= c < 12 and not is_last(b, j, 1):
                        maxima(2 * n + 3, 1, (c - 7,))
                    if c < 4 and not is_last(b, j, 1):
                        maxima(2 * n + 2, 0, (c + 1,))
                    if c == 14 and not is_last(b, j, 1):
                        copy_upper(2 * n + 3, (j + 1) % QUADS, 1)
                    if c == 15 and not is_last(b, j, 2):
                        maxima(2 * n + 4, 0, (0,))

            for c in range(8):
                chunk(0, 0, c)
            maxima(0, 0)
            for c in range(8):
                chunk(1, 1, c)
            copy_upper(0, 0, 0)
            maxima(1, 1)
            for c in range(8):
                chunk(2, 0, c)
            copy_upper(1, 0, 1)
            maxima(2, 0, (0,))
            walk(dve, stream)
            divide(QN - 1, BATCHES - 1, QUADS - 1)


def reshuffled_output(nc, g, name, heads_out, wo, bv, dh):
    shuffle = nc.dram_tensor(name + "_shuffle", (BATCHES, HEADS, 2, P, dh), F32, kind="Internal").ap()
    with ExitStack() as ctx:
        s = Stage(nc, ctx, g.sems, name + "_out")
        rows = s.sb("rows", [P, TILES, P])
        rowsT = s.sb("rowsT", [P, TILES * P])
        wo_sb = s.sb("wo", [P, P])
        bv_rows = s.sb("bv_rows", [P, P])
        biased = s.sem("biased")
        spread, gathered, w_loaded = s.sem("spread"), s.sem("gathered"), s.sem("w_loaded")
        rows_transposed, rowsT_ready, product_done = s.sem("rows_transposed"), s.sem("rowsT_ready"), s.sem("product_done")
        block = ctx.enter_context(nc.Block())

        @block.sync
        def _(sp):
            sp.dma_start(bv_rows[:, :], bv.partition_broadcast(P)).then_inc(w_loaded, 16)
            sp.dma_start(wo_sb[:, :], wo).then_inc(w_loaded, 16)
            sp.wait_ge(biased, 1)
            for b in range(BATCHES):
                for q in range(2):
                    sp.dma_start(shuffle[b, :, q].rearrange("h p e -> p h e"),
                                 heads_out[:, 2 * b + q, :].rearrange("p (h e) -> p h e", e=dh)).then_inc(spread, 16)
            sp.wait_ge(spread, 16 * TILES)
            sp.dma_start(rows[:, :, :], shuffle.rearrange("b h q p e -> (b h q p e)").rearrange("(t p c) -> p t c", p=P, c=P))\
                .then_inc(gathered, 16)

        @block.tensor
        def _(pe):
            pe.wait_ge(gathered, 16)
            transpose_tokens(g, pe, rows, 0, rows_transposed)
            pe.wait_ge(rowsT_ready, 1)
            pe.wait_ge(w_loaded, 32)
            for t in range(TILES):
                last = pe.matmul(g.ps[:, (TILES + t) * P:(TILES + t + 1) * P], rowsT[:, t * P:(t + 1) * P], wo_sb[:, :],
                                 start=True, stop=True)
            last.then_inc(product_done, 1)

        @block.scalar
        def _(act):
            act.wait_ge(rows_transposed, 1)
            act.activation(rowsT[:, :], g.ps[:, 0:TILES * P], ACT.Copy).then_inc(rowsT_ready, 1)

        @block.vector
        def _(dve):
            dve.wait_ge(w_loaded, 32)
            dve.tensor_tensor(heads_out[:, :, :], heads_out[:, :, :],
                              bv_rows[:, :].unsqueeze(1).to_broadcast([P, TILES, P]), ALU.add).then_inc(biased, 1)
            dve.wait_ge(product_done, 1)
            dve.tensor_tensor(g.x[:, :, :], g.x[:, :, :],
                              g.ps[:, TILES * P:2 * TILES * P].rearrange("p (t c) -> p t c", c=P), ALU.add)


SLOTS = 8
SPAN = 3 * P


def slot_scores(pe, g, mask, i, q_tile, k_tiles):
    c = i * BANK
    pe.matmul(g.ps[:, c:c + SPAN], g.identb[:, :], mask[:, :], start=True, stop=False, skip_group_check=True)
    pe.matmul(g.ps[:, c:c + P], q_tile(0), k_tiles(1), start=False, stop=False, skip_group_check=True)
    return pe.matmul(g.ps[:, c + P:c + SPAN], q_tile(1), k_tiles(2), start=False, stop=True, skip_group_check=True)


def slot_peaks(dve, g, half, peaks):
    banks = g.ps[:, half * 4 * BANK:(half + 1) * 4 * BANK].rearrange("p (i n) -> p i n", n=BANK)
    s = slice(4 * half, 4 * half + 4)
    dve.tensor_reduce(peaks[:, 0, s], banks[:, :, 0:P], AX.X, ALU.max, negate=True)
    return dve.tensor_reduce(peaks[:, 1, s], banks[:, :, P:SPAN], AX.X, ALU.max, negate=True)


def slot_exps(act, g, i, probs, peaks, sums, scale):
    c = i * BANK
    act.activation(probs[:, i, 0:P], g.ps[:, c:c + P], ACT.Exp, bias=peaks[:, 0, i:i + 1], scale=scale(0),
                   accum_out=sums[:, 0, i:i + 1])
    return act.activation(probs[:, i, P:SPAN], g.ps[:, c + P:c + SPAN], ACT.Exp, bias=peaks[:, 1, i:i + 1],
                          scale=scale(1), accum_out=sums[:, 1, i:i + 1])


def slot_normalize(dve, half, probs, inverse):
    s = slice(4 * half, 4 * half + 4)
    dve.tensor_tensor(probs[:, s, 0:P], probs[:, s, 0:P], inverse[:, 0, s].unsqueeze(2).to_broadcast([P, 4, P]),
                      ALU.mult)
    return dve.tensor_tensor(probs[:, s, P:SPAN], probs[:, s, P:SPAN],
                             inverse[:, 1, s].unsqueeze(2).to_broadcast([P, 4, 2 * P]), ALU.mult)


def slot_transposes(pe, g, i, probs):
    c = (6 + i % 2) * BANK
    for j in range(3):
        ins = pe.transpose(g.ps[:, c + j * P:c + (j + 1) * P], probs[:, i, j * P:(j + 1) * P], g.ident[:, :])
    return ins


def slot_mix(pe, out, value, i, probsT, **tile):
    pe.matmul(out, value(0), probsT[:, i, 0:2 * P], start=True, stop=False, skip_group_check=True, **tile)
    return pe.matmul(out[:, P:2 * P], value(1), probsT[:, i, 2 * P:SPAN], start=False, stop=True,
                     skip_group_check=True, **tile)


LHEADS = 8
LDIM = 64
INNER = LHEADS * LDIM
SEQ = 2 * P
TOKENS = BATCHES * SEQ


def local_stage(nc, g, d):
    with ExitStack() as ctx:
        s = Stage(nc, ctx, g.sems, "local")
        yT = s.sb("yT", [P, TOKENS])
        norm_to_channels(nc, g, "local_norm", yT)
        for layer in range(2):
            local_attention(nc, g, d, yT, layer)
            local_mlp(nc, g, d, yT, layer)
        channels_to_x(nc, g, "local_end", yT)


def norm_to_channels(nc, g, name, dst):
    with ExitStack() as ctx:
        s = Stage(nc, ctx, g.sems, name)
        hn = s.sb("hn", [P, TILES, P])
        sq = s.sb("sq", [P, TILES, P])
        st = s.sb("st", [P, 3, TILES])
        steps = NormSteps(s)
        hn_ready, transposed, order_sem = s.sem("hn_ready"), s.sem("transposed"), s.sem("dve_order")
        block = ctx.enter_context(nc.Block())

        @block.vector
        def _(dve):
            order = Order(dve, order_sem)
            norm_vector(dve, order, g.x[:, :, :], hn[:, :, :], sq[:, :, :], st, steps, 1)
            dve.sem_inc(hn_ready, 1)

        @block.scalar
        def _(act):
            norm_scalar(act, hn[:, :, :], sq[:, :, :], st, steps, 1)
            act.wait_ge(transposed, 1)
            act.activation(dst[:, :], g.ps[:, 0:TOKENS], ACT.Copy)

        @block.tensor
        def _(pe):
            pe.wait_ge(hn_ready, 1)
            transpose_tokens(g, pe, hn, 0, transposed)


def channels_to_x(nc, g, name, src):
    with ExitStack() as ctx:
        s = Stage(nc, ctx, g.sems, name)
        transposed = s.sem("transposed")
        block = ctx.enter_context(nc.Block())

        @block.tensor
        def _(pe):
            for t in range(TILES):
                last = pe.transpose(g.ps[:, t * P:(t + 1) * P], src[:, t * P:(t + 1) * P], g.ident[:, :])
            last.then_inc(transposed, 1)

        @block.vector
        def _(dve):
            dve.wait_ge(transposed, 1)
            dve.tensor_tensor(g.x[:, :, :], g.x[:, :, :], g.ps[:, 0:TOKENS].rearrange("p (t c) -> p t c", c=P), ALU.add)


def local_attention(nc, g, d, yT, layer):
    with ExitStack() as ctx:
        s = Stage(nc, ctx, g.sems, f"local{layer}")
        wqkv = s.sb("wqkv", [P, 3 * INNER])
        wo = s.sb("wo", [P, INNER // P, P])
        rotary = s.sb("rotary", [P, 4, 2, LDIM])
        turned = s.sb("turned", [P, 4, 2, LDIM])
        scales = s.sb("scales", [P, 2, LDIM])
        shifted = [s.sb(f"shifted{i}", [P, SEQ]) for i in range(2)]
        qk = s.sb("qk", [P, 4, LHEADS, LDIM])
        value = [s.sb(f"value{i}", [P, 2, INNER]) for i in range(2)]
        squares = s.sb("squares", [P, 4, LHEADS, LDIM])
        norm = s.sb("norm", [P, 4, LHEADS])
        rnorm = s.sb("rnorm", [P, 4, LHEADS])
        q_gain = [s.sb(f"q_gain{i}", [P, 2, LHEADS]) for i in range(2)]
        part = s.sb("part", [P, 4, LHEADS, LDIM])
        turn = s.sb("turn", [P, 4, LHEADS, LDIM])
        qT = s.sb("qT", [P, 4, SEQ])
        kT = s.sb("kT", [P, 4, SEQ])
        peaks = s.sb("peaks", [P, 2, SLOTS])
        shifts = s.sb("shifts", [P, 2, SLOTS])
        sums = s.sb("sums", [P, 2, SLOTS])
        inverse = s.sb("inverse", [P, 2, SLOTS])
        probs = s.sb("probs", [P, SLOTS, SPAN])
        probsT = s.sb("probsT", [P, SLOTS, SPAN])
        oT = s.sb("oT", [P, 4, SEQ])
        names = ("loaded edge_zeroed turned_ready shifted_ready q_product k_product v_product q_taken k_taken "
                 "v_taken q_squares k_squares squared_sums norm_ready clamped rnorm_ready gain_ready q_part "
                 "q_turned k_part k_turned q_transposed k_transposed qT_ready kT_ready scores_ready peaks_ready "
                 "shifts_ready exp_done inverse_ready normalized mixed mix_taken out_product out_added "
                 "pool_order").split()
        m = {n: s.sem(n) for n in names}
        transposed = [s.sem(f"transposed{i}") for i in range(2)]
        probsT_copied = [s.sem(f"probsT_copied{i}") for i in range(2)]
        ps = g.ps
        even, odd = (ps[:, i * BANK:(i + 1) * BANK] for i in (4, 5))
        front_ps = ps[:, 6 * BANK:8 * BANK]
        block = ctx.enter_context(nc.Block())
        LOADS = 3 + 4

        @block.sync
        def _(sp):
            sp.dma_start(wqkv[:, :], d["L0_ffn_wqkv"][layer]).then_inc(m["loaded"], 16)
            sp.dma_start(wo[:, :, :], d["L0_ffn_wo"][layer].rearrange("(j p) c -> p j c", p=P)).then_inc(m["loaded"], 16)
            for i in range(4):
                sp.dma_start(rotary[:, i, :, :], d["rotary"][i].rearrange("(t p) e -> p t e", p=P)).then_inc(m["loaded"], 16)
            sp.dma_start(scales[:, 0, :], d["L0_ffn_q_scale"][layer].partition_broadcast(P)).then_inc(m["loaded"], 16)
            sp.dma_start(scales[:, 1, :], d["L0_ffn_k_scale"][layer].partition_broadcast(P)).then_inc(m["loaded"], 16)

        def walk(eng, window):
            def pair(b):
                for k in range(2):
                    for half in range(2):
                        window(b + k, half, k)

            pair(0)
            with eng.Fori(1, BATCHES // 2 - 1) as two:
                pair(two * 2)
            pair(BATCHES - 2)

        def has(b, ahead):
            return not isinstance(b, int) or 0 <= b + ahead < BATCHES

        @block.gpsimd
        def _(pool):
            order = Order(pool, m["pool_order"])
            for k in range(2):
                order.done(pool.memset(shifted[k][64:P, 0:1], 0.0))
            pool.sem_inc(m["edge_zeroed"], 1)
            pool.wait_ge(m["loaded"], 16 * (LOADS + 1))
            half = LDIM // 2
            for i in range(2):
                full = scales[:, i, :].unsqueeze(1).to_broadcast([P, 2, LDIM])
                order.done(pool.tensor_tensor(turned[:, 2 * i], rotary[:, 2 * i], full, ALU.mult))
                for a, b in ((0, half), (half, 0)):
                    order.done(pool.tensor_tensor(turned[:, 2 * i + 1, :, a:a + half],
                                                  rotary[:, 2 * i + 1, :, a:a + half],
                                                  scales[:, i, b:b + half].unsqueeze(1).to_broadcast([P, 2, half]),
                                                  ALU.mult))
            pool.sem_inc(m["turned_ready"], 1)

            def front(b):
                pool.wait_ge(m["k_taken"], b + 1)
                wait(pool, m["k_transposed"], b)
                k, t = qk[:, 2:4], turned[:, 2].unsqueeze(2)
                pool.tensor_tensor(turn[:, 2:4], k, t.to_broadcast([P, 2, LHEADS, LDIM]), ALU.mult)
                for a, c in ((0, half), (half, 0)):
                    ins = pool.tensor_tensor(part[:, 2:4, :, a:a + half], k[:, :, :, c:c + half],
                                             turned[:, 3, :, a:a + half].unsqueeze(2)
                                             .to_broadcast([P, 2, LHEADS, half]), ALU.mult)
                ins.then_inc(m["k_part"], 1)
                pool.wait_ge(m["k_part"], b * 2 + 1)
                pool.tensor_tensor(turn[:, 2:4], turn[:, 2:4], part[:, 2:4], ALU.add).then_inc(m["k_part"], 1)
                pool.wait_ge(m["k_part"], b * 2 + 2)
                pool.wait_ge(m["rnorm_ready"], b + 1)
                pool.tensor_tensor(turn[:, 2:4], turn[:, 2:4],
                                   rnorm[:, 2:4, :].unsqueeze(3).to_broadcast([P, 2, LHEADS, LDIM]), ALU.mult)\
                    .then_inc(m["k_turned"], 1)

            front(0)
            with pool.Fori(1, BATCHES) as b:
                front(b)

        @block.vector
        def _(dve):
            half = LDIM // 2
            dve.wait_ge(m["turned_ready"], 1)

            def turn_queries(b):
                dve.wait_ge(m["q_taken"], b + 1)
                wait(dve, m["q_transposed"], b)
                q = qk[:, 0:2]
                dve.tensor_tensor(turn[:, 0:2], q, turned[:, 0].unsqueeze(2).to_broadcast([P, 2, LHEADS, LDIM]),
                                  ALU.mult)
                for a, c in ((0, half), (half, 0)):
                    ins = dve.tensor_tensor(part[:, 0:2, :, a:a + half], q[:, :, :, c:c + half],
                                            turned[:, 1, :, a:a + half].unsqueeze(2)
                                            .to_broadcast([P, 2, LHEADS, half]), ALU.mult)
                ins.then_inc(m["q_part"], 1)
                dve.wait_ge(m["q_part"], b + 1)
                dve.tensor_tensor(turn[:, 0:2], turn[:, 0:2], part[:, 0:2], ALU.add).then_inc(m["q_turned"], 1)

            def sum_squares(b, i, name):
                dve.wait_ge(m[name], b + 1)
                wait(dve, m["gain_ready"], b)
                dve.tensor_reduce(norm[:, i:i + 2, :], squares[:, i:i + 2, :, :], AX.X, ALU.add)\
                    .then_inc(m["squared_sums"], 1)

            def gains(b, k):
                dve.wait_ge(m["norm_ready"], b + 1)
                dve.tensor_scalar(norm[:, :, :], norm[:, :, :], 1e-12, None, ALU.max).then_inc(m["clamped"], 1)
                dve.wait_ge(m["clamped"], b + 1)
                wait(dve, m["k_turned"], b)
                dve.reciprocal(rnorm[:, :, :], norm[:, :, :]).then_inc(m["rnorm_ready"], 1)
                dve.wait_ge(m["rnorm_ready"], b + 1)
                dve.tensor_scalar(q_gain[k][:, :, :], rnorm[:, 0:2, :], 8.0, None, ALU.mult).then_inc(m["gain_ready"], 1)

            def take_keys(b):
                dve.wait_ge(m["k_transposed"], b + 1)
                dve.tensor_copy(kT[:, :, :], front_ps.rearrange("p (j n) -> p j n", n=SEQ)).then_inc(m["kT_ready"], 1)

            def maxima(b, hf, k):
                u = b * 2 + hf
                for i in range(2):
                    dve.wait_ge(m["scores_ready"], u * 2 + i + 1)
                    c = slice(4 * hf + 2 * i, 4 * hf + 2 * i + 2)
                    banks = ps[:, 2 * i * BANK:(2 * i + 2) * BANK].rearrange("p (i n) -> p i n", n=BANK)
                    dve.tensor_reduce(peaks[:, 0, c], banks[:, :, 0:P], AX.X, ALU.max, negate=True)
                    dve.tensor_reduce(peaks[:, 1, c], banks[:, :, P:SPAN], AX.X, ALU.max, negate=True)\
                        .then_inc(m["peaks_ready"], 1)
                    dve.wait_ge(m["peaks_ready"], u * 2 + i + 1)
                    dve.wait_ge(m["gain_ready"], b + 1)
                    dve.tensor_tensor(shifts[:, :, c], peaks[:, :, c], q_gain[k][:, :, c], ALU.mult)\
                        .then_inc(m["shifts_ready"], 1)

            def normalize(b, hf):
                u = b * 2 + hf
                dve.wait_ge(m["exp_done"], u * 4 + 4)
                h = slice(4 * hf, 4 * hf + 4)
                dve.reciprocal(inverse[:, :, h], sums[:, :, h]).then_inc(m["inverse_ready"], 1)
                dve.wait_ge(m["inverse_ready"], u + 1)
                slot_normalize(dve, hf, probs, inverse).then_inc(m["normalized"], 1)

            def take_odd(b, hf, slots=(0, 1)):
                u = b * 2 + hf
                wait(dve, m["mixed"], u - 1)
                for i in slots:
                    dve.wait_ge(transposed[1], u * 2 + i + 1)
                    dve.tensor_copy(probsT[:, 4 * hf + 2 * i + 1, :], odd[:, 0:SPAN]).then_inc(probsT_copied[1], 1)

            def add_output(b):
                dve.wait_ge(m["out_product"], b + 1)
                cols = yT[:, bass.ds(b * SEQ, SEQ)]
                dve.tensor_tensor(cols, cols, odd[:, 0:SEQ], ALU.add).then_inc(m["out_added"], 1)

            def window(b, hf, k):
                if hf == 0:
                    maxima(b, 0, k)
                    if has(b, -1):
                        take_odd(b - 1, 1)
                    if has(b, 1):
                        turn_queries(b + 1)
                    normalize(b, 0)
                    if has(b, 1):
                        sum_squares(b + 1, 0, "q_squares")
                        sum_squares(b + 1, 2, "k_squares")
                else:
                    maxima(b, 1, k)
                    take_odd(b, 0, (0,))
                    if has(b, 1):
                        gains(b + 1, 1 - k)
                    take_odd(b, 0, (1,))
                    if has(b, -1):
                        add_output(b - 1)
                    if has(b, 1):
                        take_keys(b + 1)
                    normalize(b, 1)

            turn_queries(0)
            sum_squares(0, 0, "q_squares")
            sum_squares(0, 2, "k_squares")
            gains(0, 0)
            take_keys(0)
            walk(dve, window)
            take_odd(BATCHES - 1, 1)
            add_output(BATCHES - 1)

        @block.scalar
        def _(act):
            def shift(b, k):
                wait(act, m["v_product"], b - 1)
                act.activation(shifted[k][0:64, :], yT[0:64, bass.ds(b * SEQ, SEQ)], ACT.Copy)
                act.activation(shifted[k][64:P, 1:SEQ], yT[64:P, bass.ds(b * SEQ, SEQ - 1)], ACT.Copy)\
                    .then_inc(m["shifted_ready"], 1)

            def take(b, name, i):
                act.wait_ge(m[name + "_product"], b + 1)
                wait(act, m[name + "_turned"], b)
                act.activation(qk[:, i:i + 2, :, :].rearrange("p i h e -> p (i h e)"), front_ps, ACT.Copy)\
                    .then_inc(m[name + "_taken"], 1)

            def square(b, name, i):
                act.wait_ge(m[name + "_taken"], b + 1)
                wait(act, m["squared_sums"], b * 2)
                act.activation(squares[:, i:i + 2, :, :], qk[:, i:i + 2, :, :], ACT.Square)\
                    .then_inc(m[name + "_squares"], 1)

            def root(b):
                act.wait_ge(m["squared_sums"], b * 2 + 2)
                act.activation(norm[:, :, :], norm[:, :, :], ACT.Sqrt).then_inc(m["norm_ready"], 1)

            def take_value(b, k):
                act.wait_ge(m["v_product"], b + 1)
                wait(act, m["mixed"], b * 2 - 2)
                act.activation(value[k][:, :, :].rearrange("p t n -> p (t n)"), front_ps, ACT.Copy)\
                    .then_inc(m["v_taken"], 1)

            def take_queries(b):
                act.wait_ge(m["q_transposed"], b + 1)
                wait(act, m["scores_ready"], b * 4)
                act.activation(qT[:, :, :].rearrange("p j n -> p (j n)"), front_ps, ACT.Copy)\
                    .then_inc(m["qT_ready"], 1)

            def exps(b, hf, k, slots):
                u = b * 2 + hf
                for i in slots:
                    act.wait_ge(m["shifts_ready"], u * 2 + i // 2 + 1)
                    wait(act, transposed[1], u * 2 - 2)
                    n, gain = 4 * hf + i, q_gain[k]
                    c = i * BANK
                    act.activation(probs[:, n, 0:P], ps[:, c:c + P], ACT.Exp, bias=shifts[:, 0, n:n + 1],
                                   scale=gain[:, 0, n:n + 1], accum_out=sums[:, 0, n:n + 1])
                    act.activation(probs[:, n, P:SPAN], ps[:, c + P:c + SPAN], ACT.Exp, bias=shifts[:, 1, n:n + 1],
                                   scale=gain[:, 1, n:n + 1], accum_out=sums[:, 1, n:n + 1]).then_inc(m["exp_done"], 1)

            def take_even(b, hf, i):
                u = b * 2 + hf
                wait(act, m["mixed"], u - 1)
                act.wait_ge(transposed[0], u * 2 + i + 1)
                act.activation(probsT[:, 4 * hf + 2 * i, :], even[:, 0:SPAN], ACT.Copy).then_inc(probsT_copied[0], 1)

            def take_mix(b, hf):
                act.wait_ge(m["mixed"], b * 2 + hf + 1)
                wait(act, m["out_product"], b)
                act.activation(oT[:, 2 * hf:2 * hf + 2, :].rearrange("p j n -> p (j n)"), even, ACT.Copy)\
                    .then_inc(m["mix_taken"], 1)

            def window(b, hf, k):
                if hf == 0:
                    exps(b, 0, k, (0,))
                    if has(b, -1):
                        take_even(b - 1, 1, 0)
                    if has(b, 1):
                        take(b + 1, "q", 0)
                    exps(b, 0, k, (1,))
                    if has(b, -1):
                        take_even(b - 1, 1, 1)
                    if has(b, 1):
                        take(b + 1, "k", 2)
                    exps(b, 0, k, (2, 3))
                    if has(b, 1):
                        square(b + 1, "q", 0)
                        square(b + 1, "k", 2)
                    if has(b, -1):
                        take_mix(b - 1, 1)
                else:
                    if has(b, 1):
                        take_value(b + 1, 1 - k)
                    take_even(b, 0, 0)
                    if has(b, 1):
                        root(b + 1)
                    exps(b, 1, k, (0,))
                    take_even(b, 0, 1)
                    exps(b, 1, k, (1,))
                    if has(b, 1):
                        take_queries(b + 1)
                    exps(b, 1, k, (2, 3))
                    take_mix(b, 0)
                    if has(b, 2):
                        shift(b + 2, k)

            shift(0, 0)
            shift(1, 1)
            take(0, "q", 0)
            take(0, "k", 2)
            square(0, "q", 0)
            square(0, "k", 2)
            root(0)
            take_value(0, 0)
            take_queries(0)
            walk(act, window)
            for i in range(2):
                take_even(BATCHES - 1, 1, i)
            take_mix(BATCHES - 1, 1)

        @block.tensor
        def _(pe):
            pe.wait_ge(m["loaded"], 16 * (LOADS + 1))
            pe.wait_ge(m["edge_zeroed"], 1)

            def project(b, k, j, name, before, count):
                pe.wait_ge(m["shifted_ready"], b + 1)
                wait(pe, m[before], count)
                for t in range(2):
                    ins = pe.matmul(front_ps[:, t * BANK:(t + 1) * BANK], shifted[k][:, t * P:(t + 1) * P],
                                    wqkv[:, j * INNER:(j + 1) * INNER], start=True, stop=True)
                ins.then_inc(m[name + "_product"], 1)

            def front_transpose(b, i, name, before):
                pe.wait_ge(m[before], b + 1)
                pe.wait_ge(m[name + "_turned"], b + 1)
                for j in range(4):
                    for t in range(2):
                        c = j * SEQ + t * P
                        ins = pe.transpose(front_ps[:, c:c + P],
                                           turn[:, i + t, 2 * j:2 * j + 2, :].rearrange("p h e -> p (h e)"),
                                           g.ident[:, :])
                ins.then_inc(m[name + "_transposed"], 1)

            def scores(b, hf):
                u = b * 2 + hf
                pe.wait_ge(m["qT_ready"], b + 1)
                pe.wait_ge(m["kT_ready"], b + 1)
                for i in range(4):
                    wait(pe, m["exp_done"], u * 4 + i - 3)
                    j, rows = 2 * hf + i // 2, slice(64 * (i % 2), 64 * (i % 2) + 64)
                    ins = slot_scores(pe, g, g.band, i, lambda t: qT[rows, j, t * P:(t + 1) * P],
                                      lambda n: kT[rows, j, 0:n * P])
                    if i % 2 == 1:
                        ins.then_inc(m["scores_ready"], 1)

            def transposes(b, hf, slots):
                u = b * 2 + hf
                pe.wait_ge(m["normalized"], u + 1)
                for i in slots:
                    if i == 0:
                        wait(pe, m["mix_taken"], u)
                    if i == 1 and hf == 1:
                        wait(pe, m["out_added"], b)
                    if i == 1 and hf == 0:
                        wait(pe, probsT_copied[1], u * 2)
                    if i >= 2:
                        pe.wait_ge(probsT_copied[i % 2], u * 2 + 1)
                    bank = (even, odd)[i % 2]
                    for c in range(3):
                        ins = pe.transpose(bank[:, c * P:(c + 1) * P], probs[:, 4 * hf + i, c * P:(c + 1) * P],
                                           g.ident[:, :])
                    ins.then_inc(transposed[i % 2], 1)

            def mix(b, hf, k):
                u = b * 2 + hf
                pe.wait_ge(m["v_taken"], b + 1)
                for side in range(2):
                    pe.wait_ge(probsT_copied[side], u * 2 + 2)
                for i in range(4):
                    n, r = 4 * hf + i, i % 2
                    ins = slot_mix(pe, even[64 * r:64 * r + 64, (i // 2) * SEQ:(i // 2 + 1) * SEQ],
                                   lambda kt: value[k][:, kt, n * LDIM:(n + 1) * LDIM], n, probsT)
                ins.then_inc(m["mixed"], 1)

            def output(b):
                pe.wait_ge(m["mix_taken"], b * 2 + 2)
                if has(b, 1):
                    pe.wait_ge(probsT_copied[1], b * 4 + 6)
                else:
                    pe.wait_ge(probsT_copied[1], b * 4 + 4)
                for j in range(4):
                    ins = pe.matmul(odd[:, 0:SEQ], wo[:, j, :], oT[:, j, :], start=(j == 0), stop=(j == 3))
                ins.then_inc(m["out_product"], 1)

            def window(b, hf, k):
                scores(b, hf)
                if hf == 0:
                    if has(b, -1):
                        transposes(b - 1, 1, (0, 1))
                    if has(b, 1):
                        project(b + 1, 1 - k, 0, "q", "kT_ready", b + 1)
                    if has(b, -1):
                        transposes(b - 1, 1, (2, 3))
                    if has(b, 1):
                        project(b + 1, 1 - k, 1, "k", "q_taken", b + 2)
                    if has(b, -1):
                        mix(b - 1, 1, 1 - k)
                else:
                    if has(b, 1):
                        project(b + 1, 1 - k, 2, "v", "k_taken", b + 2)
                    transposes(b, 0, (0, 1))
                    if has(b, 1):
                        front_transpose(b + 1, 0, "q", "v_taken")
                    transposes(b, 0, (2, 3))
                    if has(b, -1):
                        output(b - 1)
                    if has(b, 1):
                        front_transpose(b + 1, 2, "k", "qT_ready")
                    mix(b, 0, k)

            project(0, 0, 0, "q", "kT_ready", 0)
            project(0, 0, 1, "k", "q_taken", 1)
            project(0, 0, 2, "v", "k_taken", 1)
            front_transpose(0, 0, "q", "v_taken")
            front_transpose(0, 2, "k", "qT_ready")
            walk(pe, window)
            transposes(BATCHES - 1, 1, range(4))
            mix(BATCHES - 1, 1, 1)
            output(BATCHES - 1)


def local_mlp(nc, g, d, yT, layer):
    hid = d["L0_ffn_w2"].shape[1]
    chunks = [(c, min(P, hid - c)) for c in range(0, hid, P)]
    parts = len(chunks)
    slices = TOKENS // BANK
    with ExitStack() as ctx:
        s = Stage(nc, ctx, g.sems, f"mlp{layer}")
        w1 = s.sb("w1", [P, 2 * hid])
        w2 = s.sb("w2", [P, parts, P])
        b1 = s.sb("b1", [P, 2, parts])
        cols = s.sb("cols", [P, 4])
        gain, offset, b2, eps = (cols[:, i:i + 1] for i in range(4))
        mean_of = s.sb("mean_of", [P, P])
        h = s.sb("h", [P, TOKENS])
        sq = s.sb("sq", [P, TOKENS])
        gate = s.sb("gate", [P, 2, BANK])
        hidden = s.sb("hidden", [P, parts, TOKENS])
        names = ("loaded constants upper_shifted lower_shifted mean_product centred squared var_product std_ready "
                 "inverse_ready scaled h_ready gate_product gate_ready a_product hidden_ready out_product "
                 "out_added").split()
        m = {n: s.sem(n) for n in names}
        ps = g.ps
        loads = 1 + parts * 3 + 3
        block = ctx.enter_context(nc.Block())

        def bank(i):
            return ps[:, i * BANK:(i + 1) * BANK]

        def tokens(c):
            return slice(c * BANK, (c + 1) * BANK)

        @block.sync
        def _(sp):
            sp.dma_start(w1[:, :], d["L0_ffn_w1"][layer]).then_inc(m["loaded"], 16)
            for j, (c, n) in enumerate(chunks):
                sp.dma_start(w2[0:n, j, :], d["L0_ffn_w2"][layer][c:c + n, :]).then_inc(m["loaded"], 16)
                for k in range(2):
                    sp.dma_start(b1[0:n, k, j:j + 1], column(d["L0_ffn_b1"][layer][k * hid + c:k * hid + c + n]))\
                        .then_inc(m["loaded"], 16)
            for c, name in ((gain, "ln_g"), (offset, "ln_b"), (b2, "b2")):
                sp.dma_start(c, column(d["L0_ffn_" + name][layer])).then_inc(m["loaded"], 16)

        @block.gpsimd
        def _(pool):
            pool.memset(mean_of[:, :], 1.0 / P).then_inc(m["constants"], 1)
            pool.memset(eps, EPS).then_inc(m["constants"], 1)
            pool.wait_ge(m["constants"], 2)
            pool.memset(h[64:P, :].rearrange("p (b l) -> p b l", l=SEQ)[:, :, 0:1], 0.0).then_inc(m["constants"], 1)

        @block.vector
        def _(dve):
            def scale(c):
                dve.wait_ge(m["std_ready"], c + 1)
                dve.reciprocal(sq[:, tokens(c)], sq[:, tokens(c)]).then_inc(m["inverse_ready"], 1)
                dve.wait_ge(m["inverse_ready"], c + 1)
                dve.tensor_tensor(h[:, tokens(c)], h[:, tokens(c)], sq[:, tokens(c)], ALU.mult).then_inc(m["scaled"], 1)

            def hide(i):
                c, j = i // parts, i % parts
                n = chunks[j][1]
                dve.wait_ge(m["gate_ready"], i + 1)
                dve.wait_ge(m["a_product"], i + 1)
                dve.scalar_tensor_tensor(out=hidden[0:n, j, tokens(c)], in0=bank(2 + i % 2)[0:n, :],
                                         scalar=b1[0:n, 0, j:j + 1], in1=gate[0:n, i % 2, :], op0=ALU.add,
                                         op1=ALU.mult).then_inc(m["hidden_ready"], 1)

            def add(c):
                dve.wait_ge(m["out_product"], c + 1)
                dve.scalar_tensor_tensor(out=yT[:, tokens(c)], in0=bank(4 + c % 2), scalar=b2, in1=yT[:, tokens(c)],
                                         op0=ALU.add, op1=ALU.add).then_inc(m["out_added"], 1)

            for c in range(slices):
                dve.tensor_copy(h[0:64, tokens(c)], yT[0:64, tokens(c)]).then_inc(m["lower_shifted"], 1)
            for c in range(slices):
                dve.wait_ge(m["mean_product"], c + 1)
                dve.tensor_tensor(h[:, tokens(c)], h[:, tokens(c)], bank(c), ALU.subtract).then_inc(m["centred"], 1)
            for c in range(2):
                scale(c)
            for i in range(slices * parts):
                if i % parts == 0 and 0 < i and i // parts + 1 < slices:
                    scale(i // parts + 1)
                hide(i)
                if i % parts == 0 and i > 0:
                    add(i // parts - 1)
            add(slices - 1)

        @block.scalar
        def _(act):
            act.wait_ge(m["constants"], 3)
            for c in range(slices):
                h3, y3 = (a[64:P, tokens(c)].rearrange("p (b l) -> p b l", l=SEQ) for a in (h, yT))
                act.activation(h3[:, :, 1:SEQ], y3[:, :, 0:SEQ - 1], ACT.Copy).then_inc(m["upper_shifted"], 1)
            for c in range(slices):
                act.wait_ge(m["centred"], c + 1)
                act.activation(sq[:, tokens(c)], h[:, tokens(c)], ACT.Square).then_inc(m["squared"], 1)
            for c in range(slices):
                act.wait_ge(m["var_product"], c + 1)
                act.activation(sq[:, tokens(c)], bank(4 + c), ACT.Sqrt, bias=eps).then_inc(m["std_ready"], 1)
            act.wait_ge(m["loaded"], 16 * loads)

            def affine(c):
                act.wait_ge(m["scaled"], c + 1)
                act.activation(h[:, tokens(c)], h[:, tokens(c)], ACT.Identity, bias=offset, scale=gain)\
                    .then_inc(m["h_ready"], 1)

            affine(0)
            affine(1)
            for i in range(slices * parts):
                j = i % parts
                n = chunks[j][1]
                if j == 1 and 0 < i // parts and i // parts + 1 < slices:
                    affine(i // parts + 1)
                act.wait_ge(m["gate_product"], i + 1)
                wait(act, m["hidden_ready"], i - 1)
                act.activation(gate[0:n, i % 2, :], bank(i % 2)[0:n, :], ACT.Gelu, bias=b1[0:n, 1, j:j + 1])\
                    .then_inc(m["gate_ready"], 1)

        @block.tensor
        def _(pe):
            def out(c):
                pe.wait_ge(m["hidden_ready"], (c + 1) * parts)
                wait(pe, m["out_added"], c - 1)
                for j, (_, n) in enumerate(chunks):
                    ins = pe.matmul(bank(4 + c % 2), w2[0:n, j, :], hidden[0:n, j, tokens(c)], start=(j == 0),
                                    stop=(j == parts - 1))
                ins.then_inc(m["out_product"], 1)

            pe.wait_ge(m["constants"], 3)
            for c in range(slices):
                pe.wait_ge(m["lower_shifted"], c + 1)
                pe.wait_ge(m["upper_shifted"], c + 1)
                pe.matmul(bank(c), mean_of[:, :], h[:, tokens(c)], start=True, stop=True).then_inc(m["mean_product"], 1)
            for c in range(slices):
                pe.wait_ge(m["squared"], c + 1)
                pe.matmul(bank(4 + c), mean_of[:, :], sq[:, tokens(c)], start=True, stop=True)\
                    .then_inc(m["var_product"], 1)
            pe.wait_ge(m["loaded"], 16 * loads)
            pe.wait_ge(m["centred"], slices)
            pe.wait_ge(m["std_ready"], slices)
            for i in range(slices * parts):
                c, j = i // parts, i % parts
                off, n = chunks[j]
                if j == 0:
                    pe.wait_ge(m["h_ready"], c + 1)
                wait(pe, m["gate_ready"], i - 1)
                pe.matmul(bank(i % 2)[0:n, :], w1[:, hid + off:hid + off + n], h[:, tokens(c)], start=True, stop=True)\
                    .then_inc(m["gate_product"], 1)
                wait(pe, m["hidden_ready"], i - 1)
                pe.matmul(bank(2 + i % 2)[0:n, :], w1[:, off:off + n], h[:, tokens(c)], start=True, stop=True)\
                    .then_inc(m["a_product"], 1)
                if j == 0 and c > 0:
                    out(c - 1)
            out(slices - 1)


def causal_stage(nc, g, d):
    with ExitStack() as outer:
        so = Stage(nc, outer, g.sems, "causal")
        hT = so.sb("hT", [P, TOKENS])
        norm_to_channels(nc, g, "causal_norm", hT)
        causal_attention(nc, g, d, hT)


def causal_attention(nc, g, d, hT):
    with ExitStack() as ctx:
        s = Stage(nc, ctx, g.sems, "causal_attn")
        raw = s.sb("raw", [P, 3, P])
        wT = s.sb("wT", [P, 3, P])
        bcol = s.sb("bcol", [P, 3])
        qT = s.sb("qT", [P, TOKENS])
        kT = s.sb("kT", [P, TOKENS])
        value = s.sb("value", [P, TILES, P])
        peaks = s.sb("peaks", [P, 2, SLOTS])
        sums = s.sb("sums", [P, 2, SLOTS])
        inverse = s.sb("inverse", [P, 2, SLOTS])
        probs = s.sb("probs", [P, SLOTS, SPAN])
        probsT = s.sb("probsT", [P, SLOTS, SPAN])
        oT = s.sb("oT", [P, TOKENS])
        names = ("loaded w_transposed w_ready q_product k_product v_product q_ready k_ready v_ready scores_ready "
                 "peaks_ready exp_done normalized mixed o_ready o_transposed inverse_ready").split()
        m = {n: s.sem(n) for n in names}
        transposed = [s.sem(f"transposed{i}") for i in range(2)]
        probsT_copied = [s.sem(f"probsT_copied{i}") for i in range(2)]
        ps = g.ps
        lo, hi = ps[:, 0:TOKENS], ps[:, TOKENS:2 * TOKENS]
        block = ctx.enter_context(nc.Block())

        @block.sync
        def _(sp):
            for i, n in enumerate("qkv"):
                sp.dma_start(raw[:, i, :], d["L1_attn_W" + n]).then_inc(m["loaded"], 16)
                sp.dma_start(bcol[:, i:i + 1], column(d["L1_attn_b" + n])).then_inc(m["loaded"], 16)

        @block.tensor
        def _(pe):
            pe.wait_ge(m["loaded"], 96)
            for i in range(3):
                last = pe.transpose(ps[:, i * P:(i + 1) * P], raw[:, i, :], g.ident[:, :])
            last.then_inc(m["w_transposed"], 1)
            pe.wait_ge(m["w_ready"], 1)
            for base, i, done in ((0, 0, "q_product"), (TOKENS, 1, "k_product")):
                for k in range(TOKENS // BANK):
                    last = pe.matmul(ps[:, base + k * BANK:base + (k + 1) * BANK], wT[:, i, :],
                                     hT[:, k * BANK:(k + 1) * BANK], start=True, stop=True)
                last.then_inc(m[done], 1)
            pe.wait_ge(m["q_ready"], 1)
            for t in range(TILES):
                last = pe.matmul(ps[:, t * P:(t + 1) * P], hT[:, t * P:(t + 1) * P], wT[:, 2, :], start=True, stop=True)
            last.then_inc(m["v_product"], 1)
            pe.wait_ge(m["k_ready"], 1)
            pe.wait_ge(m["v_ready"], 1)
            for b in range(BATCHES):
                c = b * SEQ
                ins = slot_scores(pe, g, g.causal, b, lambda t: qT[:, c + t * P:c + (t + 1) * P],
                                  lambda n: kT[:, c:c + n * P])
                if b % 4 == 3:
                    ins.then_inc(m["scores_ready"], 1)
            pe.wait_ge(m["exp_done"], 2)
            for b in range(BATCHES):
                if b % 4 == 0:
                    pe.wait_ge(m["normalized"], b // 4 + 1)
                if b >= 2:
                    pe.wait_ge(probsT_copied[b % 2], b // 2)
                slot_transposes(pe, g, b, probs).then_inc(transposed[b % 2], 1)
            for b in range(BATCHES):
                pe.wait_ge(probsT_copied[b % 2], b // 2 + 1)
                last = slot_mix(pe, ps[:, b * SEQ:(b + 1) * SEQ], lambda kt: value[:, 2 * b + kt, :], b, probsT)
            last.then_inc(m["mixed"], 1)
            pe.wait_ge(m["o_ready"], 1)
            for t in range(TILES):
                last = pe.transpose(ps[:, TOKENS + t * P:TOKENS + (t + 1) * P], oT[:, t * P:(t + 1) * P], g.ident[:, :])
            last.then_inc(m["o_transposed"], 1)

        @block.scalar
        def _(act):
            act.wait_ge(m["w_transposed"], 1)
            act.activation(wT[:, :, :].rearrange("p i c -> p (i c)"), ps[:, 0:3 * P], ACT.Copy).then_inc(m["w_ready"], 1)
            act.wait_ge(m["loaded"], 96)
            act.wait_ge(m["k_product"], 1)
            act.activation(kT[:, :], hi, ACT.Identity, bias=bcol[:, 1:2]).then_inc(m["k_ready"], 1)
            act.wait_ge(m["v_product"], 1)
            act.activation(value[:, :, :].rearrange("p t c -> p (t c)"), lo, ACT.Copy).then_inc(m["v_ready"], 1)
            for b in range(BATCHES):
                if b % 4 == 0:
                    act.wait_ge(m["peaks_ready"], b // 4 + 1)
                ins = slot_exps(act, g, b, probs, peaks, sums, lambda t: 1.0)
                if b % 4 == 3:
                    ins.then_inc(m["exp_done"], 1)
            for b in range(0, BATCHES, 2):
                act.wait_ge(transposed[0], b // 2 + 1)
                act.activation(probsT[:, b, :], ps[:, 6 * BANK:6 * BANK + SPAN], ACT.Copy).then_inc(probsT_copied[0], 1)
            act.wait_ge(m["mixed"], 1)
            act.activation(oT[:, :], lo, ACT.Identity, bias=bcol[:, 2:3]).then_inc(m["o_ready"], 1)

        @block.vector
        def _(dve):
            dve.wait_ge(m["loaded"], 96)
            dve.wait_ge(m["q_product"], 1)
            dve.tensor_scalar(qT[:, :], lo, bcol[:, 0:1], float(P) ** -0.5, ALU.add, ALU.mult).then_inc(m["q_ready"], 1)
            for half in range(2):
                dve.wait_ge(m["scores_ready"], half + 1)
                slot_peaks(dve, g, half, peaks).then_inc(m["peaks_ready"], 1)
            for half in range(2):
                dve.wait_ge(m["exp_done"], half + 1)
                h = slice(4 * half, 4 * half + 4)
                dve.reciprocal(inverse[:, :, h], sums[:, :, h]).then_inc(m["inverse_ready"], 1)
                dve.wait_ge(m["inverse_ready"], half + 1)
                slot_normalize(dve, half, probs, inverse).then_inc(m["normalized"], 1)
            for b in range(1, BATCHES, 2):
                dve.wait_ge(transposed[1], b // 2 + 1)
                dve.tensor_copy(probsT[:, b, :], ps[:, 7 * BANK:7 * BANK + SPAN]).then_inc(probsT_copied[1], 1)
            dve.wait_ge(m["o_transposed"], 1)
            dve.tensor_tensor(g.x[:, :, :], g.x[:, :, :], hi.rearrange("p (t c) -> p t c", c=P), ALU.add)


LIMIT = 100.0


def binary_stage(nc, g, d):
    with ExitStack() as outer:
        so = Stage(nc, outer, g.sems, "binary")
        hT = so.sb("hT", [P, TOKENS])
        norm_to_channels(nc, g, "binary_norm", hT)
        binary_product(nc, g, d, hT)


def binary_product(nc, g, d, hT):
    with ExitStack() as ctx:
        s = Stage(nc, ctx, g.sems, "binary_product")
        w = s.sb("w", [P, P])
        wT = s.sb("wT", [P, P])
        scale = s.sb("scale", [P, P])
        bias = s.sb("bias", [P, P])
        y = s.sb("y", [P, TILES, P])
        loaded, signs, w_transposed, w_ready = s.sem("loaded"), s.sem("signs"), s.sem("w_transposed"), s.sem("w_ready")
        product_done, dve_order = s.sem("product_done"), s.sem("dve_order")
        block = ctx.enter_context(nc.Block())
        wide = [P, TILES, P]

        @block.sync
        def _(sp):
            sp.dma_start(w[:, :], d["L1_ffn_weights"]).then_inc(loaded, 16)
            sp.dma_start(scale[:, :], d["L1_ffn_scale"].partition_broadcast(P)).then_inc(loaded, 16)
            sp.dma_start(bias[:, :], d["L1_ffn_bias"].partition_broadcast(P)).then_inc(loaded, 16)

        @block.vector
        def _(dve):
            order = Order(dve, dve_order)
            dve.wait_ge(loaded, 48)
            order.done(dve.tensor_scalar(w[:, :], w[:, :], 0.0, 2.0, ALU.is_ge, ALU.mult))
            dve.tensor_scalar(w[:, :], w[:, :], 1.0, None, ALU.subtract).then_inc(signs, 1)
            dve.wait_ge(product_done, 1)
            order.done(dve.tensor_tensor(y[:, :, :], g.ps[:, 0:TOKENS].rearrange("p (t c) -> p t c", c=P),
                                         scale[:, :].unsqueeze(1).to_broadcast(wide), ALU.mult))
            order.done(dve.tensor_tensor(y[:, :, :], y[:, :, :], bias[:, :].unsqueeze(1).to_broadcast(wide), ALU.add))
            order.done(dve.tensor_scalar(y[:, :, :], y[:, :, :], -LIMIT, LIMIT, ALU.max, ALU.min))
            dve.tensor_tensor(g.x[:, :, :], g.x[:, :, :], y[:, :, :], ALU.add)

        @block.scalar
        def _(act):
            act.wait_ge(w_transposed, 1)
            act.activation(wT[:, :], g.ps[:, 0:P], ACT.Copy).then_inc(w_ready, 1)

        @block.tensor
        def _(pe):
            pe.wait_ge(signs, 1)
            pe.transpose(g.ps[:, 0:P], w[:, :], g.ident[:, :]).then_inc(w_transposed, 1)
            pe.wait_ge(w_ready, 1)
            for t in range(TILES):
                last = pe.matmul(g.ps[:, t * P:(t + 1) * P], hT[:, t * P:(t + 1) * P], wT[:, :], start=True, stop=True)
            last.then_inc(product_done, 1)


class Globals:
    pass


def build(nc, d, out):
    g = Globals()
    with ExitStack() as ctx:
        g.x = ctx.enter_context(nc.sbuf_tensor("x_residual", [P, 16, P], F32))
        g.ident = ctx.enter_context(nc.sbuf_tensor("ident", [P, P], F32))
        g.identb = ctx.enter_context(nc.sbuf_tensor("identb", [P, P], BF16))
        g.causal = ctx.enter_context(nc.sbuf_tensor("causal_mask", [P, 3 * P], BF16))
        g.band = ctx.enter_context(nc.sbuf_tensor("band_mask", [P, 3 * P], BF16))
        g.ps = ctx.enter_context(nc.psum_tensor("banks", [P, 8 * BANK], F32))
        g.ctxT = ctx.enter_context(nc.sbuf_tensor("contextT", [P, BATCHES, KEYS], F32))
        stages = [load_stage, context_stage, scan_stage,
                  lambda *a: narrow_cross_stage(*a, "L0_xattn", 8 ** -0.5),
                  local_stage, causal_stage,
                  lambda *a: cross_stage(*a, "L1_xattn", 64 ** -0.5),
                  binary_stage]
        for stage in stages:
            with ExitStack() as sem_ctx:
                g.sems = Semaphores(nc, sem_ctx)
                stage(nc, g, d)
                g.sems.clear()
        stored = ctx.enter_context(nc.semaphore("stored"))
        block = ctx.enter_context(nc.Block())

        @block.sync
        def _(sp):
            sp.dma_start(out.rearrange("b (t p) c -> p (b t) c", p=P), g.x[:, :, :]).then_inc(stored, 16)
            sp.wait_ge(stored, 16)


def rotary_tables():
    import numpy as np
    f = np.float32
    half = np.arange(0, LDIM, 2, dtype=f)
    inv_freq = (f(1.0) / np.power(f(10000.0), half / f(LDIM))).astype(f)
    t = np.arange(SEQ, dtype=f)
    freqs = np.tile(t[:, None] * inv_freq[None, :], (1, 2)).astype(f)
    base = ((half + f(0.4 * LDIM)) / f(1.4 * LDIM)).astype(f)
    power = ((t - SEQ // 2) / f(WINDOW // 2)).astype(f)
    scale = np.tile(np.power(base[None, :], power[:, None]), (1, 2)).astype(f)
    sign = np.where(np.arange(LDIM) < LDIM // 2, f(-1.0), f(1.0))
    cos, sin = np.cos(freqs), np.sin(freqs) * sign
    return np.stack([cos * scale, sin * scale, cos / scale, sin / scale]).astype(f)


def kernel(**inputs):
    import numpy as np
    from concourse import bacc
    from concourse.bass_utils import run_bass_kernel_spmd

    nc = bacc.Bacc("TRN2", target_bir_lowering=False, num_devices=1)
    arrays, d = {}, {}
    for name, a in list(inputs.items()) + [("rotary", rotary_tables())]:
        a = np.ascontiguousarray(a)
        arrays[f"in_{name}_dram"] = a
        d[name] = nc.dram_tensor(f"in_{name}_dram", a.shape, mybir.dt.from_np(a.dtype), kind="ExternalInput").ap()
    out = nc.dram_tensor("out_0_dram", inputs["x"].shape, F32, kind="ExternalOutput").ap()
    build(nc, d, out)
    r = run_bass_kernel_spmd(nc, [arrays], core_ids=[0])
    return r.results[0]["out_0_dram"]
```
